# Optimizing a Trainium2 kernel written in Bass

```python
import numpy as np
import jax
import jax.numpy as jnp

def _softmax(x, axis=-1):
    return jax.nn.softmax(x, axis=axis)

def _gelu(x):
    return jax.nn.gelu(x, approximate=True)

def _silu(x):
    return jax.nn.silu(x)

def _sigmoid(x):
    return jax.nn.sigmoid(x)

def _layernorm(x, axis=-1, eps=1e-05):
    m = jnp.mean(x, axis=axis, keepdims=True)
    v = jnp.var(x, axis=axis, keepdims=True)
    return (x - m) / jnp.sqrt(v + eps)

def _scatter_add(tgt, idx, src, axis=0):
    return tgt.at[idx].add(src)

def _segment_sum(src, seg, n):
    return jax.ops.segment_sum(src, seg, n)
kernel_name = 'mk_decoder_preln_d1_seqx_r4_7ee32b'

def setup_inputs(seed: int=0):
    np.random.seed(seed)
    _w = jnp.asarray

    def _rec_inputs():
        import jax
        import jax.numpy as jnp
        _rk = jax.random.key(seed)
        x = -0.0003929 + 0.9999 * jax.random.normal(jax.random.fold_in(_rk, 1), (8, 512, 256), jnp.float32)
        _lenS = 512 - jax.random.randint(jax.random.fold_in(_rk, 7), (8,), 0, max(1, 512 // 4) + 1, jnp.int32)
        _lenS2 = 512 - jax.random.randint(jax.random.fold_in(_rk, 8), (8,), 0, max(1, 512 // 4) + 1, jnp.int32)
        _ctx_1024P = jax.random.normal(jax.random.fold_in(_rk, 11), (8, 16, 256), jnp.float32)
        _ctx_1024c = jax.random.dirichlet(jax.random.fold_in(_rk, 511), 0.3 * jnp.ones((16,), jnp.float32), (8, 512))
        _ctx_1024t = jnp.einsum('bsk,bkd->bsd', _ctx_1024c, _ctx_1024P)
        _ctx_1024t = _ctx_1024t * jax.lax.rsqrt(jnp.mean(jnp.square(_ctx_1024t)) + 1e-12) * 0.953939
        ctx_1024 = 2.81802e-05 + 1.00001 * (_ctx_1024t + 0.3 * jax.random.normal(jax.random.fold_in(_rk, 611), (8, 512, 256), jnp.float32))
        return (x, ctx_1024)
    x, ctx_1024 = _rec_inputs()

    def _L0_attn_setup():
        import jax, jax.numpy as jnp
        import numpy as np
        B, S, D, H = (2, 512, 256, 16)
        DK = D // H
        key = jax.random.key(seed)
        ks = jax.random.split(key, 9)
        s = 0.02
        return {'embeddings': jax.random.normal(ks[0], (B, S, D), jnp.float32), 'Wq': jax.random.normal(ks[1], (H, D, DK), jnp.float32) * s, 'bq': jax.random.normal(ks[2], (H, DK), jnp.float32) * s, 'Wk': jax.random.normal(ks[3], (H, D, DK), jnp.float32) * s, 'bk': jax.random.normal(ks[4], (H, DK), jnp.float32) * s, 'Wv': jax.random.normal(ks[5], (H, D, DK), jnp.float32) * s, 'bv': jax.random.normal(ks[6], (H, DK), jnp.float32) * s, 'Wo': jax.random.normal(ks[7], (D, D), jnp.float32) * s, 'bo': jax.random.normal(ks[8], (D,), jnp.float32) * s}
    _L0_attn_all = _L0_attn_setup()
    _L0_attn_in = {k: v for k, v in _L0_attn_all.items() if k in ('Wq', 'bq', 'Wk', 'bk', 'Wv', 'bv', 'Wo', 'bo')}
    del _L0_attn_all

    def _L0_xattn_setup():
        import jax, jax.numpy as jnp
        import numpy as np
        D = 256
        key = jax.random.key(seed)
        ks = jax.random.split(key, 9)
        B, Nq, Nk = (8, 512, 512)
        s = 1.0 / np.sqrt(D)
        return {'query': jax.random.normal(ks[0], (B, Nq, D), jnp.float32), 'key': jax.random.normal(ks[1], (B, Nk, D), jnp.float32), 'value': jax.random.normal(ks[2], (B, Nk, D), jnp.float32), 'Wq': jax.random.uniform(ks[3], (D, D), jnp.float32, -s, s), 'bq': jax.random.uniform(ks[4], (D,), jnp.float32, -s, s), 'Wk': jax.random.uniform(ks[5], (D, D), jnp.float32, -s, s), 'bk': jax.random.uniform(ks[6], (D,), jnp.float32, -s, s), 'Wv': jax.random.uniform(ks[7], (D, D), jnp.float32, -s, s), 'bv': jax.random.uniform(ks[8], (D,), jnp.float32, -s, s)}
    _L0_xattn_all = _L0_xattn_setup()
    _L0_xattn_in = {k: v for k, v in _L0_xattn_all.items() if k in ('Wq', 'bq', 'Wk', 'bk', 'Wv', 'bv')}
    del _L0_xattn_all

    def _L0_ffn_setup():
        import jax, jax.numpy as jnp
        import numpy as np
        EMB = 256
        HID = 512
        HEADS = 16
        HEAD_DIM = EMB // HEADS
        EXPERTS = 8
        TOPK = 2
        EPS = 1e-05

        def layernorm(x, scale, shift):
            mean = jnp.mean(x, axis=-1, keepdims=True)
            var = jnp.mean((x - mean) ** 2, axis=-1, keepdims=True)
            return scale * (x - mean) / jnp.sqrt(var + EPS) + shift

        def attention(x, wq, wk, wv, wo, bo):
            b, t, _ = x.shape
            q = (x @ wq).reshape(b, t, HEADS, HEAD_DIM)
            k = (x @ wk).reshape(b, t, HEADS, HEAD_DIM)
            v = (x @ wv).reshape(b, t, HEADS, HEAD_DIM)
            scores = jnp.einsum('bqhd,bkhd->bhqk', q, k)
            mask = jnp.arange(t)[:, None] < jnp.arange(t)[None, :]
            scores = jnp.where(mask, -jnp.inf, scores)
            attn = jax.nn.softmax(scores / np.sqrt(HEAD_DIM), axis=-1)
            ctx = jnp.einsum('bhqk,bkhd->bqhd', attn, v).reshape(b, t, EMB)
            return ctx @ wo + bo

        def moe_ff(x, gate_w, w1, w2, w3):
            b, t, d = x.shape
            xf = x.reshape(b * t, d)
            scores = xf @ gate_w
            topk_scores, topk_idx = jax.lax.top_k(scores, TOPK)
            topk_probs = jax.nn.softmax(topk_scores, axis=-1)
            weight = jnp.sum(jax.nn.one_hot(topk_idx, EXPERTS, dtype=xf.dtype) * topk_probs[..., None], axis=1)
            h = jax.nn.silu(jnp.einsum('td,edh->eth', xf, w1)) * jnp.einsum('td,edh->eth', xf, w2)
            out_e = jnp.einsum('eth,ehd->etd', h, w3)
            out = jnp.einsum('etd,te->td', out_e, weight)
            return out.reshape(b, t, d)
        key = jax.random.key(seed)
        ks = jax.random.split(key, 12)
        s = lambda k, shape, fan: jax.random.normal(k, shape, jnp.float32) / np.sqrt(fan)
        return {'x': jax.random.normal(ks[0], (2, 512, EMB), jnp.float32), 'ln1_scale': jnp.ones((EMB,), jnp.float32), 'ln1_shift': jnp.zeros((EMB,), jnp.float32), 'wq': s(ks[1], (EMB, EMB), EMB), 'wk': s(ks[2], (EMB, EMB), EMB), 'wv': s(ks[3], (EMB, EMB), EMB), 'wo': s(ks[4], (EMB, EMB), EMB), 'bo': jnp.zeros((EMB,), jnp.float32), 'ln2_scale': jnp.ones((EMB,), jnp.float32), 'ln2_shift': jnp.zeros((EMB,), jnp.float32), 'gate_w': s(ks[5], (EMB, EXPERTS), EMB), 'w1': s(ks[6], (EXPERTS, EMB, HID), EMB), 'w2': s(ks[7], (EXPERTS, EMB, HID), EMB), 'w3': s(ks[8], (EXPERTS, HID, EMB), HID)}
    _L0_ffn_all = _L0_ffn_setup()
    _L0_ffn_in = {k: v for k, v in _L0_ffn_all.items() if k in ('ln1_scale', 'ln1_shift', 'wq', 'wk', 'wv', 'wo', 'bo', 'ln2_scale', 'ln2_shift', 'gate_w', 'w1', 'w2', 'w3')}
    del _L0_ffn_all
    return {'x': x, 'ctx_1024': ctx_1024, 'L0_attn_Wq': _L0_attn_in['Wq'], 'L0_attn_bq': _L0_attn_in['bq'], 'L0_attn_Wk': _L0_attn_in['Wk'], 'L0_attn_bk': _L0_attn_in['bk'], 'L0_attn_Wv': _L0_attn_in['Wv'], 'L0_attn_bv': _L0_attn_in['bv'], 'L0_attn_Wo': _L0_attn_in['Wo'], 'L0_attn_bo': _L0_attn_in['bo'], 'L0_xattn_Wq': _L0_xattn_in['Wq'], 'L0_xattn_bq': _L0_xattn_in['bq'], 'L0_xattn_Wk': _L0_xattn_in['Wk'], 'L0_xattn_bk': _L0_xattn_in['bk'], 'L0_xattn_Wv': _L0_xattn_in['Wv'], 'L0_xattn_bv': _L0_xattn_in['bv'], 'L0_ffn_ln1_scale': _L0_ffn_in['ln1_scale'], 'L0_ffn_ln1_shift': _L0_ffn_in['ln1_shift'], 'L0_ffn_wq': _L0_ffn_in['wq'], 'L0_ffn_wk': _L0_ffn_in['wk'], 'L0_ffn_wv': _L0_ffn_in['wv'], 'L0_ffn_wo': _L0_ffn_in['wo'], 'L0_ffn_bo': _L0_ffn_in['bo'], 'L0_ffn_ln2_scale': _L0_ffn_in['ln2_scale'], 'L0_ffn_ln2_shift': _L0_ffn_in['ln2_shift'], 'L0_ffn_gate_w': _L0_ffn_in['gate_w'], 'L0_ffn_w1': _L0_ffn_in['w1'], 'L0_ffn_w2': _L0_ffn_in['w2'], 'L0_ffn_w3': _L0_ffn_in['w3']}

def reference(x, ctx_1024, L0_attn_Wq, L0_attn_bq, L0_attn_Wk, L0_attn_bk, L0_attn_Wv, L0_attn_bv, L0_attn_Wo, L0_attn_bo, L0_xattn_Wq, L0_xattn_bq, L0_xattn_Wk, L0_xattn_bk, L0_xattn_Wv, L0_xattn_bv, L0_ffn_ln1_scale, L0_ffn_ln1_shift, L0_ffn_wq, L0_ffn_wk, L0_ffn_wv, L0_ffn_wo, L0_ffn_bo, L0_ffn_ln2_scale, L0_ffn_ln2_shift, L0_ffn_gate_w, L0_ffn_w1, L0_ffn_w2, L0_ffn_w3):
    import jax
    import jax.numpy as jnp

    def _L0_attn_ref(embeddings, Wq, bq, Wk, bk, Wv, bv, Wo, bo):
        import jax, jax.numpy as jnp
        import numpy as np
        B, S, D, H = (2, 512, 256, 16)
        DK = D // H
        b, s, d = embeddings.shape
        dk = Wq.shape[-1]
        q = jnp.einsum('bsd,hdk->bhsk', embeddings, Wq) + bq[None, :, None, :]
        k = jnp.einsum('bsd,hdk->bhsk', embeddings, Wk) + bk[None, :, None, :]
        v = jnp.einsum('bsd,hdk->bhsk', embeddings, Wv) + bv[None, :, None, :]
        scores = jnp.einsum('bhqk,bhsk->bhqs', q, k) / jnp.sqrt(jnp.float32(dk))
        causal_mask = jnp.triu(jnp.ones((s, s), dtype=bool), k=1)
        scores = jnp.where(causal_mask, jnp.float32(-1000000000.0), scores)
        weights = jax.nn.softmax(scores, axis=-1)
        ctx = jnp.einsum('bhqs,bhsk->bhqk', weights, v)
        concat = ctx.transpose(0, 2, 1, 3).reshape(b, s, d)
        return concat @ Wo + bo

    def _L0_xattn_ref(query, key, value, Wq, bq, Wk, bk, Wv, bv):
        import jax, jax.numpy as jnp
        import numpy as np
        D = 256
        q = jnp.einsum('bnd,ed->bne', query, Wq) + bq
        k = jnp.einsum('bnd,ed->bne', key, Wk) + bk
        v = jnp.einsum('bnd,ed->bne', value, Wv) + bv
        scores = jnp.einsum('bqd,bkd->bqk', q, k)
        attn = jax.nn.softmax(scores, axis=-1)
        return jnp.einsum('bqk,bkd->bqd', attn, v)

    def _L0_ffn_ref(x, ln1_scale, ln1_shift, wq, wk, wv, wo, bo, ln2_scale, ln2_shift, gate_w, w1, w2, w3):
        import jax, jax.numpy as jnp
        import numpy as np
        EMB = 256
        HID = 512
        HEADS = 16
        HEAD_DIM = EMB // HEADS
        EXPERTS = 8
        TOPK = 2
        EPS = 1e-05

        def layernorm(x, scale, shift):
            mean = jnp.mean(x, axis=-1, keepdims=True)
            var = jnp.mean((x - mean) ** 2, axis=-1, keepdims=True)
            return scale * (x - mean) / jnp.sqrt(var + EPS) + shift

        def attention(x, wq, wk, wv, wo, bo):
            b, t, _ = x.shape
            q = (x @ wq).reshape(b, t, HEADS, HEAD_DIM)
            k = (x @ wk).reshape(b, t, HEADS, HEAD_DIM)
            v = (x @ wv).reshape(b, t, HEADS, HEAD_DIM)
            scores = jnp.einsum('bqhd,bkhd->bhqk', q, k)
            mask = jnp.arange(t)[:, None] < jnp.arange(t)[None, :]
            scores = jnp.where(mask, -jnp.inf, scores)
            attn = jax.nn.softmax(scores / np.sqrt(HEAD_DIM), axis=-1)
            ctx = jnp.einsum('bhqk,bkhd->bqhd', attn, v).reshape(b, t, EMB)
            return ctx @ wo + bo

        def moe_ff(x, gate_w, w1, w2, w3):
            b, t, d = x.shape
            xf = x.reshape(b * t, d)
            scores = xf @ gate_w
            topk_scores, topk_idx = jax.lax.top_k(scores, TOPK)
            topk_probs = jax.nn.softmax(topk_scores, axis=-1)
            weight = jnp.sum(jax.nn.one_hot(topk_idx, EXPERTS, dtype=xf.dtype) * topk_probs[..., None], axis=1)
            h = jax.nn.silu(jnp.einsum('td,edh->eth', xf, w1)) * jnp.einsum('td,edh->eth', xf, w2)
            out_e = jnp.einsum('eth,ehd->etd', h, w3)
            out = jnp.einsum('etd,te->td', out_e, weight)
            return out.reshape(b, t, d)
        h = layernorm(x, ln1_scale, ln1_shift)
        x = x + attention(h, wq, wk, wv, wo, bo)
        h = layernorm(x, ln2_scale, ln2_shift)
        x = x + moe_ff(h, gate_w, w1, w2, w3)
        return x
    x = x + _L0_attn_ref(_layernorm(x, axis=-1), L0_attn_Wq, L0_attn_bq, L0_attn_Wk, L0_attn_bk, L0_attn_Wv, L0_attn_bv, L0_attn_Wo, L0_attn_bo)
    x = x + _L0_xattn_ref(_layernorm(x, axis=-1), ctx_1024, ctx_1024, L0_xattn_Wq, L0_xattn_bq, L0_xattn_Wk, L0_xattn_bk, L0_xattn_Wv, L0_xattn_bv)
    x = x + _L0_ffn_ref(_layernorm(x, axis=-1), L0_ffn_ln1_scale, L0_ffn_ln1_shift, L0_ffn_wq, L0_ffn_wk, L0_ffn_wv, L0_ffn_wo, L0_ffn_bo, L0_ffn_ln2_scale, L0_ffn_ln2_shift, L0_ffn_gate_w, L0_ffn_w1, L0_ffn_w2, L0_ffn_w3)
    return x

_drawn_inputs = setup_inputs


def setup_inputs(seed=0):
    import zlib

    import numpy as np

    out = dict(_drawn_inputs(seed))
    spreads = {'L0_ffn_ln1_scale': (1.0, 0.2),
     'L0_ffn_ln1_shift': (0.0, 0.1),
     'L0_ffn_bo': (0.0, 0.1),
     'L0_ffn_ln2_scale': (1.0, 0.2),
     'L0_ffn_ln2_shift': (0.0, 0.1)}
    factors = {'L0_attn_Wq': 8.0,
     'L0_attn_bq': 8.0,
     'L0_attn_Wk': 8.0,
     'L0_attn_bk': 8.0,
     'L0_attn_bv': 3.697,
     'L0_xattn_bk': 8.0}
    for name, (base, spread) in spreads.items():
        noise = np.random.default_rng([zlib.crc32(name.encode()), seed]).standard_normal(out[name].shape)
        drawn = base * np.exp(spread * noise) if base else spread * noise
        out[name] = jnp.asarray(drawn.astype(out[name].dtype))
    for name, factor in factors.items():
        out[name] = (out[name] * factor).astype(out[name].dtype)
    return out
```

```python
from contextlib import ExitStack

import concourse.bass as bass
from concourse import mybir

ALU = mybir.AluOpType
ACT = mybir.ActivationFunctionType
AX_X = mybir.AxisListType.X
F32 = mybir.dt.float32
BF16 = mybir.dt.bfloat16
I32 = mybir.dt.int32
U32 = mybir.dt.uint32

P = 128
NSEQ = 8
SEQ = 512
D = 256
KC = D // P
TT = SEQ // P
NT = NSEQ * TT
H = 16
DK = D // H
HG = 4
NG = H // HG
EPS = 1e-5
MASKED = -1e30

E_N = 8
HID = 512
HC = HID // P
MT = (2 * NSEQ * SEQ + E_N * (P - 1)) // P


def wait(eng, sem, value):
    if not (isinstance(value, int) and value <= 0):
        eng.wait_ge(sem, value)


def wait_apart(eng, sem, value, passed):
    eng.wait_ge(sem, value)
    eng.sem_inc(passed, 1)


PRO, FIRST, MID, LAST, DRAIN = -1, 0, 1, NSEQ - 1, NSEQ


def each_body(eng, emit):
    emit(-1, PRO, 1)
    emit(0, FIRST, 0)
    with eng.Fori(0, (NSEQ - 2) // 2) as i:
        for k in range(2):
            emit(i * 2 + (1 + k), MID, (1 + k) % 2)
    emit(NSEQ - 1, LAST, 1)
    emit(NSEQ, DRAIN, 0)


def runs(kind, off):
    at = {PRO: -1, FIRST: 0, MID: 1, LAST: NSEQ - 1, DRAIN: NSEQ}[kind] + off
    return 0 <= at < NSEQ


class Turns:

    def __init__(self, hooks):
        self.jobs = [(name, off, bank) for at in sorted(hooks) for name, off, bank in hooks[at] if bank is not None]

    def count(self, kind, bank, upto=None):
        n = 0
        for name, off, b in self.jobs:
            if name == upto:
                break
            n += b == bank and runs(kind, off)
        return n

    def before(self, c, kind, name):
        bank = next(b for n, _, b in self.jobs if n == name)
        local = self.count(kind, bank, name)
        pro = self.count(PRO, bank)
        if kind == PRO:
            return local
        if kind == FIRST:
            return pro + local
        first = pro + self.count(FIRST, bank)
        mid = self.count(MID, bank)
        if kind == DRAIN:
            return first + mid * (NSEQ - 2) + self.count(LAST, bank) + local
        return (c - 1) * mid + (first + local)


QROWS = (0, 0, 0, 1, 1, 2)
KROWS = (0, 1, 2, 0, 1, 0)
SROWS = len(QROWS) * DK
MROWS = SROWS + 3

ROW_UNITS = [(0, (0, 1, 2, 3)), (1, (0, 1)), (1, (2, 3))] + [(2, (h,)) for h in range(HG)] + [(3, (h,)) for h in range(HG)]
KEY_UNITS = [(0, (h,)) for h in range(HG)] + [(1, (h,)) for h in range(HG)] + [(2, (0, 1)), (2, (2, 3)), (3, (0, 1, 2, 3))]
NU = len(ROW_UNITS)
assert NU == len(KEY_UNITS)
KEY_DONE = [max(u for u, (kt, _) in enumerate(KEY_UNITS) if kt == t) + 1 for t in range(TT)]
ROW_BANKS = 3
PT_OFF = [HG * sum(SEQ - P * j for j in range(t)) for t in range(TT + 1)]
PV_AT = {1: 0, 4: 1, 7: 2, 9: 3}
VCOLS = 32


def row_before(u, g4):
    return g4 * NU + (u - ROW_BANKS + 1 if u >= ROW_BANKS else {0: 9, 1: 10, 2: 8}[u] + 1 - NU)


ATT_HOOKS = {
    (0, 0): [("stats1", 1, None)],
    (0, 1): [("ut0", -1, 0)],
    (0, 2): [("norm1", 1, None)],
    (0, 3): [("mt3", -1, 1)],
    (0, 4): [("stats2", 1, None)],
    (0, 6): [("norm2", 1, None)],
    (0, 8): [("ht0", 1, 0), ("ht1", 1, 1)],
    (0, 10): [("q0", 1, 0)],
    (1, 1): [("ut1", -1, 0)],
    (1, 3): [("mt0", 0, 1)],
    (1, 4): [("q1", 1, 1)],
    (1, 6): [("k0", 1, 0)],
    (1, 8): [("k1", 1, 1)],
    (2, 1): [("ut2", -1, 0)],
    (2, 3): [("mt1", 0, 1)],
    (3, 1): [("ut3", -1, 0)],
    (3, 3): [("mt2", 0, 1)],
    (3, 4): [("v0", 1, 0), ("v1", 1, 1)],
    (3, 7): [("ct0", -1, 0), ("ct1", -1, 1)],
    (3, 10): [("wo0", -1, 0), ("wo1", -1, 1)],
}
ATT_TURNS = Turns(ATT_HOOKS)
PARTS = ("q0", "q1", "k0", "k1")


def attention_phase(nc, consts, x_sb, name, w, x_dram=None, y_sb=None):
    first = x_dram is not None
    ident, ident_bf, neg_mask, minus_half = consts["ident"], consts["ident_bf"], consts["neg_mask"], consts["minus_half"]
    part_dram = nc.dram_tensor(f"{name}_parts", (2, 4, 3, P, SEQ), BF16).ap()
    max_dram = nc.dram_tensor(f"{name}_max", (NG, 3, HG * TT, P), BF16).ap()
    with ExitStack() as ctx:
        def sb(n, shape, dt=F32):
            return ctx.enter_context(nc.sbuf_tensor(f"{name}_{n}", shape, dt))

        def sem(n):
            return ctx.enter_context(nc.semaphore(f"{name}_{n}"))

        wq, wk, wv, wo = (sb(n, [P, KC, D]) for n in ("wq", "wk", "wv", "wo"))
        bo_row = sb("bo_row", [P, D])
        if first:
            bq, bk = sb("bq", [P, KC]), sb("bk", [P, KC])
            bv_row = sb("bv_row", [P, D])
        else:
            ln_scale, ln_shift = sb("ln_scale", [P, KC]), sb("ln_shift", [P, KC])
        stats, mv = sb("stats", [P, TT, 6]), sb("mv", [P, TT, 2])
        var_eps, rstd = sb("var_eps", [P, TT]), sb("rstd", [P, TT])
        hn = sb("hn", [P, TT, D])
        ht = sb("ht", [P, KC, SEQ])
        proj32 = [sb(f"proj32_{i}", [P, SEQ]) for i in range(2)]
        rest32 = [sb(f"rest32_{i}", [P, SEQ]) for i in range(2)]
        parts = [sb(f"parts_{n}", [P, 3, SEQ], BF16) for n in PARTS]
        q_rows = [sb(f"q_rows{g}", [MROWS, HG, SEQ], BF16) for g in range(NG)]
        k_rows = [sb(f"k_rows{g}", [MROWS, HG, SEQ], BF16) for g in range(NG)]
        maxes = sb("maxes", [P, HG, TT])
        max_rest = sb("max_rest", [P, HG * TT])
        max_bf = sb("max_bf", [P, HG * TT], BF16)
        max_parts = sb("max_parts", [P, P])
        max_rows = sb("max_rows", [3 * HG * TT, P], BF16)
        probs = [sb(f"probs{i}", [P, PT_OFF[TT]]) for i in range(2)]
        values = [sb(f"values{i}", [P, TT, H, VCOLS]) for i in range(2)]
        ctx_raw = sb("ctx_raw", [P, SEQ])
        sums = sb("sums", [P, TT, HG])
        ctx_tok = sb("ctx_tok", [P, TT, D])
        ctx_t = sb("ctx_t", [P, KC, SEQ])

        row_ps = [ctx.enter_context(nc.psum_tensor(f"{name}_row{i}", [P, SEQ], F32)) for i in range(ROW_BANKS)]
        key_ps = [ctx.enter_context(nc.psum_tensor(f"{name}_key{i}", [P, SEQ], F32)) for i in range(2)]
        ctx_ps = ctx.enter_context(nc.psum_tensor(f"{name}_ctx", [P, SEQ], F32))
        misc_ps = [ctx.enter_context(nc.psum_tensor(f"{name}_misc{i}", [P, SEQ], F32)) for i in range(2)]

        weights_in = sem("weights_in")
        x_in = [sem(f"x_in{i}") for i in range(2)]
        setup_done = sem("setup_done")
        ln_steps, rstd_done, resid_done = sem("ln_steps"), sem("rstd_done"), sem("resid_done")
        proj_done, split_done, low_done = sem("proj_done"), sem("split_done"), sem("low_done")
        parts_out = [sem(f"parts_out{i}") for i in range(2)]
        rows_in = [sem(f"rows_in{g}") for g in range(NG)]
        row_scores, row_max = sem("row_scores"), sem("row_max")
        max_steps, max_out = sem("max_steps"), [sem(f"max_out{i}") for i in range(2)]
        max_in = [sem(f"max_in{g}") for g in range(NG)]
        key_scores, exp_done, mask_done = sem("key_scores"), sem("exp_done"), sem("mask_done")
        pv_done, ctx_out, sums_done = sem("pv_done"), sem("ctx_out"), sem("sums_done")
        LN_ALL = 4 if first else 8
        W_ALL = 16 * (11 if first else 7)
        passed = {e: sem(f"passed_{e}") for e in ("sp", "dve", "pool")}
        misc_full, misc_free = [sem(f"misc_full{i}") for i in range(2)], [sem(f"misc_free{i}") for i in range(2)]

        def slots(c, kind):
            for g in range(NG):
                row = (c, g) if runs(kind, 0) else None
                back2 = (c, g - 2) if g >= 2 else (c - 1, g + 2)
                key = back2 if runs(kind, 0 if g >= 2 else -1) else None
                back3 = (c, 0) if g == 3 else (c - 1, g + 1)
                pv = back3 if runs(kind, 0 if g == 3 else -1) else None
                yield g, row, key, pv

        def hooks(c, kind, g, step):
            for job, off, bank in ATT_HOOKS.get((g, step), []):
                if runs(kind, off):
                    turn = ATT_TURNS.before(c, kind, job) if bank is not None else None
                    yield job, c + off, bank, turn

        def tiles(c):
            return bass.ds(c * TT, TT)

        with nc.Block() as block:

            @block.sync
            def _(sp):
                sp.dma_start(wo[:], w["wo"].rearrange("(c p) n -> p c n", p=P)).then_inc(weights_in, 16)
                if first:
                    for src, dst in ((w["wq"], wq), (w["wk"], wk), (w["wv"], wv)):
                        for kc in range(KC):
                            sp.dma_start(dst[:, kc, :].rearrange("p (h k) -> p h k", h=H),
                                         src[:, kc * P:(kc + 1) * P, :].rearrange("h p k -> p h k")).then_inc(weights_in, 16)
                    for src, dst in ((w["bq"], bq), (w["bk"], bk)):
                        sp.dma_start(dst[:], src.rearrange("(c g) k -> (g k) c", c=KC),
                                     allow_slow_non_contiguous=True).then_inc(weights_in, 16)
                    sp.dma_start(bv_row[:], w["bv"].rearrange("(o h) k -> o (h k)", o=1).to_broadcast([P, D])).then_inc(weights_in, 16)
                else:
                    for src, dst in ((w["wq"], wq), (w["wk"], wk), (w["wv"], wv)):
                        sp.dma_start(dst[:], src.rearrange("(c p) n -> p c n", p=P)).then_inc(weights_in, 16)
                    for src, dst in ((w["ln_scale"], ln_scale), (w["ln_shift"], ln_shift)):
                        sp.dma_start(dst[:], src.rearrange("(c p) -> p c", p=P),
                                     allow_slow_non_contiguous=True).then_inc(weights_in, 16)
                sp.dma_start(bo_row[:], w["bo"].rearrange("(o n) -> o n", o=1).to_broadcast([P, D])).then_inc(weights_in, 16)

                def load_x(c, parity):
                    sp.dma_start(x_sb[:, tiles(c), :],
                                 x_dram[bass.ds(c, 1), :, :].rearrange("o (t p) d -> p (o t) d", p=P)).then_inc(x_in[parity], 16)

                def store_parts(c, j, parity):
                    sp.wait_ge(low_done, c * 4 + (j + 1))
                    sp.dma_start(part_dram[parity, j].rearrange("s p t -> p s t"), parts[j][:]).then_inc(parts_out[parity], 16)

                def load_rows(c, g, parity):
                    wait_apart(sp, parts_out[parity], (c - parity) * 32 + 64, passed["sp"])
                    wait(sp, key_scores, ((c - 1) * NG + (g + 1)) * NU)
                    for rows, order, j0 in ((q_rows, QROWS, 0), (k_rows, KROWS, 2)):
                        src = part_dram[parity, j0 + g // 2]
                        for r, part in enumerate(order):
                            sp.dma_start(rows[g][r * DK:(r + 1) * DK, :, :],
                                         src[part, (g % 2) * 64:(g % 2) * 64 + 64, :].rearrange("(h d) t -> d h t", h=HG)
                                         ).then_inc(rows_in[g], 16)

                def body(c, kind, parity):
                    if first and kind in (PRO, FIRST):
                        for b in range(4) if kind == PRO else range(4, NSEQ):
                            wait(sp, x_in[b % 2], b // 2 * 16)
                            load_x(b, b % 2)
                    for g, row, key, pv in slots(c, kind):
                        for step in range(NU):
                            for job, b, bank, turn in hooks(c, kind, g, step):
                                if job[:2] == "mt":
                                    mg = int(job[2])
                                    sp.wait_ge(misc_free[1], turn + 1)
                                    sp.dma_start(max_dram[mg].rearrange("s r t -> (s r) t"), max_rows[:]).then_inc(max_out[mg % 2], 16)
                                    sp.wait_ge(max_out[mg % 2], (b * 2 + (mg // 2 + 1)) * 16)
                                    sp.dma_start(q_rows[mg][SROWS:MROWS, :, :].rearrange("s h t -> s (h t)"),
                                                 max_dram[mg].rearrange("s r t -> s (r t)")).then_inc(max_in[mg], 16)
                                if job in PARTS:
                                    store_parts(b, PARTS.index(job), 1 - parity)
                        if g < 2 and runs(kind, 0):
                            load_rows(c, g + 2, parity)
                        if g >= 2 and runs(kind, 1):
                            load_rows(c + 1, g - 2, 1 - parity)

                each_body(sp, body)
                for mg in range(NG):
                    sp.wait_ge(max_in[mg], 16 * NSEQ)

            @block.tensor
            def _(pe):
                pe.wait_ge(setup_done, 1)

                def rows_unit(c, g, u):
                    qt, heads = ROW_UNITS[u]
                    n = (qt + 1) * P
                    out = row_ps[u % ROW_BANKS]
                    if u == 0:
                        pe.wait_ge(rows_in[g], (c + 1) * (16 * 2 * len(QROWS)))
                    wait(pe, row_max, row_before(u, c * NG + g))
                    for k, h in enumerate(heads):
                        pe.matmul(out[:, k * n:(k + 1) * n], q_rows[g][0:SROWS, h, qt * P:(qt + 1) * P],
                                  k_rows[g][0:SROWS, h, 0:n], start=(k == 0), stop=False, skip_group_check=True)
                    diag = out[:, 0:len(heads) * n].rearrange("p (h n) -> p h n", n=n)[:, :, qt * P:n]
                    pe.matmul(diag, ident_bf[:], neg_mask[:, 0:len(heads), :], start=False, stop=True,
                              skip_group_check=True).then_inc(row_scores, 1)

                def key_unit(c, g, u):
                    kt, heads = KEY_UNITS[u]
                    n = SEQ - kt * P
                    out = key_ps[(u + g) % 2]
                    if u == 0:
                        pe.wait_ge(max_in[g], (c + 1) * 16)
                    wait(pe, exp_done, (c * NG + g) * NU + (u - 1))
                    for k, h in enumerate(heads):
                        mm = pe.matmul(out[:, k * n:(k + 1) * n], k_rows[g][0:MROWS, h, kt * P:(kt + 1) * P],
                                       q_rows[g][0:MROWS, h, kt * P:SEQ], start=True, stop=True, skip_group_check=True)
                    mm.then_inc(key_scores, 1)

                def pv(c, g, kt, parity):
                    if kt == 0:
                        wait(pe, ctx_out, c * NG + g)
                    pe.wait_ge(mask_done, (c * NG + g) * TT + (kt + 1))
                    p = probs[g % 2][:, PT_OFF[kt]:PT_OFF[kt + 1]].rearrange("p (h n) -> p h n", h=HG)
                    for h in range(HG):
                        mm = pe.matmul(ctx_ps[VCOLS * h:VCOLS * (h + 1), kt * P:SEQ], values[parity][:, kt, g * HG + h, :],
                                       p[:, h, :], start=(kt == 0), stop=(kt == TT - 1), skip_group_check=True)
                    if kt == TT - 1:
                        mm.then_inc(pv_done, 1)

                def transposes(out, pieces, sem_):
                    for k, piece in enumerate(pieces):
                        mm = pe.transpose(out[:, k * P:(k + 1) * P], piece, ident[:])
                    mm.then_inc(sem_, 1)

                def product(out, lhs, rhs, sem_=None):
                    for kc in range(KC):
                        mm = pe.matmul(out, lhs(kc), rhs(kc), start=(kc == 0), stop=(kc == KC - 1), skip_group_check=True)
                    if sem_ is not None:
                        mm.then_inc(sem_, 1)

                def body(c, kind, parity):
                    for g, row, key, pvg in slots(c, kind):
                        for step in range(NU):
                            if row:
                                rows_unit(*row, step)
                            if key:
                                key_unit(*key, step)
                            if pvg and step in PV_AT:
                                pv(*pvg, PV_AT[step], parity if g == 3 else 1 - parity)
                            for job, b, bank, turn in hooks(c, kind, g, step):
                                if bank is None:
                                    continue
                                out, full = misc_ps[bank], misc_full[bank]
                                wait(pe, misc_free[bank], turn)
                                k = int(job[2]) if len(job) == 3 else int(job[1])
                                if job[:2] == "ut":
                                    pe.wait_ge(ctx_out, b * NG + (k + 1))
                                    transposes(out, [ctx_raw[:, t * P:(t + 1) * P] for t in range(TT)], full)
                                elif job[:2] == "mt":
                                    pe.wait_ge(max_steps, (b * NG + (k + 1)) * 4)
                                    pe.transpose(out[:, 0:P], max_parts[:], ident[:]).then_inc(full, 1)
                                elif job[:2] == "ht":
                                    if k == 0:
                                        pe.wait_ge(ln_steps, (b + 1) * LN_ALL)
                                    transposes(out, [hn[:, t, k * P:(k + 1) * P] for t in range(TT)], full)
                                elif job[0] in "qk":
                                    if kind == PRO and job == "q0":
                                        pe.wait_ge(weights_in, W_ALL)
                                    if job == "q0":
                                        pe.wait_ge(misc_free[1], ATT_TURNS.before(c, kind, "ht1") + 1)
                                    wt = wq if job[0] == "q" else wk
                                    product(out[:], lambda kc: wt[:, kc, k * P:(k + 1) * P], lambda kc: ht[:, kc, :], full)
                                elif job[0] == "v":
                                    for t in range(2):
                                        product(out[:, t * D:(t + 1) * D], lambda kc: ht[:, kc, (2 * k + t) * P:(2 * k + t + 1) * P],
                                                lambda kc: wv[:, kc, :], full if t == 1 else None)
                                elif job[:2] == "ct":
                                    transposes(out, [ctx_tok[:, t, k * P:(k + 1) * P] for t in range(TT)], full)
                                elif job[:2] == "wo":
                                    if k == 0:
                                        pe.wait_ge(misc_free[1], ATT_TURNS.before(c, kind, "ct1") + 1)
                                    for t in range(2):
                                        product(out[:, t * D:(t + 1) * D], lambda kc: ctx_t[:, kc, (2 * k + t) * P:(2 * k + t + 1) * P],
                                                lambda kc: wo[:, kc, :], full if t == 1 else None)

                each_body(pe, body)

            @block.scalar
            def _(act):
                act.wait_ge(setup_done, 1)
                act.wait_ge(weights_in, W_ALL)

                def exp_unit(c, g, u):
                    kt, heads = KEY_UNITS[u]
                    n = SEQ - kt * P
                    if u == 0:
                        wait(act, pv_done, c * NG + (g - 1))
                    act.wait_ge(key_scores, (c * NG + g) * NU + (u + 1))
                    at = PT_OFF[kt] + heads[0] * n
                    act.activation(probs[g % 2][:, at:at + len(heads) * n], key_ps[(u + g) % 2][:, 0:len(heads) * n],
                                   ACT.Exp, scale=DK ** -0.5).then_inc(exp_done, 1)

                def body(c, kind, parity):
                    for g, row, key, pvg in slots(c, kind):
                        for step in range(NU):
                            if key:
                                exp_unit(*key, step)
                            for job, b, bank, turn in hooks(c, kind, g, step):
                                if bank is None or job[:2] in ("ut", "wo") or job[0] == "v":
                                    continue
                                k = int(job[2]) if len(job) == 3 else int(job[1])
                                act.wait_ge(misc_full[bank], turn + 1)
                                src, free = misc_ps[bank], misc_free[bank]
                                if job[:2] == "mt":
                                    act.activation(max_rows[:], src[0:3 * HG * TT, 0:P], ACT.Copy).then_inc(free, 1)
                                elif job[:2] == "ht":
                                    if first:
                                        act.activation(ht[:, k, :], src[:], ACT.Copy).then_inc(free, 1)
                                    else:
                                        act.activation(ht[:, k, :], src[:], ACT.Identity, scale=ln_scale[:, k:k + 1],
                                                       bias=ln_shift[:, k:k + 1]).then_inc(free, 1)
                                elif job[:2] == "ct":
                                    act.activation(ctx_t[:, k, :], src[:], ACT.Copy).then_inc(free, 1)
                                else:
                                    j = PARTS.index(job)
                                    wait(act, low_done, b * 4 + (j - 1))
                                    if first:
                                        bias = (bq if job[0] == "q" else bk)[:, k:k + 1]
                                        act.activation(proj32[j % 2][:], src[:], ACT.Identity, bias=bias).then_inc(proj_done, 1)
                                        act.activation(parts[j][:, 0, :], src[:], ACT.Identity, bias=bias).then_inc(free, 1)
                                    else:
                                        act.activation(proj32[j % 2][:], src[:], ACT.Copy).then_inc(proj_done, 1)
                                        act.activation(parts[j][:, 0, :], src[:], ACT.Copy).then_inc(free, 1)
                        if pvg:
                            pc, pg = pvg
                            act.wait_ge(pv_done, pc * NG + (pg + 1))
                            act.activation(ctx_raw[:], ctx_ps[:], ACT.Copy).then_inc(ctx_out, 1)

                each_body(act, body)

            @block.vector
            def _(dve):
                for g in range(NG):
                    dve.memset(k_rows[g][SROWS:MROWS, :, :], 1.0)
                for i in range(2):
                    dve.memset(values[i][:, :, :, DK:DK + 1], 1.0)
                    dve.memset(values[i][:, :, :, DK + 1:VCOLS], 0.0)
                dve.memset(max_parts[:], 0.0).then_inc(setup_done, 1)
                dve.wait_ge(setup_done, 1)
                dve.wait_ge(weights_in, W_ALL)

                def ln_stats(b, n, src):
                    base = b * LN_ALL + n * 4
                    for t in range(TT):
                        ins = dve.bn_stats(stats[:, t, :], src(t))
                    ins.then_inc(ln_steps, 1)
                    wait_apart(dve, ln_steps, base + 1, passed["dve"])
                    for t in range(TT):
                        ins = dve.bn_aggr(mv[:, t, :], stats[:, t, :])
                    ins.then_inc(ln_steps, 1)
                    dve.wait_ge(ln_steps, base + 2)
                    dve.tensor_scalar(var_eps[:], mv[:, :, 1], EPS, None, ALU.add).then_inc(ln_steps, 1)

                def ln_apply(b, n, src, dst):
                    dve.wait_ge(rstd_done, b * (LN_ALL // 4) + (n + 1))
                    for t in range(TT):
                        ins = dve.tensor_scalar(dst(t), src(t), mv[:, t, 0:1], rstd[:, t:t + 1], ALU.subtract, ALU.mult)
                    ins.then_inc(ln_steps, 1)

                def body(c, kind, parity):
                    for g, row, key, pvg in slots(c, kind):
                        for step in range(NU):
                            if row:
                                qt, heads = ROW_UNITS[step]
                                n = (qt + 1) * P
                                dve.wait_ge(row_scores, (c * NG + g) * NU + (step + 1))
                                dve.tensor_reduce(maxes[:, heads[0]:heads[-1] + 1, qt],
                                                  row_ps[step % ROW_BANKS][:, 0:len(heads) * n].rearrange("p (h n) -> p h n", n=n),
                                                  AX_X, ALU.max).then_inc(row_max, 1)
                            for job, b, bank, turn in hooks(c, kind, g, step):
                                xt = (lambda t: x_sb[:, b * TT + t, :])
                                if job == "stats1":
                                    if first:
                                        wait_apart(dve, x_in[1 - parity], (b - (1 - parity)) * 8 + 16, passed["dve"])
                                    ln_stats(b, 0, xt)
                                elif job == "norm1":
                                    if first:
                                        ln_apply(b, 0, xt, lambda t: hn[:, t, :])
                                    else:
                                        ln_apply(b, 0, xt, lambda t: y_sb[:, b * TT + t, :])
                                elif job == "stats2" and not first:
                                    wait_apart(dve, ln_steps, b * LN_ALL + 4, passed["dve"])
                                    ln_stats(b, 1, lambda t: y_sb[:, b * TT + t, :])
                                elif job == "norm2" and not first:
                                    ln_apply(b, 1, lambda t: y_sb[:, b * TT + t, :], lambda t: hn[:, t, :])
                                elif job in PARTS:
                                    j = PARTS.index(job)
                                    dve.wait_ge(misc_free[bank], turn + 1)
                                    dve.tensor_tensor(rest32[j % 2][:], proj32[j % 2][:], parts[j][:, 0, :],
                                                      ALU.subtract).then_inc(split_done, 1)
                                    dve.wait_ge(split_done, (b * 4 + j) * 2 + 1)
                                    dve.tensor_copy(parts[j][:, 1, :], rest32[j % 2][:]).then_inc(split_done, 1)
                                elif job[:2] == "ut":
                                    k = int(job[2])
                                    dve.wait_ge(misc_full[bank], turn + 1)
                                    src = misc_ps[bank][:].rearrange("p (t h n) -> p t h n", t=TT, h=HG)
                                    dve.reciprocal(sums[:], src[:, :, :, DK]).then_inc(sums_done, 1)
                                    dve.wait_ge(sums_done, b * NG + (k + 1))
                                    dve.tensor_tensor(
                                        ctx_tok[:, :, k * HG * DK:(k + 1) * HG * DK].rearrange("p t (h n) -> p t h n", h=HG),
                                        src[:, :, :, 0:DK], sums[:].unsqueeze(3).to_broadcast([P, TT, HG, DK]),
                                        ALU.mult).then_inc(misc_free[bank], 1)
                                elif job in ("v0", "v1"):
                                    k = int(job[1])
                                    dve.wait_ge(misc_full[bank], turn + 1)
                                    out = values[1 - parity][:, 2 * k:2 * k + 2, :, 0:DK]
                                    src = misc_ps[bank][:].rearrange("p (t h n) -> p t h n", t=2, h=H)
                                    if first:
                                        for t in range(2):
                                            ins = dve.tensor_tensor(out[:, t], src[:, t], bv_row[:].rearrange("p (h n) -> p h n", h=H), ALU.add)
                                    else:
                                        ins = dve.tensor_copy(out, src)
                                    ins.then_inc(misc_free[bank], 1)
                                elif job in ("wo0", "wo1"):
                                    k = int(job[2])
                                    dve.wait_ge(misc_full[bank], turn + 1)
                                    dve.wait_ge(resid_done, b + 1)
                                    xs = x_sb[:, bass.ds(b * TT + 2 * k, 2), :]
                                    src = misc_ps[bank][:].rearrange("p (t n) -> p t n", t=2)
                                    if first:
                                        dve.tensor_tensor(xs, src, xs, ALU.add).then_inc(misc_free[bank], 1)
                                    else:
                                        ys = y_sb[:, bass.ds(b * TT + 2 * k, 2), :]
                                        dve.tensor_tensor(ys, src, ys, ALU.add).then_inc(misc_free[bank], 1)
                                        dve.wait_ge(misc_free[bank], turn + 1)
                                        dve.tensor_tensor(xs, ys, xs, ALU.add)
                        if row:
                            g4 = (c * NG + g)
                            mflat = maxes[:].rearrange("p h t -> p (h t)")
                            m = HG * TT
                            dve.wait_ge(row_max, (g4 + 1) * NU)
                            dve.tensor_scalar(max_bf[:], mflat, -1.0, None, ALU.mult).then_inc(max_steps, 1)
                            dve.wait_ge(max_steps, g4 * 4 + 1)
                            dve.tensor_copy(max_parts[:, 0:m], max_bf[:])
                            dve.scalar_tensor_tensor(out=max_rest[:], in0=mflat, scalar=-1.0, in1=max_bf[:],
                                                     op0=ALU.mult, op1=ALU.subtract).then_inc(max_steps, 1)
                            dve.wait_ge(max_steps, g4 * 4 + 2)
                            dve.tensor_copy(max_bf[:], max_rest[:]).then_inc(max_steps, 1)
                            dve.wait_ge(max_steps, g4 * 4 + 3)
                            dve.tensor_copy(max_parts[:, m:2 * m], max_bf[:])
                            dve.tensor_tensor(max_parts[:, 2 * m:3 * m], max_rest[:], max_bf[:], ALU.subtract).then_inc(max_steps, 1)

                each_body(dve, body)

            @block.gpsimd
            def _(pool):
                pool.wait_ge(weights_in, W_ALL)

                def body(c, kind, parity):
                    for g, row, key, pvg in slots(c, kind):
                        for step in range(NU):
                            if key:
                                kc_, kg = key
                                for kt in range(TT):
                                    if step == KEY_DONE[kt] - 1:
                                        wait_apart(pool, exp_done, (kc_ * NG + kg) * NU + KEY_DONE[kt], passed["pool"])
                                        p = probs[kg % 2][:, PT_OFF[kt]:PT_OFF[kt + 1]].rearrange("p (h n) -> p h n", h=HG)[:, :, 0:P]
                                        pool.affine_select(out=p, in_=p, compare_op=ALU.is_ge, fill=0.0, base=0,
                                                           pattern=[[0, HG], [1, P]], channel_multiplier=-1).then_inc(mask_done, 1)
                            for job, b, bank, turn in hooks(c, kind, g, step):
                                n_ln = LN_ALL // 4
                                if job == "norm1":
                                    pool.wait_ge(ln_steps, b * LN_ALL + 3)
                                    pool.tensor_tensor(rstd[:], var_eps[:], minus_half[:].to_broadcast([P, TT]), ALU.pow).then_inc(rstd_done, 1)
                                elif job == "norm2" and not first:
                                    pool.wait_ge(ln_steps, b * LN_ALL + 7)
                                    pool.tensor_tensor(rstd[:], var_eps[:], minus_half[:].to_broadcast([P, TT]), ALU.pow).then_inc(rstd_done, 1)
                                elif job in PARTS:
                                    j = PARTS.index(job)
                                    pool.wait_ge(split_done, (b * 4 + j) * 2 + 2)
                                    pool.tensor_tensor(parts[j][:, 2, :], rest32[j % 2][:], parts[j][:, 1, :], ALU.subtract).then_inc(low_done, 1)
                                    if job == "k1":
                                        pool.wait_ge(ln_steps, (b + 1) * LN_ALL)
                                        r = (x_sb if first else y_sb)[:, tiles(b), :]
                                        pool.tensor_tensor(r, r, bo_row[:].unsqueeze(1).to_broadcast([P, TT, D]), ALU.add).then_inc(resid_done, 1)

                each_body(pool, body)


def make_constants(nc, ctx):
    ident = ctx.enter_context(nc.sbuf_tensor("ident", [P, P], F32))
    ident_bf = ctx.enter_context(nc.sbuf_tensor("ident_bf", [P, P], BF16))
    neg_mask = ctx.enter_context(nc.sbuf_tensor("neg_mask", [P, HG, P], BF16))
    minus_half = ctx.enter_context(nc.sbuf_tensor("minus_half", [P, 1], F32))
    filled = ctx.enter_context(nc.semaphore("filled"))
    with nc.Block() as block:

        @block.gpsimd
        def _(pool):
            pool.memset(minus_half[:], -0.5)
            pool.memset(ident[:], 0.0)
            pool.memset(ident_bf[:], 0.0)
            pool.memset(neg_mask[:], 0.0).then_inc(filled, 1)
            pool.wait_ge(filled, 1)
            for t in (ident, ident_bf):
                pool.affine_select(out=t[:], in_=t[:], compare_op=ALU.not_equal, fill=1.0, base=0,
                                   pattern=[[-1, P]], channel_multiplier=1)
            pool.affine_select(out=neg_mask[:], in_=neg_mask[:], compare_op=ALU.is_ge, fill=MASKED, base=0,
                               pattern=[[0, HG], [-1, P]], channel_multiplier=1).then_inc(filled, 1)

    return dict(ident=ident, ident_bf=ident_bf, neg_mask=neg_mask, minus_half=minus_half)


CROSS_HOOKS = {
    (0, 0): [("stats", 1, None)],
    (0, 1): [("ct0", 1, 0), ("ct1", 1, 1)],
    (0, 2): [("norm", 1, None)],
    (1, 0): [("k0", 1, 0), ("k1", 1, 1)],
    (1, 2): [("ht0", 1, 0), ("ht1", 1, 1)],
    (2, 0): [("q0", 1, 0), ("q1", 1, 1)],
    (3, 0): [("v0", 1, 0), ("v1", 1, 1)],
}
CROSS_TURNS = Turns(CROSS_HOOKS)
CROSS_STEPS = 3
ZERO_TILES = 9
assert (MT + 1) % ZERO_TILES == 0


def cross_phase(nc, consts, x_sb, w, ctx_dram, sorted_dram):
    ident, minus_half = consts["ident"], consts["minus_half"]
    with ExitStack() as ctx:
        def sb(n, shape, dt=F32):
            return ctx.enter_context(nc.sbuf_tensor(f"cross_{n}", shape, dt))

        def psum(n):
            return [ctx.enter_context(nc.psum_tensor(f"cross_{n}{i}", [P, SEQ], F32)) for i in range(2)]

        def sem(n):
            return ctx.enter_context(nc.semaphore(f"cross_{n}"))

        w_rows = [sb(f"{n}_rows", [P, KC, D]) for n in ("wq", "wk", "wv")]
        w_turned = [sb(f"{n}_turned", [P, KC, D]) for n in ("wq", "wk", "wv")]
        bq, bk, bv_row = sb("bq", [P, KC]), sb("bk", [P, KC]), sb("bv_row", [P, D])
        stats, mv = sb("stats", [P, TT, 6]), sb("mv", [P, TT, 2])
        var_eps, rstd = sb("var_eps", [P, TT]), sb("rstd", [P, TT])
        hn, ht = sb("hn", [P, TT, D]), sb("ht", [P, KC, SEQ])
        ctx_in_sb = [sb(f"ctx_in{i}", [P, TT, D]) for i in range(2)]
        ctx_t = sb("ctx_t", [P, KC, SEQ])
        q_t = [sb(f"q_t{i}", [P, KC, SEQ]) for i in range(2)]
        k_t = [sb(f"k_t{i}", [P, KC, SEQ]) for i in range(2)]
        values = [sb(f"values{i}", [P, TT, D]) for i in range(2)]
        row_max, minus_max = sb("row_max", [P, 2]), sb("minus_max", [P, 2])
        sums, inv_sums = sb("sums", [P, TT]), sb("inv_sums", [P, TT])
        probs = [sb(f"probs{i}", [P, SEQ]) for i in range(2)]
        probs_t = [sb(f"probs_t{i}", [P, TT, P]) for i in range(2)]
        score_ps, turn_ps, out_ps, misc_ps = psum("score"), psum("turn"), psum("out"), psum("misc")

        zeros = sb("zeros", [P, ZERO_TILES * D])
        zeros_set, zeroed = sem("zeros_set"), sem("zeroed")
        weights_in, w_full, w_ready = sem("weights_in"), sem("w_full"), sem("w_ready")
        ctx_loaded = [sem(f"ctx_loaded{i}") for i in range(2)]
        ln_steps, rstd_done = sem("ln_steps"), sem("rstd_done")
        scores_done, max_done, minus_done, exp_done = sem("scores_done"), sem("max_done"), sem("minus_done"), sem("exp_done")
        turn_full, turn_free, out_full, inv_done, out_free = (sem(n) for n in ("turn_full", "turn_free", "out_full", "inv_done", "out_free"))
        misc_full, misc_free = [sem(f"misc_full{i}") for i in range(2)], [sem(f"misc_free{i}") for i in range(2)]
        passed = sem("passed")
        W_ALL = 6 * 16

        def slots(c, kind):
            for qt in range(TT):
                score = (c, qt) if runs(kind, 0) else None
                turn = ((c, qt - 1) if qt >= 1 else (c - 1, TT - 1)) if runs(kind, 0 if qt >= 1 else -1) else None
                out = ((c, qt - 2) if qt >= 2 else (c - 1, qt + 2)) if runs(kind, 0 if qt >= 2 else -1) else None
                yield qt, score, turn, out

        def hooks(c, kind, g, step):
            for job, off, bank in CROSS_HOOKS.get((g, step), []):
                if runs(kind, off):
                    turn = CROSS_TURNS.before(c, kind, job) if bank is not None else None
                    yield job, c + off, bank, turn

        with nc.Block() as block:

            @block.sync
            def _(sp):
                for src, dst in zip((w["wq"], w["wk"], w["wv"]), w_rows):
                    sp.dma_start(dst[:], src.rearrange("(c p) n -> p c n", p=P)).then_inc(weights_in, 16)
                for src, dst in ((w["bq"], bq), (w["bk"], bk)):
                    sp.dma_start(dst[:], src.rearrange("(c p) -> p c", p=P),
                                 allow_slow_non_contiguous=True).then_inc(weights_in, 16)
                sp.dma_start(bv_row[:], w["bv"].rearrange("(o n) -> o n", o=1).to_broadcast([P, D])).then_inc(weights_in, 16)

                sp.dma_start(ctx_in_sb[0][:], ctx_dram[0].rearrange("(t p) d -> p t d", p=P)).then_inc(ctx_loaded[0], 16)
                sp.dma_start(ctx_in_sb[1][:], ctx_dram[1].rearrange("(t p) d -> p t d", p=P)).then_inc(ctx_loaded[1], 16)
                sp.wait_ge(zeros_set, 1)
                by_row = sorted_dram.rearrange("(p n a) d -> n p (a d)", p=P, a=ZERO_TILES)
                for n in range((MT + 1) // ZERO_TILES):
                    sp.dma_start(by_row[n], zeros[:]).then_inc(zeroed, 16)
                mid_turns = CROSS_TURNS.count(MID, 1)
                at = CROSS_TURNS.before(-1, PRO, "ct1") + 1
                sp.wait_ge(misc_free[1], at)
                sp.dma_start(ctx_in_sb[0][:], ctx_dram[2].rearrange("(t p) d -> p t d", p=P)).then_inc(ctx_loaded[0], 16)
                at = CROSS_TURNS.before(0, FIRST, "ct1") + 1
                sp.wait_ge(misc_free[1], at)
                sp.dma_start(ctx_in_sb[1][:], ctx_dram[3].rearrange("(t p) d -> p t d", p=P)).then_inc(ctx_loaded[1], 16)
                with sp.Fori(0, (NSEQ - 4) // 2) as i:
                    for k in range(2):
                        sp.wait_ge(misc_free[1], i * (2 * mid_turns) + (at + (k + 1) * mid_turns))
                        sp.dma_start(ctx_in_sb[k][:], ctx_dram[bass.ds(i * 2 + (4 + k), 1), :, :].rearrange("o (t p) d -> p (o t) d", p=P)
                                     ).then_inc(ctx_loaded[k], 16)
                sp.wait_ge(zeroed, (MT + 1) // ZERO_TILES * 16)

            @block.tensor
            def _(pe):
                pe.wait_ge(weights_in, W_ALL)
                for rows, out in zip(w_rows, (misc_ps[0], misc_ps[1], score_ps[0])):
                    for kc in range(KC):
                        for ec in range(KC):
                            mm = pe.transpose(out[:, (kc * KC + ec) * P:(kc * KC + ec + 1) * P],
                                              rows[:, ec, kc * P:(kc + 1) * P], ident[:])
                    mm.then_inc(w_full, 1)
                pe.wait_ge(w_ready, 3)

                def product(out, n, lhs, rhs, sem_=None):
                    for kc in range(n):
                        mm = pe.matmul(out, lhs(kc), rhs(kc), start=(kc == 0), stop=(kc == n - 1), skip_group_check=True)
                    if sem_ is not None:
                        mm.then_inc(sem_, 1)

                def body(c, kind, parity):
                    for qt, score, turn_, out_ in slots(c, kind):
                        if score:
                            n = c * TT + qt
                            wait(pe, exp_done, n - 1)
                            product(score_ps[qt % 2][:], KC, lambda kc: q_t[parity][:, kc, qt * P:(qt + 1) * P],
                                    lambda kc: k_t[parity][:, kc, :], scores_done)
                        if turn_:
                            tc, tq = turn_
                            n = tc * TT + tq
                            pe.wait_ge(exp_done, n + 1)
                            wait(pe, turn_free, n - 1)
                            for kt in range(TT):
                                mm = pe.transpose(turn_ps[tq % 2][:, kt * P:(kt + 1) * P], probs[tq % 2][:, kt * P:(kt + 1) * P], ident[:])
                            mm.then_inc(turn_full, 1)
                        if out_:
                            oc, oq = out_
                            n = oc * TT + oq
                            op = parity if qt >= 2 else 1 - parity
                            pe.wait_ge(turn_free, n + 1)
                            wait(pe, out_free, n - 1)
                            product(out_ps[oq % 2][:, 0:D], TT, lambda kt: probs_t[oq % 2][:, kt, :], lambda kt: values[op][:, kt, :], out_full)
                        for step in range(CROSS_STEPS):
                            for job, b, bank, turn in hooks(c, kind, qt, step):
                                if bank is None:
                                    continue
                                out, full = misc_ps[bank], misc_full[bank]
                                wait(pe, misc_free[bank], turn)
                                k = int(job[-1])
                                if job[:2] == "ct":
                                    if k == 0:
                                        pe.wait_ge(ctx_loaded[1 - parity], (b - (1 - parity)) * 8 + 16)
                                    for t in range(TT):
                                        mm = pe.transpose(out[:, t * P:(t + 1) * P], ctx_in_sb[1 - parity][:, t, k * P:(k + 1) * P], ident[:])
                                    mm.then_inc(full, 1)
                                elif job[:2] == "ht":
                                    pe.wait_ge(ln_steps, (b + 1) * 4)
                                    for t in range(TT):
                                        mm = pe.transpose(out[:, t * P:(t + 1) * P], hn[:, t, k * P:(k + 1) * P], ident[:])
                                    mm.then_inc(full, 1)
                                elif job[0] in "qk":
                                    if k == 0:
                                        pe.wait_ge(misc_free[1], CROSS_TURNS.before(c, kind, job[0] + "1"))
                                    src, wt = (ht, w_turned[0]) if job[0] == "q" else (ctx_t, w_turned[1])
                                    product(out[:], KC, lambda kc: wt[:, kc, k * P:(k + 1) * P], lambda kc: src[:, kc, :], full)
                                else:
                                    for t in range(2):
                                        product(out[:, t * D:(t + 1) * D], KC, lambda kc: ctx_t[:, kc, (2 * k + t) * P:(2 * k + t + 1) * P],
                                                lambda kc: w_turned[2][:, kc, :], full if t == 1 else None)

                each_body(pe, body)

            @block.scalar
            def _(act):
                for n, src in enumerate((misc_ps[0], misc_ps[1], score_ps[0])):
                    act.wait_ge(w_full, n + 1)
                    act.activation(w_turned[n][:].rearrange("p c n -> p (c n)"), src[:], ACT.Copy).then_inc(w_ready, 1)
                act.wait_ge(weights_in, W_ALL)

                def body(c, kind, parity):
                    for qt, score, turn_, out_ in slots(c, kind):
                        if score:
                            n = c * TT + qt
                            act.wait_ge(minus_done, n + 1)
                            act.activation(probs[qt % 2][:], score_ps[qt % 2][:], ACT.Exp, bias=minus_max[:, qt % 2:qt % 2 + 1],
                                           accum_out=sums[:, qt:qt + 1]).then_inc(exp_done, 1)
                        if turn_:
                            tc, tq = turn_
                            act.wait_ge(turn_full, tc * TT + tq + 1)
                            act.activation(probs_t[tq % 2][:].rearrange("p t n -> p (t n)"), turn_ps[tq % 2][:], ACT.Copy).then_inc(turn_free, 1)
                        for step in range(CROSS_STEPS):
                            for job, b, bank, turn in hooks(c, kind, qt, step):
                                if bank is None or job[0] == "v":
                                    continue
                                k = int(job[-1])
                                act.wait_ge(misc_full[bank], turn + 1)
                                src, free = misc_ps[bank], misc_free[bank]
                                if job[:2] in ("ct", "ht"):
                                    act.activation((ctx_t if job[0] == "c" else ht)[:, k, :], src[:], ACT.Copy).then_inc(free, 1)
                                else:
                                    dst, bias = (q_t, bq) if job[0] == "q" else (k_t, bk)
                                    act.activation(dst[1 - parity][:, k, :], src[:], ACT.Identity, bias=bias[:, k:k + 1]).then_inc(free, 1)

                each_body(act, body)

            @block.vector
            def _(dve):
                dve.wait_ge(weights_in, W_ALL)

                def body(c, kind, parity):
                    for qt, score, turn_, out_ in slots(c, kind):
                        if score:
                            n = c * TT + qt
                            dve.wait_ge(scores_done, n + 1)
                            dve.tensor_reduce(row_max[:, qt % 2:qt % 2 + 1], score_ps[qt % 2][:], AX_X, ALU.max).then_inc(max_done, 1)
                            dve.wait_ge(max_done, n + 1)
                            dve.tensor_scalar(minus_max[:, qt % 2:qt % 2 + 1], row_max[:, qt % 2:qt % 2 + 1], -1.0, None, ALU.mult).then_inc(minus_done, 1)
                        if out_:
                            oc, oq = out_
                            n = oc * TT + oq
                            dve.wait_ge(exp_done, n + 1)
                            dve.reciprocal(inv_sums[:, oq:oq + 1], sums[:, oq:oq + 1]).then_inc(inv_done, 1)
                            dve.wait_ge(inv_done, n + 1)
                            dve.wait_ge(out_full, n + 1)
                            xs = x_sb[:, oc * TT + oq, :]
                            dve.scalar_tensor_tensor(out=xs, in0=out_ps[oq % 2][:, 0:D], scalar=inv_sums[:, oq:oq + 1], in1=xs,
                                                     op0=ALU.mult, op1=ALU.add).then_inc(out_free, 1)
                        for step in range(CROSS_STEPS):
                            for job, b, bank, turn in hooks(c, kind, qt, step):
                                xt = (lambda t: x_sb[:, b * TT + t, :])
                                if job == "stats":
                                    for t in range(TT):
                                        ins = dve.bn_stats(stats[:, t, :], xt(t))
                                    ins.then_inc(ln_steps, 1)
                                    wait_apart(dve, ln_steps, b * 4 + 1, passed)
                                    for t in range(TT):
                                        ins = dve.bn_aggr(mv[:, t, :], stats[:, t, :])
                                    ins.then_inc(ln_steps, 1)
                                    dve.wait_ge(ln_steps, b * 4 + 2)
                                    dve.tensor_scalar(var_eps[:], mv[:, :, 1], EPS, None, ALU.add).then_inc(ln_steps, 1)
                                elif job == "norm":
                                    dve.wait_ge(rstd_done, b + 1)
                                    for t in range(TT):
                                        ins = dve.tensor_scalar(hn[:, t, :], xt(t), mv[:, t, 0:1], rstd[:, t:t + 1], ALU.subtract, ALU.mult)
                                    ins.then_inc(ln_steps, 1)
                                elif job[0] == "v":
                                    k = int(job[-1])
                                    dve.wait_ge(misc_full[bank], turn + 1)
                                    dve.tensor_tensor(values[1 - parity][:, 2 * k:2 * k + 2, :], misc_ps[bank][:].rearrange("p (t n) -> p t n", t=2),
                                                      bv_row[:].unsqueeze(1).to_broadcast([P, 2, D]), ALU.add).then_inc(misc_free[bank], 1)

                each_body(dve, body)

            @block.gpsimd
            def _(pool):
                pool.memset(zeros[:], 0.0).then_inc(zeros_set, 1)

                def body(c, kind, parity):
                    if runs(kind, 1):
                        b = c + 1
                        pool.wait_ge(ln_steps, b * 4 + 3)
                        pool.tensor_tensor(rstd[:], var_eps[:], minus_half[:].to_broadcast([P, TT]), ALU.pow).then_inc(rstd_done, 1)

                each_body(pool, body)


def routing_phase(nc, ctx, consts, y_sb, w, sorted_dram, weights):
    ident, minus_half = consts["ident"], consts["minus_half"]

    def keep(n, shape, dt=F32):
        return ctx.enter_context(nc.sbuf_tensor(f"moe_{n}", shape, dt))

    row_of = [keep(f"row_of{k}", [P, NT], U32) for k in range(2)]
    weight_of = [keep(f"weight_of{k}", [P, NT]) for k in range(2)]
    tile_expert = keep("tile_expert", [1, MT + 1], I32)
    ln_scale, ln_shift = keep("ln_scale", [P, KC]), keep("ln_shift", [P, KC])
    with ExitStack() as inner:
        def sb(n, shape, dt=F32):
            return inner.enter_context(nc.sbuf_tensor(f"route_{n}", shape, dt))

        def sem(n):
            return inner.enter_context(nc.semaphore(f"route_{n}"))

        def psum(n):
            return inner.enter_context(nc.psum_tensor(f"route_{n}", [P, SEQ], F32))

        gate = sb("gate", [P, KC, E_N])
        stats, mv = [sb(f"stats{i}", [P, TT, 6]) for i in range(2)], [sb(f"mv{i}", [P, TT, 2]) for i in range(2)]
        var_eps, rstd = [sb(f"var_eps{i}", [P, TT]) for i in range(2)], [sb(f"rstd{i}", [P, TT]) for i in range(2)]
        hn = [sb(f"hn{i}", [P, TT, D]) for i in range(2)]
        ht = [sb(f"ht{i}", [P, KC, SEQ]) for i in range(2)]
        logits = sb("logits", [P, NT, E_N])
        top, top_at = sb("top", [P, NT, 8]), sb("top_at", [P, NT, 8], U32)
        expert_of = sb("expert_of", [P, NT, 2])
        iota_i, iota_e = sb("iota_i", [P, E_N], I32), sb("iota_e", [P, E_N])
        iota_ti, iota_t = sb("iota_ti", [1, MT + 1], I32), sb("iota_t", [1, MT + 1])
        one_hot = [sb(f"one_hot{k}", [P, NT, E_N]) for k in range(2)]
        chosen = sb("chosen", [P, NT, E_N], BF16)
        before_bf, ones_bf = sb("before_bf", [P, P], BF16), sb("ones_bf", [P, P], BF16)
        ones = sb("ones", [P, NT])
        total, upto, base = sb("total", [P, NT, E_N]), sb("upto", [P, NT, E_N]), sb("base", [P, NT, E_N])
        padded, padded_i, n_tiles, tiles_upto = sb("padded", [P, E_N]), sb("padded_i", [P, E_N], I32), sb("n_tiles", [P, E_N]), sb("tiles_upto", [P, E_N])
        picked = [sb(f"picked{k}", [P, NT, E_N]) for k in range(2)]
        row_f = [sb(f"row_f{k}", [P, NT]) for k in range(2)]
        passed_tile, tile_f = sb("passed_tile", [1, MT + 1, E_N]), sb("tile_f", [1, MT + 1])
        diff, ratio, denom = sb("diff", [P, NT]), sb("ratio", [P, NT]), sb("denom", [P, NT])
        turn_ps = [[psum(f"turn{i}{k}") for k in range(2)] for i in range(2)]
        gate_ps = [psum(f"gate{i}") for i in range(2)]
        count_ps = psum("count")

        loaded, made, iota_made = sem("loaded"), sem("made"), sem("iota_made")
        ln_steps, rstd_done = sem("ln_steps"), sem("rstd_done")
        turned, ht_done, gated, logits_done = sem("turned"), sem("ht_done"), sem("gated"), sem("logits_done")
        steps, chosen_done, counted, ratio_done, rows_done, scattered = (
            sem(n) for n in ("steps", "chosen_done", "counted", "ratio_done", "rows_done", "scattered"))
        passed = sem("passed")

        with nc.Block() as block:

            @block.sync
            def _(sp):
                sp.dma_start(gate[:], w["gate_w"].rearrange("(c p) n -> p c n", p=P)).then_inc(loaded, 16)
                for src, dst in ((w["ln2_scale"], ln_scale), (w["ln2_shift"], ln_shift)):
                    sp.dma_start(dst[:], src.rearrange("(c p) -> p c", p=P), allow_slow_non_contiguous=True).then_inc(loaded, 16)
                for name, dst, chunks in weights["parts"]:
                    for e in range(E_N):
                        sp.dma_start(dst[:, e], w[name][e].rearrange("(c p) n -> p c n", p=P)).then_inc(weights["in"], 16)

            @block.gpsimd
            def _(pool):
                pool.memset(before_bf[:], 1.0).then_inc(made, 1)
                pool.wait_ge(made, 1)
                pool.affine_select(out=before_bf[:], in_=before_bf[:], compare_op=ALU.is_ge, fill=0.0, base=-1,
                                   pattern=[[1, P]], channel_multiplier=-1).then_inc(made, 1)
                pool.memset(ones_bf[:], 1.0).then_inc(made, 1)
                pool.iota(iota_i[:], pattern=[[1, E_N]], base=0, channel_multiplier=0).then_inc(iota_made, 1)
                pool.wait_ge(iota_made, 1)
                pool.iota(iota_ti[:], pattern=[[1, MT + 1]], base=0, channel_multiplier=0).then_inc(iota_made, 1)
                with pool.Fori(0, NSEQ // 2) as i:
                    for k in range(2):
                        pool.wait_ge(ln_steps, i * 8 + (k * 4 + 3))
                        pool.tensor_tensor(rstd[k][:], var_eps[k][:], minus_half[:].to_broadcast([P, TT]), ALU.pow).then_inc(rstd_done, 1)
                pool.wait_ge(rows_done, 2)
                for t in range(NT):
                    for k in range(2):
                        pool.indirect_dma_start(out=sorted_dram, out_offset=bass.IndirectOffsetOnAxis(ap=row_of[k][:, t:t + 1], axis=0),
                                                in_=y_sb[:, t, :], in_offset=None).then_inc(scattered, 16)
                pool.wait_ge(scattered, 2 * NT * 16)

            @block.tensor
            def _(pe):
                pe.wait_ge(loaded, 48)
                with pe.Fori(0, NSEQ // 2) as i:
                    for k in range(2):
                        c = i * 2 + k
                        pe.wait_ge(ln_steps, i * 8 + (k * 4 + 4))
                        for kc in range(KC):
                            for t in range(TT):
                                mm = pe.transpose(turn_ps[k][kc][:, t * P:(t + 1) * P], hn[k][:, t, kc * P:(kc + 1) * P], ident[:])
                        mm.then_inc(turned, 1)
                        pe.wait_ge(ht_done, c + 1)
                        for t in range(TT):
                            for kc in range(KC):
                                mm = pe.matmul(gate_ps[k][:, t * E_N:(t + 1) * E_N], ht[k][:, kc, t * P:(t + 1) * P], gate[:, kc, :],
                                               start=(kc == 0), stop=(kc == KC - 1), skip_group_check=True)
                        mm.then_inc(gated, 1)
                pe.wait_ge(chosen_done, 1)
                pe.wait_ge(made, 3)
                flat = chosen[:].rearrange("p t e -> p (t e)")
                pe.matmul(count_ps[:, 0:NT * E_N], before_bf[:], flat, start=True, stop=True, skip_group_check=True)
                pe.matmul(count_ps[:, NT * E_N:2 * NT * E_N], ones_bf[:], flat, start=True, stop=True,
                          skip_group_check=True).then_inc(counted, 1)

            @block.scalar
            def _(act):
                act.wait_ge(loaded, 48)
                with act.Fori(0, NSEQ // 2) as i:
                    for k in range(2):
                        act.wait_ge(turned, i * 2 + (k + 1))
                        act.activation(y_sb[:, bass.ds(i * (2 * TT) + k * TT, TT), :], hn[k][:], ACT.Copy)
                        for kc in range(KC):
                            ins = act.activation(ht[k][:, kc, :], turn_ps[k][kc][:], ACT.Identity, scale=ln_scale[:, kc:kc + 1],
                                                 bias=ln_shift[:, kc:kc + 1])
                        ins.then_inc(ht_done, 1)
                act.wait_ge(steps, 3)
                act.activation(ratio[:], diff[:], ACT.Exp).then_inc(ratio_done, 1)

            @block.vector
            def _(dve):
                with dve.Fori(0, NSEQ // 2) as i:
                    for k in range(2):
                        c = i * 2 + k
                        for t in range(TT):
                            ins = dve.bn_stats(stats[k][:, t, :], y_sb[:, c * TT + t, :])
                        ins.then_inc(ln_steps, 1)
                        wait_apart(dve, ln_steps, i * 8 + (k * 4 + 1), passed)
                        for t in range(TT):
                            ins = dve.bn_aggr(mv[k][:, t, :], stats[k][:, t, :])
                        ins.then_inc(ln_steps, 1)
                        dve.wait_ge(ln_steps, i * 8 + (k * 4 + 2))
                        dve.tensor_scalar(var_eps[k][:], mv[k][:, :, 1], EPS, None, ALU.add).then_inc(ln_steps, 1)
                        dve.wait_ge(rstd_done, i * 2 + (k + 1))
                        for t in range(TT):
                            ins = dve.tensor_scalar(hn[k][:, t, :], y_sb[:, c * TT + t, :], mv[k][:, t, 0:1], rstd[k][:, t:t + 1], ALU.subtract, ALU.mult)
                        ins.then_inc(ln_steps, 1)
                        dve.wait_ge(gated, c + 1)
                        dve.tensor_copy(logits[:, bass.ds(c * TT, TT), :], gate_ps[k][:, 0:TT * E_N].rearrange("p (t e) -> p t e", t=TT)
                                        ).then_inc(logits_done, 1)
                dve.wait_ge(logits_done, NSEQ)
                step = 0

                def done(ins):
                    nonlocal step
                    step += 1
                    ins.then_inc(steps, 1)
                    dve.wait_ge(steps, step)

                for t in range(NT):
                    ins = dve.max(top[:, t, :], logits[:, t, :])
                done(ins)
                for t in range(NT):
                    ins = dve.max_index(top_at[:, t, :], top[:, t, :], logits[:, t, :])
                done(ins)
                done(dve.tensor_tensor(diff[:], top[:, :, 1], top[:, :, 0], ALU.subtract))
                dve.wait_ge(iota_made, 2)
                dve.tensor_copy(iota_e[:], iota_i[:])
                dve.tensor_copy(iota_t[:], iota_ti[:])
                dve.memset(ones[:], 1.0)
                done(dve.tensor_copy(expert_of[:], top_at[:, :, 0:2]))
                for k in range(2):
                    ins = dve.tensor_tensor(one_hot[k][:], iota_e[:].unsqueeze(1).to_broadcast([P, NT, E_N]),
                                            expert_of[:, :, k:k + 1].to_broadcast([P, NT, E_N]), ALU.is_equal)
                done(ins)
                dve.tensor_tensor(chosen[:], one_hot[0][:], one_hot[1][:], ALU.add).then_inc(chosen_done, 1)
                dve.wait_ge(ratio_done, 1)
                done(dve.tensor_scalar(denom[:], ratio[:], 1.0, None, ALU.add))
                done(dve.reciprocal(weight_of[0][:], denom[:]))
                dve.tensor_tensor(weight_of[1][:], weight_of[0][:], ratio[:], ALU.mult)
                dve.wait_ge(counted, 1)
                done(dve.tensor_copy(total[:].rearrange("p t e -> p (t e)"), count_ps[:, NT * E_N:2 * NT * E_N]))
                for e in range(E_N):
                    ins = dve.tensor_tensor_scan(upto[:, :, e], ones[:], total[:, :, e], 0.0, ALU.mult, ALU.add)
                done(ins)
                done(dve.tensor_scalar(padded[:], upto[:, NT - 1, :], float(P - 1), None, ALU.add))
                done(dve.tensor_copy(padded_i[:], padded[:]))
                shift = P.bit_length() - 1
                done(dve.tensor_scalar(padded_i[:], padded_i[:], shift, None, ALU.logical_shift_right))
                done(dve.tensor_copy(n_tiles[:], padded_i[:]))
                done(dve.tensor_tensor_scan(tiles_upto[:], ones[:, 0:E_N], n_tiles[:], 0.0, ALU.mult, ALU.add))
                done(dve.tensor_tensor(padded[:], tiles_upto[:], n_tiles[:], ALU.subtract))
                done(dve.tensor_tensor(base[:], upto[:], total[:], ALU.subtract))
                done(dve.tensor_tensor(base[:].rearrange("p t e -> p (t e)"), count_ps[:, 0:NT * E_N],
                                       base[:].rearrange("p t e -> p (t e)"), ALU.add))
                done(dve.scalar_tensor_tensor(out=base[:], in0=padded[:].unsqueeze(1).to_broadcast([P, NT, E_N]), scalar=float(P),
                                              in1=base[:], op0=ALU.mult, op1=ALU.add))
                for k in range(2):
                    ins = dve.tensor_tensor(picked[k][:], one_hot[k][:], base[:], ALU.mult)
                done(ins)
                for k in range(2):
                    ins = dve.tensor_reduce(row_f[k][:], picked[k][:], AX_X, ALU.add)
                done(ins)
                for k in range(2):
                    dve.tensor_copy(row_of[k][:], row_f[k][:]).then_inc(rows_done, 1)
                done(dve.tensor_tensor(passed_tile[:], iota_t[:].unsqueeze(2).to_broadcast([1, MT + 1, E_N]),
                                       tiles_upto[0:1, :].unsqueeze(1).to_broadcast([1, MT + 1, E_N]), ALU.is_ge))
                done(dve.tensor_reduce(tile_f[:], passed_tile[:], AX_X, ALU.add))
                done(dve.tensor_scalar(tile_f[:], tile_f[:], float(E_N - 1), None, ALU.min))
                done(dve.tensor_copy(tile_expert[:], tile_f[:]))

    return row_of, weight_of, tile_expert, ln_scale, ln_shift


def expert_phase(nc, consts, weights, tile_expert, ln_scale, ln_shift, sorted_dram, expert_dram):
    ident = consts["ident"]
    w1, w2, w3 = (dst for _, dst, _ in weights["parts"])
    with ExitStack() as ctx:
        def sb(n, shape, dt=F32):
            return [ctx.enter_context(nc.sbuf_tensor(f"expert_{n}{i}", shape, dt)) for i in range(2)]

        def psum(n, count):
            return [ctx.enter_context(nc.psum_tensor(f"expert_{n}{i}", [P, HID], F32)) for i in range(count)]

        def sem(n):
            return ctx.enter_context(nc.semaphore(f"expert_{n}"))

        rows, rows_t = sb("rows", [P, D]), sb("rows_t", [P, KC, P])
        silu, hidden, hidden_t, result = sb("silu", [P, HID]), sb("hidden", [P, HID]), sb("hidden_t", [P, HC, P]), sb("result", [P, D])
        turn_ps, a_ps, b_ps, ht_ps, out_ps = psum("turn", 1), psum("a", 2), psum("b", 2), psum("ht", 1), psum("out", 2)
        rows_in = [sem(f"rows_in{i}") for i in range(2)]
        turned, rows_t_done, a_done, b_done, silu_done, hidden_done = (
            sem(n) for n in ("turned", "rows_t_done", "a_done", "b_done", "silu_done", "hidden_done"))
        ht_full, ht_done, out_full, result_done = (sem(n) for n in ("ht_full", "ht_done", "out_full", "result_done"))
        stored = [sem(f"stored{i}") for i in range(2)]

        def each_step(eng, emit):
            emit(-2, 0)
            emit(-1, 1)
            with eng.Fori(0, MT // 2) as i:
                for k in range(2):
                    emit(i * 2 + k, k)
            emit(MT - 1, 0)

        def parts(j):
            static = isinstance(j, int)
            return (j + 2 if not static or j < MT - 1 else None,
                    j + 1 if not static or -1 <= j < MT - 1 else None,
                    j if not static or j >= 0 else None)

        assert MT % 2 == 1

        with nc.Block() as block:

            @block.sync
            def _(sp):
                def load(j, k):
                    sp.dma_start(rows[k][:], sorted_dram[bass.ds(j * P, P), :]).then_inc(rows_in[k], 16)

                load(0, 0)
                load(1, 1)

                with sp.Fori(0, MT // 2) as i:
                    for k in range(2):
                        sp.wait_ge(turned, i * 2 + (k + 1))
                        sp.dma_start(rows[k][:], sorted_dram[bass.ds(i * (2 * P) + (k + 2) * P, P), :]).then_inc(rows_in[k], 16)
                        sp.wait_ge(result_done, i * 2 + (k + 1))
                        sp.dma_start(expert_dram[bass.ds(i * (2 * P) + k * P, P), :], result[k][:]).then_inc(stored[k], 16)
                sp.wait_ge(result_done, MT)
                sp.dma_start(expert_dram[(MT - 1) * P:MT * P, :], result[0][:]).then_inc(stored[0], 16)
                sp.wait_ge(stored[0], (MT // 2 + 1) * 16)
                sp.wait_ge(stored[1], MT // 2 * 16)

            @block.tensor
            def _(pe):
                pe.wait_ge(weights["in"], 3 * E_N * 16)

                def expert(j):
                    return pe.value_load(tile_expert[0:1, bass.ds(j, 1)], min_val=0, max_val=E_N - 1)

                def step(j, k):
                    turn, hid, out = parts(j)
                    if turn is not None:
                        wait(pe, rows_t_done, turn)
                        pe.wait_ge(rows_in[k], (turn - k) * 8 + 16)
                        for kc in range(KC):
                            mm = pe.transpose(turn_ps[0][:, kc * P:(kc + 1) * P], rows[k][:, kc * P:(kc + 1) * P], ident[:])
                        mm.then_inc(turned, 1)
                    if hid is not None:
                        h = 1 - k
                        e = expert(hid)
                        pe.wait_ge(rows_t_done, hid + 1)
                        wait(pe, hidden_done, hid - 1)
                        for ps, wt, full in ((a_ps, w1, a_done), (b_ps, w2, b_done)):
                            for kc in range(KC):
                                mm = pe.matmul(ps[h][:], rows_t[h][:, kc, :], wt[:, e, kc, :], start=(kc == 0), stop=(kc == KC - 1))
                            mm.then_inc(full, 1)
                    if out is not None:
                        e = expert(out)
                        pe.wait_ge(hidden_done, out + 1)
                        wait(pe, ht_done, out)
                        for hc in range(HC):
                            mm = pe.transpose(ht_ps[0][:, hc * P:(hc + 1) * P], hidden[k][:, hc * P:(hc + 1) * P], ident[:])
                        mm.then_inc(ht_full, 1)
                        pe.wait_ge(ht_done, out + 1)
                        for hc in range(HC):
                            mm = pe.matmul(out_ps[k][:, 0:D], hidden_t[k][:, hc, :], w3[:, e, hc, :], start=(hc == 0), stop=(hc == HC - 1))
                        mm.then_inc(out_full, 1)

                each_step(pe, step)

            @block.scalar
            def _(act):
                def step(j, k):
                    turn, hid, out = parts(j)
                    if turn is not None:
                        act.wait_ge(turned, turn + 1)
                        for kc in range(KC):
                            ins = act.activation(rows_t[k][:, kc, :], turn_ps[0][:, kc * P:(kc + 1) * P], ACT.Identity,
                                                 scale=ln_scale[:, kc:kc + 1], bias=ln_shift[:, kc:kc + 1])
                        ins.then_inc(rows_t_done, 1)
                    if out is not None:
                        act.wait_ge(ht_full, out + 1)
                        act.activation(hidden_t[k][:].rearrange("p c n -> p (c n)"), ht_ps[0][:], ACT.Copy).then_inc(ht_done, 1)
                    if hid is not None:
                        act.wait_ge(a_done, hid + 1)
                        act.activation(silu[1 - k][:], a_ps[1 - k][:], ACT.Silu).then_inc(silu_done, 1)

                each_step(act, step)

            @block.vector
            def _(dve):
                def step(j, k):
                    turn, hid, out = parts(j)
                    if hid is not None:
                        h = 1 - k
                        dve.wait_ge(silu_done, hid + 1)
                        dve.wait_ge(b_done, hid + 1)
                        dve.tensor_tensor(hidden[h][:], b_ps[h][:], silu[h][:], ALU.mult).then_inc(hidden_done, 1)
                    if out is not None:
                        dve.wait_ge(out_full, out + 1)
                        wait(dve, stored[k], (out - k) * 8)
                        dve.tensor_copy(result[k][:], out_ps[k][:, 0:D]).then_inc(result_done, 1)

                each_step(dve, step)


def combine_phase(nc, x_sb, row_of, weight_of, expert_dram, out_dram):
    RING = 4
    with ExitStack() as ctx:
        got = [[ctx.enter_context(nc.sbuf_tensor(f"got{i}_{k}", [P, D], F32)) for k in range(2)] for i in range(RING)]
        fetched = [ctx.enter_context(nc.semaphore(f"fetched{i}")) for i in range(RING)]
        summed, stored = ctx.enter_context(nc.semaphore("summed")), ctx.enter_context(nc.semaphore("stored"))
        with nc.Block() as block:

            @block.gpsimd
            def _(pool):
                for t in range(NT):
                    if t >= RING:
                        pool.wait_ge(summed, 2 * (t - RING + 1))
                    for k in range(2):
                        pool.indirect_dma_start(out=got[t % RING][k][:], out_offset=None, in_=expert_dram,
                                                in_offset=bass.IndirectOffsetOnAxis(ap=row_of[k][:, t:t + 1], axis=0)
                                                ).then_inc(fetched[t % RING], 16)

            @block.vector
            def _(dve):
                for t in range(NT):
                    dve.wait_ge(fetched[t % RING], (t // RING + 1) * 32)
                    xt = x_sb[:, t, :]
                    for k in range(2):
                        dve.scalar_tensor_tensor(out=xt, in0=got[t % RING][k][:], scalar=weight_of[k][:, t:t + 1], in1=xt,
                                                 op0=ALU.mult, op1=ALU.add).then_inc(summed, 1)
                        dve.wait_ge(summed, 2 * t + k + 1)

            @block.sync
            def _(sp):
                for t in range(NT):
                    sp.wait_ge(summed, 2 * t + 2)
                    sp.dma_start(out_dram[t // TT, (t % TT) * P:(t % TT + 1) * P, :], x_sb[:, t, :]).then_inc(stored, 16)
                sp.wait_ge(stored, NT * 16)


def decoder_layer(nc, a, out_dram):
    with ExitStack() as ctx:
        x_sb = ctx.enter_context(nc.sbuf_tensor("x_sb", [P, NT, D], F32))
        sorted_dram = nc.dram_tensor("sorted_rows", ((MT + 1) * P, D), F32).ap()
        expert_dram = nc.dram_tensor("expert_rows", (MT * P, D), F32).ap()
        consts = make_constants(nc, ctx)
        attention_phase(nc, consts, x_sb, "self", {n: a["L0_attn_" + m] for n, m in dict(
            wq="Wq", wk="Wk", wv="Wv", wo="Wo", bq="bq", bk="bk", bv="bv", bo="bo").items()}, x_dram=a["x"])
        cross_phase(nc, consts, x_sb, {n: a["L0_xattn_" + m] for n, m in dict(
            wq="Wq", wk="Wk", wv="Wv", bq="bq", bk="bk", bv="bv").items()}, a["ctx_1024"], sorted_dram)
        with ExitStack() as moe:
            y_sb = moe.enter_context(nc.sbuf_tensor("y_sb", [P, NT, D], F32))
            attention_phase(nc, consts, x_sb, "ffn", {n: a["L0_ffn_" + m] for n, m in dict(
                wq="wq", wk="wk", wv="wv", wo="wo", bo="bo", ln_scale="ln1_scale", ln_shift="ln1_shift").items()}, y_sb=y_sb)
            w1, w2 = (moe.enter_context(nc.sbuf_tensor(n, [P, E_N, KC, HID], F32)) for n in ("w1_sb", "w2_sb"))
            w3 = moe.enter_context(nc.sbuf_tensor("w3_sb", [P, E_N, HC, D], F32))
            weights = {"in": moe.enter_context(nc.semaphore("expert_weights_in")),
                       "parts": [("w1", w1, KC), ("w2", w2, KC), ("w3", w3, HC)]}
            w = {n: a["L0_ffn_" + n] for n in ("gate_w", "ln2_scale", "ln2_shift", "w1", "w2", "w3")}
            row_of, weight_of, tile_expert, ln_scale, ln_shift = routing_phase(nc, moe, consts, y_sb, w, sorted_dram, weights)
            expert_phase(nc, consts, weights, tile_expert, ln_scale, ln_shift, sorted_dram, expert_dram)
            combine_phase(nc, x_sb, row_of, weight_of, expert_dram, out_dram)


_INS = ["x", "ctx_1024"] + ["L0_attn_" + n for n in ("Wq", "bq", "Wk", "bk", "Wv", "bv", "Wo", "bo")] + [
    "L0_xattn_" + n for n in ("Wq", "bq", "Wk", "bk", "Wv", "bv")] + [
    "L0_ffn_" + n for n in ("ln1_scale", "ln1_shift", "wq", "wk", "wv", "wo", "bo", "ln2_scale", "ln2_shift", "gate_w", "w1", "w2", "w3")]


def kernel(**inputs):
    import numpy as _np
    import concourse.bacc as _bacc
    from concourse import mybir as _mybir
    from concourse.bass_utils import run_bass_kernel_spmd as _run

    nc = _bacc.Bacc("TRN2", target_bir_lowering=False, num_devices=1)
    arrays, args = {}, {}
    for name in _INS:
        a = _np.ascontiguousarray(inputs[name])
        arrays[f"in_{name}_dram"] = a
        args[name] = nc.dram_tensor(f"in_{name}_dram", a.shape, _mybir.dt.from_np(a.dtype), kind="ExternalInput").ap()
    out = nc.dram_tensor("out_0_dram", (NSEQ, SEQ, D), F32, kind="ExternalOutput").ap()
    decoder_layer(nc, args, out)
    r = _run(nc, [arrays], core_ids=[0])
    return r.results[0]["out_0_dram"]
```

```python
from contextlib import ExitStack

import concourse.bass as bass
from concourse import mybir

ALU = mybir.AluOpType
ACT = mybir.ActivationFunctionType
AX_X = mybir.AxisListType.X
F32 = mybir.dt.float32
BF16 = mybir.dt.bfloat16
I32 = mybir.dt.int32
U32 = mybir.dt.uint32

P = 128
NSEQ = 8
SEQ = 512
D = 256
KC = D // P
TT = SEQ // P
NT = NSEQ * TT
H = 16
DK = D // H
HG = 4
NG = H // HG
EPS = 1e-5
MASKED = -1e30

E_N = 8
HID = 512
HC = HID // P
MT = (2 * NSEQ * SEQ + E_N * (P - 1)) // P
REGION = NT * P + P
PAD_TILE = E_N * REGION
PLACE, WEIGHT = D, D + 1
ROW = D + 2


def wait(eng, sem, value):
    if not (isinstance(value, int) and value <= 0):
        eng.wait_ge(sem, value)


def wait_apart(eng, sem, value, passed):
    eng.wait_ge(sem, value)
    eng.sem_inc(passed, 1)


PRO, FIRST, MID, LAST, DRAIN = -1, 0, 1, NSEQ - 1, NSEQ


def each_body(eng, emit):
    emit(-1, PRO, 1)
    emit(0, FIRST, 0)
    with eng.Fori(0, (NSEQ - 2) // 2) as i:
        for k in range(2):
            emit(i * 2 + (1 + k), MID, (1 + k) % 2)
    emit(NSEQ - 1, LAST, 1)
    emit(NSEQ, DRAIN, 0)


def runs(kind, off):
    at = {PRO: -1, FIRST: 0, MID: 1, LAST: NSEQ - 1, DRAIN: NSEQ}[kind] + off
    return 0 <= at < NSEQ


class Turns:

    def __init__(self, hooks):
        self.jobs = [(name, off, bank) for at in sorted(hooks) for name, off, bank in hooks[at] if bank is not None]

    def count(self, kind, bank, upto=None):
        n = 0
        for name, off, b in self.jobs:
            if name == upto:
                break
            n += b == bank and runs(kind, off)
        return n

    def before(self, c, kind, name):
        bank = next(b for n, _, b in self.jobs if n == name)
        local = self.count(kind, bank, name)
        pro = self.count(PRO, bank)
        if kind == PRO:
            return local
        if kind == FIRST:
            return pro + local
        first = pro + self.count(FIRST, bank)
        mid = self.count(MID, bank)
        if kind == DRAIN:
            return first + mid * (NSEQ - 2) + self.count(LAST, bank) + local
        return (c - 1) * mid + (first + local)


QROWS = (0, 0, 0, 1, 1, 2)
KROWS = (0, 1, 2, 0, 1, 0)
SROWS = len(QROWS) * DK
MROWS = SROWS + 3

ROW_UNITS = [(0, (0, 1, 2, 3)), (1, (0, 1)), (1, (2, 3))] + [(2, (h,)) for h in range(HG)] + [(3, (h,)) for h in range(HG)]
KEY_UNITS = [(0, (h,)) for h in range(HG)] + [(1, (h,)) for h in range(HG)] + [(2, (0, 1)), (2, (2, 3)), (3, (0, 1, 2, 3))]
NU = len(ROW_UNITS)
assert NU == len(KEY_UNITS)
KEY_DONE = [max(u for u, (kt, _) in enumerate(KEY_UNITS) if kt == t) + 1 for t in range(TT)]
ROW_BANKS = 3
PT_OFF = [HG * sum(SEQ - P * j for j in range(t)) for t in range(TT + 1)]
PV_AT = {1: 0, 4: 1, 7: 2, 9: 3}
VCOLS = 32


def row_before(u, g4):
    return g4 * NU + (u - ROW_BANKS + 1 if u >= ROW_BANKS else {0: 9, 1: 10, 2: 8}[u] + 1 - NU)


ATT_HOOKS = {
    (0, 0): [("stats1", 1, None)],
    (0, 1): [("ut0", -1, 0)],
    (0, 2): [("norm1", 1, None)],
    (0, 3): [("mt3", -1, 1)],
    (0, 4): [("stats2", 1, None)],
    (0, 6): [("norm2", 1, None)],
    (0, 8): [("ht0", 1, 0), ("ht1", 1, 1)],
    (0, 10): [("q0", 1, 0)],
    (1, 1): [("ut1", -1, 0)],
    (1, 3): [("mt0", 0, 1)],
    (1, 4): [("q1", 1, 1)],
    (1, 6): [("k0", 1, 0)],
    (1, 8): [("k1", 1, 1)],
    (2, 1): [("ut2", -1, 0)],
    (2, 3): [("mt1", 0, 1)],
    (3, 1): [("ut3", -1, 0)],
    (3, 3): [("mt2", 0, 1)],
    (3, 4): [("v0", 1, 0), ("v1", 1, 1)],
    (3, 7): [("ct0", -1, 0), ("ct1", -1, 1)],
    (3, 10): [("wo0", -1, 0), ("wo1", -1, 1)],
}
ATT_TURNS = Turns(ATT_HOOKS)
PARTS = ("q0", "q1", "k0", "k1")


def attention_phase(nc, consts, x_sb, name, w, x_dram=None, y_sb=None):
    first = x_dram is not None
    ident, ident_bf, neg_mask, minus_half = consts["ident"], consts["ident_bf"], consts["neg_mask"], consts["minus_half"]
    part_dram = nc.dram_tensor(f"{name}_parts", (2, 4, 3, P, SEQ), BF16).ap()
    max_dram = nc.dram_tensor(f"{name}_max", (NG, 3, HG * TT, P), BF16).ap()
    with ExitStack() as ctx:
        def sb(n, shape, dt=F32):
            return ctx.enter_context(nc.sbuf_tensor(f"{name}_{n}", shape, dt))

        def sem(n):
            return ctx.enter_context(nc.semaphore(f"{name}_{n}"))

        wq, wk, wv, wo = (sb(n, [P, KC, D]) for n in ("wq", "wk", "wv", "wo"))
        bo_row = sb("bo_row", [P, D])
        if first:
            bq, bk = sb("bq", [P, KC]), sb("bk", [P, KC])
            bv_row = sb("bv_row", [P, D])
        else:
            ln_scale, ln_shift = sb("ln_scale", [P, KC]), sb("ln_shift", [P, KC])
        stats, mv = sb("stats", [P, TT, 6]), sb("mv", [P, TT, 2])
        var_eps, rstd = sb("var_eps", [P, TT]), sb("rstd", [P, TT])
        hn = sb("hn", [P, TT, D])
        ht = sb("ht", [P, KC, SEQ])
        proj32 = [sb(f"proj32_{i}", [P, SEQ]) for i in range(2)]
        rest32 = [sb(f"rest32_{i}", [P, SEQ]) for i in range(2)]
        parts = [sb(f"parts_{n}", [P, 3, SEQ], BF16) for n in PARTS]
        q_rows = [sb(f"q_rows{g}", [MROWS, HG, SEQ], BF16) for g in range(NG)]
        k_rows = [sb(f"k_rows{g}", [MROWS, HG, SEQ], BF16) for g in range(NG)]
        maxes = sb("maxes", [P, HG, TT])
        max_rest = sb("max_rest", [P, HG * TT])
        max_bf = sb("max_bf", [P, HG * TT], BF16)
        max_parts = sb("max_parts", [P, P])
        max_rows = sb("max_rows", [3 * HG * TT, P], BF16)
        probs = [sb(f"probs{i}", [P, PT_OFF[TT]]) for i in range(2)]
        values = [sb(f"values{i}", [P, TT, H, VCOLS]) for i in range(2)]
        ctx_raw = sb("ctx_raw", [P, SEQ])
        sums = sb("sums", [P, TT, HG])
        ctx_tok = sb("ctx_tok", [P, TT, D])
        ctx_t = sb("ctx_t", [P, KC, SEQ])

        row_ps = [ctx.enter_context(nc.psum_tensor(f"{name}_row{i}", [P, SEQ], F32)) for i in range(ROW_BANKS)]
        key_ps = [ctx.enter_context(nc.psum_tensor(f"{name}_key{i}", [P, SEQ], F32)) for i in range(2)]
        ctx_ps = ctx.enter_context(nc.psum_tensor(f"{name}_ctx", [P, SEQ], F32))
        misc_ps = [ctx.enter_context(nc.psum_tensor(f"{name}_misc{i}", [P, SEQ], F32)) for i in range(2)]

        weights_in = sem("weights_in")
        x_in = [sem(f"x_in{i}") for i in range(2)]
        setup_done = sem("setup_done")
        ln_steps, rstd_done, resid_done = sem("ln_steps"), sem("rstd_done"), sem("resid_done")
        proj_done, split_done, low_done = sem("proj_done"), sem("split_done"), sem("low_done")
        parts_out = [sem(f"parts_out{i}") for i in range(2)]
        rows_in = [sem(f"rows_in{g}") for g in range(NG)]
        row_scores, row_max = sem("row_scores"), sem("row_max")
        max_steps, max_out = sem("max_steps"), [sem(f"max_out{i}") for i in range(2)]
        max_in = [sem(f"max_in{g}") for g in range(NG)]
        key_scores, exp_done, mask_done = sem("key_scores"), sem("exp_done"), sem("mask_done")
        pv_done, ctx_out, sums_done = sem("pv_done"), sem("ctx_out"), sem("sums_done")
        LN_ALL = 4 if first else 8
        W_ALL = 16 * (11 if first else 7)
        passed = {e: sem(f"passed_{e}") for e in ("sp", "dve", "pool")}
        misc_full, misc_free = [sem(f"misc_full{i}") for i in range(2)], [sem(f"misc_free{i}") for i in range(2)]

        def slots(c, kind):
            for g in range(NG):
                row = (c, g) if runs(kind, 0) else None
                back2 = (c, g - 2) if g >= 2 else (c - 1, g + 2)
                key = back2 if runs(kind, 0 if g >= 2 else -1) else None
                back3 = (c, 0) if g == 3 else (c - 1, g + 1)
                pv = back3 if runs(kind, 0 if g == 3 else -1) else None
                yield g, row, key, pv

        def hooks(c, kind, g, step):
            for job, off, bank in ATT_HOOKS.get((g, step), []):
                if runs(kind, off):
                    turn = ATT_TURNS.before(c, kind, job) if bank is not None else None
                    yield job, c + off, bank, turn

        def tiles(c):
            return bass.ds(c * TT, TT)

        with nc.Block() as block:

            @block.sync
            def _(sp):
                sp.dma_start(wo[:], w["wo"].rearrange("(c p) n -> p c n", p=P)).then_inc(weights_in, 16)
                if first:
                    for src, dst in ((w["wq"], wq), (w["wk"], wk), (w["wv"], wv)):
                        for kc in range(KC):
                            sp.dma_start(dst[:, kc, :].rearrange("p (h k) -> p h k", h=H),
                                         src[:, kc * P:(kc + 1) * P, :].rearrange("h p k -> p h k")).then_inc(weights_in, 16)
                    for src, dst in ((w["bq"], bq), (w["bk"], bk)):
                        sp.dma_start(dst[:], src.rearrange("(c g) k -> (g k) c", c=KC),
                                     allow_slow_non_contiguous=True).then_inc(weights_in, 16)
                    sp.dma_start(bv_row[:], w["bv"].rearrange("(o h) k -> o (h k)", o=1).to_broadcast([P, D])).then_inc(weights_in, 16)
                else:
                    for src, dst in ((w["wq"], wq), (w["wk"], wk), (w["wv"], wv)):
                        sp.dma_start(dst[:], src.rearrange("(c p) n -> p c n", p=P)).then_inc(weights_in, 16)
                    for src, dst in ((w["ln_scale"], ln_scale), (w["ln_shift"], ln_shift)):
                        sp.dma_start(dst[:], src.rearrange("(c p) -> p c", p=P),
                                     allow_slow_non_contiguous=True).then_inc(weights_in, 16)
                sp.dma_start(bo_row[:], w["bo"].rearrange("(o n) -> o n", o=1).to_broadcast([P, D])).then_inc(weights_in, 16)

                def load_x(c, parity):
                    sp.dma_start(x_sb[:, tiles(c), :],
                                 x_dram[bass.ds(c, 1), :, :].rearrange("o (t p) d -> p (o t) d", p=P)).then_inc(x_in[parity], 16)

                def store_parts(c, j, parity):
                    sp.wait_ge(low_done, c * 4 + (j + 1))
                    sp.dma_start(part_dram[parity, j].rearrange("s p t -> p s t"), parts[j][:]).then_inc(parts_out[parity], 16)

                def load_rows(c, g, parity):
                    wait_apart(sp, parts_out[parity], (c - parity) * 32 + 64, passed["sp"])
                    wait(sp, key_scores, ((c - 1) * NG + (g + 1)) * NU)
                    for rows, order, j0 in ((q_rows, QROWS, 0), (k_rows, KROWS, 2)):
                        src = part_dram[parity, j0 + g // 2]
                        for r, part in enumerate(order):
                            sp.dma_start(rows[g][r * DK:(r + 1) * DK, :, :],
                                         src[part, (g % 2) * 64:(g % 2) * 64 + 64, :].rearrange("(h d) t -> d h t", h=HG)
                                         ).then_inc(rows_in[g], 16)

                def body(c, kind, parity):
                    if first and kind in (PRO, FIRST):
                        for b in range(4) if kind == PRO else range(4, NSEQ):
                            wait(sp, x_in[b % 2], b // 2 * 16)
                            load_x(b, b % 2)
                    for g, row, key, pv in slots(c, kind):
                        for step in range(NU):
                            for job, b, bank, turn in hooks(c, kind, g, step):
                                if job[:2] == "mt":
                                    mg = int(job[2])
                                    sp.wait_ge(misc_free[1], turn + 1)
                                    sp.dma_start(max_dram[mg].rearrange("s r t -> (s r) t"), max_rows[:]).then_inc(max_out[mg % 2], 16)
                                    sp.wait_ge(max_out[mg % 2], (b * 2 + (mg // 2 + 1)) * 16)
                                    sp.dma_start(q_rows[mg][SROWS:MROWS, :, :].rearrange("s h t -> s (h t)"),
                                                 max_dram[mg].rearrange("s r t -> s (r t)")).then_inc(max_in[mg], 16)
                                if job in PARTS:
                                    store_parts(b, PARTS.index(job), 1 - parity)
                        if g < 2 and runs(kind, 0):
                            load_rows(c, g + 2, parity)
                        if g >= 2 and runs(kind, 1):
                            load_rows(c + 1, g - 2, 1 - parity)

                each_body(sp, body)
                for mg in range(NG):
                    sp.wait_ge(max_in[mg], 16 * NSEQ)

            @block.tensor
            def _(pe):
                pe.wait_ge(setup_done, 1)

                def rows_unit(c, g, u):
                    qt, heads = ROW_UNITS[u]
                    n = (qt + 1) * P
                    out = row_ps[u % ROW_BANKS]
                    if u == 0:
                        pe.wait_ge(rows_in[g], (c + 1) * (16 * 2 * len(QROWS)))
                    wait(pe, row_max, row_before(u, c * NG + g))
                    for k, h in enumerate(heads):
                        pe.matmul(out[:, k * n:(k + 1) * n], q_rows[g][0:SROWS, h, qt * P:(qt + 1) * P],
                                  k_rows[g][0:SROWS, h, 0:n], start=(k == 0), stop=False, skip_group_check=True)
                    diag = out[:, 0:len(heads) * n].rearrange("p (h n) -> p h n", n=n)[:, :, qt * P:n]
                    pe.matmul(diag, ident_bf[:], neg_mask[:, 0:len(heads), :], start=False, stop=True,
                              skip_group_check=True).then_inc(row_scores, 1)

                def key_unit(c, g, u):
                    kt, heads = KEY_UNITS[u]
                    n = SEQ - kt * P
                    out = key_ps[(u + g) % 2]
                    if u == 0:
                        pe.wait_ge(max_in[g], (c + 1) * 16)
                    wait(pe, exp_done, (c * NG + g) * NU + (u - 1))
                    for k, h in enumerate(heads):
                        mm = pe.matmul(out[:, k * n:(k + 1) * n], k_rows[g][0:MROWS, h, kt * P:(kt + 1) * P],
                                       q_rows[g][0:MROWS, h, kt * P:SEQ], start=True, stop=True, skip_group_check=True)
                    mm.then_inc(key_scores, 1)

                def pv(c, g, kt, parity):
                    if kt == 0:
                        wait(pe, ctx_out, c * NG + g)
                    pe.wait_ge(mask_done, (c * NG + g) * TT + (kt + 1))
                    p = probs[g % 2][:, PT_OFF[kt]:PT_OFF[kt + 1]].rearrange("p (h n) -> p h n", h=HG)
                    for h in range(HG):
                        mm = pe.matmul(ctx_ps[VCOLS * h:VCOLS * (h + 1), kt * P:SEQ], values[parity][:, kt, g * HG + h, :],
                                       p[:, h, :], start=(kt == 0), stop=(kt == TT - 1), skip_group_check=True)
                    if kt == TT - 1:
                        mm.then_inc(pv_done, 1)

                def transposes(out, pieces, sem_):
                    for k, piece in enumerate(pieces):
                        mm = pe.transpose(out[:, k * P:(k + 1) * P], piece, ident[:])
                    mm.then_inc(sem_, 1)

                def product(out, lhs, rhs, sem_=None):
                    for kc in range(KC):
                        mm = pe.matmul(out, lhs(kc), rhs(kc), start=(kc == 0), stop=(kc == KC - 1), skip_group_check=True)
                    if sem_ is not None:
                        mm.then_inc(sem_, 1)

                def body(c, kind, parity):
                    for g, row, key, pvg in slots(c, kind):
                        for step in range(NU):
                            if row:
                                rows_unit(*row, step)
                            if key:
                                key_unit(*key, step)
                            if pvg and step in PV_AT:
                                pv(*pvg, PV_AT[step], parity if g == 3 else 1 - parity)
                            for job, b, bank, turn in hooks(c, kind, g, step):
                                if bank is None:
                                    continue
                                out, full = misc_ps[bank], misc_full[bank]
                                wait(pe, misc_free[bank], turn)
                                k = int(job[2]) if len(job) == 3 else int(job[1])
                                if job[:2] == "ut":
                                    pe.wait_ge(ctx_out, b * NG + (k + 1))
                                    transposes(out, [ctx_raw[:, t * P:(t + 1) * P] for t in range(TT)], full)
                                elif job[:2] == "mt":
                                    pe.wait_ge(max_steps, (b * NG + (k + 1)) * 4)
                                    pe.transpose(out[:, 0:P], max_parts[:], ident[:]).then_inc(full, 1)
                                elif job[:2] == "ht":
                                    if k == 0:
                                        pe.wait_ge(ln_steps, (b + 1) * LN_ALL)
                                    transposes(out, [hn[:, t, k * P:(k + 1) * P] for t in range(TT)], full)
                                elif job[0] in "qk":
                                    if kind == PRO and job == "q0":
                                        pe.wait_ge(weights_in, W_ALL)
                                    if job == "q0":
                                        pe.wait_ge(misc_free[1], ATT_TURNS.before(c, kind, "ht1") + 1)
                                    wt = wq if job[0] == "q" else wk
                                    product(out[:], lambda kc: wt[:, kc, k * P:(k + 1) * P], lambda kc: ht[:, kc, :], full)
                                elif job[0] == "v":
                                    for t in range(2):
                                        product(out[:, t * D:(t + 1) * D], lambda kc: ht[:, kc, (2 * k + t) * P:(2 * k + t + 1) * P],
                                                lambda kc: wv[:, kc, :], full if t == 1 else None)
                                elif job[:2] == "ct":
                                    transposes(out, [ctx_tok[:, t, k * P:(k + 1) * P] for t in range(TT)], full)
                                elif job[:2] == "wo":
                                    if k == 0:
                                        pe.wait_ge(misc_free[1], ATT_TURNS.before(c, kind, "ct1") + 1)
                                    for t in range(2):
                                        product(out[:, t * D:(t + 1) * D], lambda kc: ctx_t[:, kc, (2 * k + t) * P:(2 * k + t + 1) * P],
                                                lambda kc: wo[:, kc, :], full if t == 1 else None)

                each_body(pe, body)

            @block.scalar
            def _(act):
                act.wait_ge(setup_done, 1)
                act.wait_ge(weights_in, W_ALL)

                def exp_unit(c, g, u):
                    kt, heads = KEY_UNITS[u]
                    n = SEQ - kt * P
                    if u == 0:
                        wait(act, pv_done, c * NG + (g - 1))
                    act.wait_ge(key_scores, (c * NG + g) * NU + (u + 1))
                    at = PT_OFF[kt] + heads[0] * n
                    act.activation(probs[g % 2][:, at:at + len(heads) * n], key_ps[(u + g) % 2][:, 0:len(heads) * n],
                                   ACT.Exp, scale=DK ** -0.5).then_inc(exp_done, 1)

                def body(c, kind, parity):
                    for g, row, key, pvg in slots(c, kind):
                        for step in range(NU):
                            if key:
                                exp_unit(*key, step)
                            for job, b, bank, turn in hooks(c, kind, g, step):
                                if bank is None or job[:2] in ("ut", "wo") or job[0] == "v":
                                    continue
                                k = int(job[2]) if len(job) == 3 else int(job[1])
                                act.wait_ge(misc_full[bank], turn + 1)
                                src, free = misc_ps[bank], misc_free[bank]
                                if job[:2] == "mt":
                                    act.activation(max_rows[:], src[0:3 * HG * TT, 0:P], ACT.Copy).then_inc(free, 1)
                                elif job[:2] == "ht":
                                    if first:
                                        act.activation(ht[:, k, :], src[:], ACT.Copy).then_inc(free, 1)
                                    else:
                                        act.activation(ht[:, k, :], src[:], ACT.Identity, scale=ln_scale[:, k:k + 1],
                                                       bias=ln_shift[:, k:k + 1]).then_inc(free, 1)
                                elif job[:2] == "ct":
                                    act.activation(ctx_t[:, k, :], src[:], ACT.Copy).then_inc(free, 1)
                                else:
                                    j = PARTS.index(job)
                                    wait(act, low_done, b * 4 + (j - 1))
                                    if first:
                                        bias = (bq if job[0] == "q" else bk)[:, k:k + 1]
                                        act.activation(proj32[j % 2][:], src[:], ACT.Identity, bias=bias).then_inc(proj_done, 1)
                                        act.activation(parts[j][:, 0, :], src[:], ACT.Identity, bias=bias).then_inc(free, 1)
                                    else:
                                        act.activation(proj32[j % 2][:], src[:], ACT.Copy).then_inc(proj_done, 1)
                                        act.activation(parts[j][:, 0, :], src[:], ACT.Copy).then_inc(free, 1)
                        if pvg:
                            pc, pg = pvg
                            act.wait_ge(pv_done, pc * NG + (pg + 1))
                            act.activation(ctx_raw[:], ctx_ps[:], ACT.Copy).then_inc(ctx_out, 1)

                each_body(act, body)

            @block.vector
            def _(dve):
                for g in range(NG):
                    dve.memset(k_rows[g][SROWS:MROWS, :, :], 1.0)
                for i in range(2):
                    dve.memset(values[i][:, :, :, DK:DK + 1], 1.0)
                    dve.memset(values[i][:, :, :, DK + 1:VCOLS], 0.0)
                dve.memset(max_parts[:], 0.0).then_inc(setup_done, 1)
                dve.wait_ge(setup_done, 1)
                dve.wait_ge(weights_in, W_ALL)

                def ln_stats(b, n, src):
                    base = b * LN_ALL + n * 4
                    for t in range(TT):
                        ins = dve.bn_stats(stats[:, t, :], src(t))
                    ins.then_inc(ln_steps, 1)
                    wait_apart(dve, ln_steps, base + 1, passed["dve"])
                    for t in range(TT):
                        ins = dve.bn_aggr(mv[:, t, :], stats[:, t, :])
                    ins.then_inc(ln_steps, 1)
                    dve.wait_ge(ln_steps, base + 2)
                    dve.tensor_scalar(var_eps[:], mv[:, :, 1], EPS, None, ALU.add).then_inc(ln_steps, 1)

                def ln_apply(b, n, src, dst):
                    dve.wait_ge(rstd_done, b * (LN_ALL // 4) + (n + 1))
                    for t in range(TT):
                        ins = dve.tensor_scalar(dst(t), src(t), mv[:, t, 0:1], rstd[:, t:t + 1], ALU.subtract, ALU.mult)
                    ins.then_inc(ln_steps, 1)

                def body(c, kind, parity):
                    for g, row, key, pvg in slots(c, kind):
                        for step in range(NU):
                            if row:
                                qt, heads = ROW_UNITS[step]
                                n = (qt + 1) * P
                                dve.wait_ge(row_scores, (c * NG + g) * NU + (step + 1))
                                dve.tensor_reduce(maxes[:, heads[0]:heads[-1] + 1, qt],
                                                  row_ps[step % ROW_BANKS][:, 0:len(heads) * n].rearrange("p (h n) -> p h n", n=n),
                                                  AX_X, ALU.max).then_inc(row_max, 1)
                            for job, b, bank, turn in hooks(c, kind, g, step):
                                xt = (lambda t: x_sb[:, b * TT + t, :])
                                if job == "stats1":
                                    if first:
                                        wait_apart(dve, x_in[1 - parity], (b - (1 - parity)) * 8 + 16, passed["dve"])
                                    ln_stats(b, 0, xt)
                                elif job == "norm1":
                                    if first:
                                        ln_apply(b, 0, xt, lambda t: hn[:, t, :])
                                    else:
                                        ln_apply(b, 0, xt, lambda t: y_sb[:, b * TT + t, :])
                                elif job == "stats2" and not first:
                                    wait_apart(dve, ln_steps, b * LN_ALL + 4, passed["dve"])
                                    ln_stats(b, 1, lambda t: y_sb[:, b * TT + t, :])
                                elif job == "norm2" and not first:
                                    ln_apply(b, 1, lambda t: y_sb[:, b * TT + t, :], lambda t: hn[:, t, :])
                                elif job in PARTS:
                                    j = PARTS.index(job)
                                    dve.wait_ge(misc_free[bank], turn + 1)
                                    dve.tensor_tensor(rest32[j % 2][:], proj32[j % 2][:], parts[j][:, 0, :],
                                                      ALU.subtract).then_inc(split_done, 1)
                                    dve.wait_ge(split_done, (b * 4 + j) * 2 + 1)
                                    dve.tensor_copy(parts[j][:, 1, :], rest32[j % 2][:]).then_inc(split_done, 1)
                                elif job[:2] == "ut":
                                    k = int(job[2])
                                    dve.wait_ge(misc_full[bank], turn + 1)
                                    src = misc_ps[bank][:].rearrange("p (t h n) -> p t h n", t=TT, h=HG)
                                    dve.reciprocal(sums[:], src[:, :, :, DK]).then_inc(sums_done, 1)
                                    dve.wait_ge(sums_done, b * NG + (k + 1))
                                    dve.tensor_tensor(
                                        ctx_tok[:, :, k * HG * DK:(k + 1) * HG * DK].rearrange("p t (h n) -> p t h n", h=HG),
                                        src[:, :, :, 0:DK], sums[:].unsqueeze(3).to_broadcast([P, TT, HG, DK]),
                                        ALU.mult).then_inc(misc_free[bank], 1)
                                elif job in ("v0", "v1"):
                                    k = int(job[1])
                                    dve.wait_ge(misc_full[bank], turn + 1)
                                    out = values[1 - parity][:, 2 * k:2 * k + 2, :, 0:DK]
                                    src = misc_ps[bank][:].rearrange("p (t h n) -> p t h n", t=2, h=H)
                                    if first:
                                        for t in range(2):
                                            ins = dve.tensor_tensor(out[:, t], src[:, t], bv_row[:].rearrange("p (h n) -> p h n", h=H), ALU.add)
                                    else:
                                        ins = dve.tensor_copy(out, src)
                                    ins.then_inc(misc_free[bank], 1)
                                elif job in ("wo0", "wo1"):
                                    k = int(job[2])
                                    dve.wait_ge(misc_full[bank], turn + 1)
                                    dve.wait_ge(resid_done, b + 1)
                                    xs = x_sb[:, bass.ds(b * TT + 2 * k, 2), :]
                                    src = misc_ps[bank][:].rearrange("p (t n) -> p t n", t=2)
                                    if first:
                                        dve.tensor_tensor(xs, src, xs, ALU.add).then_inc(misc_free[bank], 1)
                                    else:
                                        ys = y_sb[:, bass.ds(b * TT + 2 * k, 2), :]
                                        dve.tensor_tensor(ys, src, ys, ALU.add).then_inc(misc_free[bank], 1)
                                        dve.wait_ge(misc_free[bank], turn + 1)
                                        dve.tensor_tensor(xs, ys, xs, ALU.add)
                        if row:
                            g4 = (c * NG + g)
                            mflat = maxes[:].rearrange("p h t -> p (h t)")
                            m = HG * TT
                            dve.wait_ge(row_max, (g4 + 1) * NU)
                            dve.tensor_scalar(max_bf[:], mflat, -1.0, None, ALU.mult).then_inc(max_steps, 1)
                            dve.wait_ge(max_steps, g4 * 4 + 1)
                            dve.tensor_copy(max_parts[:, 0:m], max_bf[:])
                            dve.scalar_tensor_tensor(out=max_rest[:], in0=mflat, scalar=-1.0, in1=max_bf[:],
                                                     op0=ALU.mult, op1=ALU.subtract).then_inc(max_steps, 1)
                            dve.wait_ge(max_steps, g4 * 4 + 2)
                            dve.tensor_copy(max_bf[:], max_rest[:]).then_inc(max_steps, 1)
                            dve.wait_ge(max_steps, g4 * 4 + 3)
                            dve.tensor_copy(max_parts[:, m:2 * m], max_bf[:])
                            dve.tensor_tensor(max_parts[:, 2 * m:3 * m], max_rest[:], max_bf[:], ALU.subtract).then_inc(max_steps, 1)

                each_body(dve, body)

            @block.gpsimd
            def _(pool):
                pool.wait_ge(weights_in, W_ALL)

                def body(c, kind, parity):
                    for g, row, key, pvg in slots(c, kind):
                        for step in range(NU):
                            if key:
                                kc_, kg = key
                                for kt in range(TT):
                                    if step == KEY_DONE[kt] - 1:
                                        wait_apart(pool, exp_done, (kc_ * NG + kg) * NU + KEY_DONE[kt], passed["pool"])
                                        p = probs[kg % 2][:, PT_OFF[kt]:PT_OFF[kt + 1]].rearrange("p (h n) -> p h n", h=HG)[:, :, 0:P]
                                        pool.affine_select(out=p, in_=p, compare_op=ALU.is_ge, fill=0.0, base=0,
                                                           pattern=[[0, HG], [1, P]], channel_multiplier=-1).then_inc(mask_done, 1)
                            for job, b, bank, turn in hooks(c, kind, g, step):
                                n_ln = LN_ALL // 4
                                if job == "norm1":
                                    pool.wait_ge(ln_steps, b * LN_ALL + 3)
                                    pool.tensor_tensor(rstd[:], var_eps[:], minus_half[:].to_broadcast([P, TT]), ALU.pow).then_inc(rstd_done, 1)
                                elif job == "norm2" and not first:
                                    pool.wait_ge(ln_steps, b * LN_ALL + 7)
                                    pool.tensor_tensor(rstd[:], var_eps[:], minus_half[:].to_broadcast([P, TT]), ALU.pow).then_inc(rstd_done, 1)
                                elif job in PARTS:
                                    j = PARTS.index(job)
                                    pool.wait_ge(split_done, (b * 4 + j) * 2 + 2)
                                    pool.tensor_tensor(parts[j][:, 2, :], rest32[j % 2][:], parts[j][:, 1, :], ALU.subtract).then_inc(low_done, 1)
                                    if job == "k1":
                                        pool.wait_ge(ln_steps, (b + 1) * LN_ALL)
                                        r = (x_sb if first else y_sb)[:, tiles(b), :]
                                        pool.tensor_tensor(r, r, bo_row[:].unsqueeze(1).to_broadcast([P, TT, D]), ALU.add).then_inc(resid_done, 1)

                each_body(pool, body)


def make_constants(nc, ctx):
    ident = ctx.enter_context(nc.sbuf_tensor("ident", [P, P], F32))
    ident_bf = ctx.enter_context(nc.sbuf_tensor("ident_bf", [P, P], BF16))
    neg_mask = ctx.enter_context(nc.sbuf_tensor("neg_mask", [P, HG, P], BF16))
    minus_half = ctx.enter_context(nc.sbuf_tensor("minus_half", [P, 1], F32))
    filled = ctx.enter_context(nc.semaphore("filled"))
    with nc.Block() as block:

        @block.gpsimd
        def _(pool):
            pool.memset(minus_half[:], -0.5)
            pool.memset(ident[:], 0.0)
            pool.memset(ident_bf[:], 0.0)
            pool.memset(neg_mask[:], 0.0).then_inc(filled, 1)
            pool.wait_ge(filled, 1)
            for t in (ident, ident_bf):
                pool.affine_select(out=t[:], in_=t[:], compare_op=ALU.not_equal, fill=1.0, base=0,
                                   pattern=[[-1, P]], channel_multiplier=1)
            pool.affine_select(out=neg_mask[:], in_=neg_mask[:], compare_op=ALU.is_ge, fill=MASKED, base=0,
                               pattern=[[0, HG], [-1, P]], channel_multiplier=1).then_inc(filled, 1)

    return dict(ident=ident, ident_bf=ident_bf, neg_mask=neg_mask, minus_half=minus_half)


CROSS_HOOKS = {
    (0, 0): [("stats", 1, None)],
    (0, 1): [("ct0", 1, 0), ("ct1", 1, 1)],
    (0, 2): [("norm", 1, None)],
    (1, 0): [("k0", 1, 0), ("k1", 1, 1)],
    (1, 2): [("ht0", 1, 0), ("ht1", 1, 1)],
    (2, 0): [("q0", 1, 0), ("q1", 1, 1)],
    (3, 0): [("v0", 1, 0), ("v1", 1, 1)],
}
CROSS_TURNS = Turns(CROSS_HOOKS)
CROSS_STEPS = 3


def cross_phase(nc, consts, x_sb, w, ctx_dram):
    ident, minus_half = consts["ident"], consts["minus_half"]
    with ExitStack() as ctx:
        def sb(n, shape, dt=F32):
            return ctx.enter_context(nc.sbuf_tensor(f"cross_{n}", shape, dt))

        def psum(n):
            return [ctx.enter_context(nc.psum_tensor(f"cross_{n}{i}", [P, SEQ], F32)) for i in range(2)]

        def sem(n):
            return ctx.enter_context(nc.semaphore(f"cross_{n}"))

        w_rows = [sb(f"{n}_rows", [P, KC, D]) for n in ("wq", "wk", "wv")]
        w_turned = [sb(f"{n}_turned", [P, KC, D]) for n in ("wq", "wk", "wv")]
        bq, bk, bv_row = sb("bq", [P, KC]), sb("bk", [P, KC]), sb("bv_row", [P, D])
        stats, mv = sb("stats", [P, TT, 6]), sb("mv", [P, TT, 2])
        var_eps, rstd = sb("var_eps", [P, TT]), sb("rstd", [P, TT])
        hn, ht = sb("hn", [P, TT, D]), sb("ht", [P, KC, SEQ])
        ctx_in_sb = [sb(f"ctx_in{i}", [P, TT, D]) for i in range(2)]
        ctx_t = sb("ctx_t", [P, KC, SEQ])
        q_t = [sb(f"q_t{i}", [P, KC, SEQ]) for i in range(2)]
        k_t = [sb(f"k_t{i}", [P, KC, SEQ]) for i in range(2)]
        values = [sb(f"values{i}", [P, TT, D]) for i in range(2)]
        row_max, minus_max = sb("row_max", [P, 2]), sb("minus_max", [P, 2])
        sums, inv_sums = sb("sums", [P, TT]), sb("inv_sums", [P, TT])
        probs = [sb(f"probs{i}", [P, SEQ]) for i in range(2)]
        probs_t = [sb(f"probs_t{i}", [P, TT, P]) for i in range(2)]
        score_ps, turn_ps, out_ps, misc_ps = psum("score"), psum("turn"), psum("out"), psum("misc")

        weights_in, w_full, w_ready = sem("weights_in"), sem("w_full"), sem("w_ready")
        ctx_loaded = [sem(f"ctx_loaded{i}") for i in range(2)]
        ln_steps, rstd_done = sem("ln_steps"), sem("rstd_done")
        scores_done, max_done, minus_done, exp_done = sem("scores_done"), sem("max_done"), sem("minus_done"), sem("exp_done")
        turn_full, turn_free, out_full, inv_done, out_free = (sem(n) for n in ("turn_full", "turn_free", "out_full", "inv_done", "out_free"))
        misc_full, misc_free = [sem(f"misc_full{i}") for i in range(2)], [sem(f"misc_free{i}") for i in range(2)]
        passed = sem("passed")
        W_ALL = 6 * 16

        def slots(c, kind):
            for qt in range(TT):
                score = (c, qt) if runs(kind, 0) else None
                turn = ((c, qt - 1) if qt >= 1 else (c - 1, TT - 1)) if runs(kind, 0 if qt >= 1 else -1) else None
                out = ((c, qt - 2) if qt >= 2 else (c - 1, qt + 2)) if runs(kind, 0 if qt >= 2 else -1) else None
                yield qt, score, turn, out

        def hooks(c, kind, g, step):
            for job, off, bank in CROSS_HOOKS.get((g, step), []):
                if runs(kind, off):
                    turn = CROSS_TURNS.before(c, kind, job) if bank is not None else None
                    yield job, c + off, bank, turn

        with nc.Block() as block:

            @block.sync
            def _(sp):
                for src, dst in zip((w["wq"], w["wk"], w["wv"]), w_rows):
                    sp.dma_start(dst[:], src.rearrange("(c p) n -> p c n", p=P)).then_inc(weights_in, 16)
                for src, dst in ((w["bq"], bq), (w["bk"], bk)):
                    sp.dma_start(dst[:], src.rearrange("(c p) -> p c", p=P),
                                 allow_slow_non_contiguous=True).then_inc(weights_in, 16)
                sp.dma_start(bv_row[:], w["bv"].rearrange("(o n) -> o n", o=1).to_broadcast([P, D])).then_inc(weights_in, 16)

                sp.dma_start(ctx_in_sb[0][:], ctx_dram[0].rearrange("(t p) d -> p t d", p=P)).then_inc(ctx_loaded[0], 16)
                sp.dma_start(ctx_in_sb[1][:], ctx_dram[1].rearrange("(t p) d -> p t d", p=P)).then_inc(ctx_loaded[1], 16)
                mid_turns = CROSS_TURNS.count(MID, 1)
                at = CROSS_TURNS.before(-1, PRO, "ct1") + 1
                sp.wait_ge(misc_free[1], at)
                sp.dma_start(ctx_in_sb[0][:], ctx_dram[2].rearrange("(t p) d -> p t d", p=P)).then_inc(ctx_loaded[0], 16)
                at = CROSS_TURNS.before(0, FIRST, "ct1") + 1
                sp.wait_ge(misc_free[1], at)
                sp.dma_start(ctx_in_sb[1][:], ctx_dram[3].rearrange("(t p) d -> p t d", p=P)).then_inc(ctx_loaded[1], 16)
                with sp.Fori(0, (NSEQ - 4) // 2) as i:
                    for k in range(2):
                        sp.wait_ge(misc_free[1], i * (2 * mid_turns) + (at + (k + 1) * mid_turns))
                        sp.dma_start(ctx_in_sb[k][:], ctx_dram[bass.ds(i * 2 + (4 + k), 1), :, :].rearrange("o (t p) d -> p (o t) d", p=P)
                                     ).then_inc(ctx_loaded[k], 16)

            @block.tensor
            def _(pe):
                pe.wait_ge(weights_in, W_ALL)
                for rows, out in zip(w_rows, (misc_ps[0], misc_ps[1], score_ps[0])):
                    for kc in range(KC):
                        for ec in range(KC):
                            mm = pe.transpose(out[:, (kc * KC + ec) * P:(kc * KC + ec + 1) * P],
                                              rows[:, ec, kc * P:(kc + 1) * P], ident[:])
                    mm.then_inc(w_full, 1)
                pe.wait_ge(w_ready, 3)

                def product(out, n, lhs, rhs, sem_=None):
                    for kc in range(n):
                        mm = pe.matmul(out, lhs(kc), rhs(kc), start=(kc == 0), stop=(kc == n - 1), skip_group_check=True)
                    if sem_ is not None:
                        mm.then_inc(sem_, 1)

                def body(c, kind, parity):
                    for qt, score, turn_, out_ in slots(c, kind):
                        if score:
                            n = c * TT + qt
                            wait(pe, exp_done, n - 1)
                            product(score_ps[qt % 2][:], KC, lambda kc: q_t[parity][:, kc, qt * P:(qt + 1) * P],
                                    lambda kc: k_t[parity][:, kc, :], scores_done)
                        if turn_:
                            tc, tq = turn_
                            n = tc * TT + tq
                            pe.wait_ge(exp_done, n + 1)
                            wait(pe, turn_free, n - 1)
                            for kt in range(TT):
                                mm = pe.transpose(turn_ps[tq % 2][:, kt * P:(kt + 1) * P], probs[tq % 2][:, kt * P:(kt + 1) * P], ident[:])
                            mm.then_inc(turn_full, 1)
                        if out_:
                            oc, oq = out_
                            n = oc * TT + oq
                            op = parity if qt >= 2 else 1 - parity
                            pe.wait_ge(turn_free, n + 1)
                            wait(pe, out_free, n - 1)
                            product(out_ps[oq % 2][:, 0:D], TT, lambda kt: probs_t[oq % 2][:, kt, :], lambda kt: values[op][:, kt, :], out_full)
                        for step in range(CROSS_STEPS):
                            for job, b, bank, turn in hooks(c, kind, qt, step):
                                if bank is None:
                                    continue
                                out, full = misc_ps[bank], misc_full[bank]
                                wait(pe, misc_free[bank], turn)
                                k = int(job[-1])
                                if job[:2] == "ct":
                                    if k == 0:
                                        pe.wait_ge(ctx_loaded[1 - parity], (b - (1 - parity)) * 8 + 16)
                                    for t in range(TT):
                                        mm = pe.transpose(out[:, t * P:(t + 1) * P], ctx_in_sb[1 - parity][:, t, k * P:(k + 1) * P], ident[:])
                                    mm.then_inc(full, 1)
                                elif job[:2] == "ht":
                                    pe.wait_ge(ln_steps, (b + 1) * 4)
                                    for t in range(TT):
                                        mm = pe.transpose(out[:, t * P:(t + 1) * P], hn[:, t, k * P:(k + 1) * P], ident[:])
                                    mm.then_inc(full, 1)
                                elif job[0] in "qk":
                                    if k == 0:
                                        pe.wait_ge(misc_free[1], CROSS_TURNS.before(c, kind, job[0] + "1"))
                                    src, wt = (ht, w_turned[0]) if job[0] == "q" else (ctx_t, w_turned[1])
                                    product(out[:], KC, lambda kc: wt[:, kc, k * P:(k + 1) * P], lambda kc: src[:, kc, :], full)
                                else:
                                    for t in range(2):
                                        product(out[:, t * D:(t + 1) * D], KC, lambda kc: ctx_t[:, kc, (2 * k + t) * P:(2 * k + t + 1) * P],
                                                lambda kc: w_turned[2][:, kc, :], full if t == 1 else None)

                each_body(pe, body)

            @block.scalar
            def _(act):
                for n, src in enumerate((misc_ps[0], misc_ps[1], score_ps[0])):
                    act.wait_ge(w_full, n + 1)
                    act.activation(w_turned[n][:].rearrange("p c n -> p (c n)"), src[:], ACT.Copy).then_inc(w_ready, 1)
                act.wait_ge(weights_in, W_ALL)

                def body(c, kind, parity):
                    for qt, score, turn_, out_ in slots(c, kind):
                        if score:
                            n = c * TT + qt
                            act.wait_ge(minus_done, n + 1)
                            act.activation(probs[qt % 2][:], score_ps[qt % 2][:], ACT.Exp, bias=minus_max[:, qt % 2:qt % 2 + 1],
                                           accum_out=sums[:, qt:qt + 1]).then_inc(exp_done, 1)
                        if turn_:
                            tc, tq = turn_
                            act.wait_ge(turn_full, tc * TT + tq + 1)
                            act.activation(probs_t[tq % 2][:].rearrange("p t n -> p (t n)"), turn_ps[tq % 2][:], ACT.Copy).then_inc(turn_free, 1)
                        for step in range(CROSS_STEPS):
                            for job, b, bank, turn in hooks(c, kind, qt, step):
                                if bank is None or job[0] == "v":
                                    continue
                                k = int(job[-1])
                                act.wait_ge(misc_full[bank], turn + 1)
                                src, free = misc_ps[bank], misc_free[bank]
                                if job[:2] in ("ct", "ht"):
                                    act.activation((ctx_t if job[0] == "c" else ht)[:, k, :], src[:], ACT.Copy).then_inc(free, 1)
                                else:
                                    dst, bias = (q_t, bq) if job[0] == "q" else (k_t, bk)
                                    act.activation(dst[1 - parity][:, k, :], src[:], ACT.Identity, bias=bias[:, k:k + 1]).then_inc(free, 1)

                each_body(act, body)

            @block.vector
            def _(dve):
                dve.wait_ge(weights_in, W_ALL)

                def body(c, kind, parity):
                    for qt, score, turn_, out_ in slots(c, kind):
                        if score:
                            n = c * TT + qt
                            dve.wait_ge(scores_done, n + 1)
                            dve.tensor_reduce(row_max[:, qt % 2:qt % 2 + 1], score_ps[qt % 2][:], AX_X, ALU.max).then_inc(max_done, 1)
                            dve.wait_ge(max_done, n + 1)
                            dve.tensor_scalar(minus_max[:, qt % 2:qt % 2 + 1], row_max[:, qt % 2:qt % 2 + 1], -1.0, None, ALU.mult).then_inc(minus_done, 1)
                        if out_:
                            oc, oq = out_
                            n = oc * TT + oq
                            dve.wait_ge(exp_done, n + 1)
                            dve.reciprocal(inv_sums[:, oq:oq + 1], sums[:, oq:oq + 1]).then_inc(inv_done, 1)
                            dve.wait_ge(inv_done, n + 1)
                            dve.wait_ge(out_full, n + 1)
                            xs = x_sb[:, oc * TT + oq, :]
                            dve.scalar_tensor_tensor(out=xs, in0=out_ps[oq % 2][:, 0:D], scalar=inv_sums[:, oq:oq + 1], in1=xs,
                                                     op0=ALU.mult, op1=ALU.add).then_inc(out_free, 1)
                        for step in range(CROSS_STEPS):
                            for job, b, bank, turn in hooks(c, kind, qt, step):
                                xt = (lambda t: x_sb[:, b * TT + t, :])
                                if job == "stats":
                                    for t in range(TT):
                                        ins = dve.bn_stats(stats[:, t, :], xt(t))
                                    ins.then_inc(ln_steps, 1)
                                    wait_apart(dve, ln_steps, b * 4 + 1, passed)
                                    for t in range(TT):
                                        ins = dve.bn_aggr(mv[:, t, :], stats[:, t, :])
                                    ins.then_inc(ln_steps, 1)
                                    dve.wait_ge(ln_steps, b * 4 + 2)
                                    dve.tensor_scalar(var_eps[:], mv[:, :, 1], EPS, None, ALU.add).then_inc(ln_steps, 1)
                                elif job == "norm":
                                    dve.wait_ge(rstd_done, b + 1)
                                    for t in range(TT):
                                        ins = dve.tensor_scalar(hn[:, t, :], xt(t), mv[:, t, 0:1], rstd[:, t:t + 1], ALU.subtract, ALU.mult)
                                    ins.then_inc(ln_steps, 1)
                                elif job[0] == "v":
                                    k = int(job[-1])
                                    dve.wait_ge(misc_full[bank], turn + 1)
                                    dve.tensor_tensor(values[1 - parity][:, 2 * k:2 * k + 2, :], misc_ps[bank][:].rearrange("p (t n) -> p t n", t=2),
                                                      bv_row[:].unsqueeze(1).to_broadcast([P, 2, D]), ALU.add).then_inc(misc_free[bank], 1)

                each_body(dve, body)

            @block.gpsimd
            def _(pool):
                def body(c, kind, parity):
                    if runs(kind, 1):
                        b = c + 1
                        pool.wait_ge(ln_steps, b * 4 + 3)
                        pool.tensor_tensor(rstd[:], var_eps[:], minus_half[:].to_broadcast([P, TT]), ALU.pow).then_inc(rstd_done, 1)

                each_body(pool, body)


def routing_phase(nc, ctx, consts, y_sb, w, sorted_dram, weights):
    ident, minus_half = consts["ident"], consts["minus_half"]

    def keep(n, shape, dt=F32):
        return ctx.enter_context(nc.sbuf_tensor(f"moe_{n}", shape, dt))

    tile_expert, tile_row = keep("tile_expert", [1, MT + 1], I32), keep("tile_row", [1, MT + 1], I32)
    ln_scale, ln_shift = keep("ln_scale", [P, KC]), keep("ln_shift", [P, KC])
    with ExitStack() as inner:
        def sb(n, shape, dt=F32):
            return inner.enter_context(nc.sbuf_tensor(f"route_{n}", shape, dt))

        def sem(n):
            return inner.enter_context(nc.semaphore(f"route_{n}"))

        def psum(n):
            return inner.enter_context(nc.psum_tensor(f"route_{n}", [P, SEQ], F32))

        gate = sb("gate", [P, KC, E_N])
        stats, mv = sb("stats", [P, TT, 6]), sb("mv", [P, TT, 2])
        var_eps, rstd = sb("var_eps", [P, TT]), sb("rstd", [P, TT])
        rows = [[sb(f"rows{i}{k}", [P, TT, ROW]) for k in range(2)] for i in range(2)]
        ht = [sb(f"ht{i}", [P, KC, SEQ]) for i in range(2)]
        logits, top, top_at = sb("logits", [P, TT, E_N]), sb("top", [P, TT, 8]), sb("top_at", [P, TT, 8], U32)
        expert_of, one_hot = sb("expert_of", [P, TT, 2]), sb("one_hot", [P, TT, 2, E_N])
        chosen = sb("chosen", [P, TT, E_N], BF16)
        diff, ratio, denom = sb("diff", [P, TT]), sb("ratio", [P, TT]), sb("denom", [P, TT])
        base, picked = sb("base", [P, TT, E_N]), sb("picked", [P, TT, 2, E_N])
        row_f = sb("row_f", [P, TT, 2])
        row_of = [sb(f"row_of{i}", [P, TT, 2], U32) for i in range(2)]
        next_row = [sb(f"next_row{i}", [P, E_N]) for i in range(2)]
        iota_i, iota_e = sb("iota_i", [P, E_N], I32), sb("iota_e", [P, E_N])
        iota_ti, iota_t = sb("iota_ti", [1, MT + 1], I32), sb("iota_t", [1, MT + 1])
        iota_pi, iota_p = sb("iota_pi", [P, 1], I32), sb("iota_p", [P, 1])
        place = sb("place", [P, NT, 2], I32)
        before_bf, ones_bf, ones = sb("before_bf", [P, P], BF16), sb("ones_bf", [P, P], BF16), sb("ones", [P, E_N])
        pad_row, pad_at, pad_f = sb("pad_row", [P, ROW]), sb("pad_at", [P, E_N], U32), sb("pad_f", [P, E_N])
        padded, padded_i, n_tiles, tiles_upto = sb("padded", [P, E_N]), sb("padded_i", [P, E_N], I32), sb("n_tiles", [P, E_N]), sb("tiles_upto", [P, E_N])
        passed_tile, skipped, tile_f = sb("passed_tile", [1, MT + 1, E_N]), sb("skipped", [1, MT + 1, E_N]), sb("tile_f", [1, MT + 1])
        turn_ps = [[psum(f"turn{i}{k}") for k in range(2)] for i in range(2)]
        gate_ps = [psum(f"gate{i}") for i in range(2)]
        count_ps = psum("count")

        loaded, made, set_up = sem("loaded"), sem("made"), sem("set_up")
        ln_steps, rstd_done, copied = sem("ln_steps"), sem("rstd_done"), sem("copied")
        turned, ht_done, gated = sem("turned"), sem("ht_done"), sem("gated")
        steps, diff_done, chosen_done, counted, ratio_done, rows_done = (
            sem(n) for n in ("steps", "diff_done", "chosen_done", "counted", "ratio_done", "rows_done"))
        rowf_done = sem("rowf_done")
        scattered = [sem(f"scattered{i}") for i in range(2)]
        pads_done, padded_out, passed = sem("pads_done"), sem("padded_out"), sem("passed")
        pads_out, passed_pool = sem("pads_out"), sem("passed_pool")
        MADE_ALL = 5
        STEPS = 9

        with nc.Block() as block:

            @block.sync
            def _(sp):
                sp.dma_start(gate[:], w["gate_w"].rearrange("(c p) n -> p c n", p=P)).then_inc(loaded, 16)
                for src, dst in ((w["ln2_scale"], ln_scale), (w["ln2_shift"], ln_shift)):
                    sp.dma_start(dst[:], src.rearrange("(c p) -> p c", p=P), allow_slow_non_contiguous=True).then_inc(loaded, 16)
                for name, dst, chunks in weights["parts"]:
                    for e in range(E_N):
                        sp.dma_start(dst[:, e], w[name][e].rearrange("(c p) n -> p c n", p=P)).then_inc(weights["in"], 16)
                sp.wait_ge(set_up, 2)
                sp.dma_start(sorted_dram[PAD_TILE:PAD_TILE + P, :], pad_row[:]).then_inc(padded_out, 16)
                sp.wait_ge(padded_out, 16)

            @block.gpsimd
            def _(pool):
                pool.iota(iota_i[:], pattern=[[1, E_N]], base=0, channel_multiplier=0)
                pool.iota(iota_ti[:], pattern=[[1, MT + 1]], base=0, channel_multiplier=0)
                pool.iota(iota_pi[:], pattern=[[0, 1]], base=0, channel_multiplier=1)
                pool.iota(place[:], pattern=[[P, NT], [NT * P, 2]], base=0, channel_multiplier=1).then_inc(made, 1)
                pool.memset(before_bf[:], 1.0).then_inc(made, 1)
                pool.wait_ge(made, 2)
                pool.affine_select(out=before_bf[:], in_=before_bf[:], compare_op=ALU.is_ge, fill=0.0, base=-1,
                                   pattern=[[1, P]], channel_multiplier=-1).then_inc(made, 1)
                pool.memset(ones_bf[:], 1.0)
                pool.memset(ones[:], 1.0)
                pool.memset(pad_row[:], 0.0).then_inc(made, 1)
                pool.wait_ge(made, 4)
                pool.iota(pad_row[:, PLACE:PLACE + 1].bitcast(I32), pattern=[[0, 1]], base=2 * NT * P, channel_multiplier=1).then_inc(made, 1)

                def body(c, kind, parity):
                    if runs(kind, 1):
                        pool.wait_ge(ln_steps, c * 4 + 7)
                        pool.tensor_tensor(rstd[:], var_eps[:], minus_half[:].to_broadcast([P, TT]), ALU.pow).then_inc(rstd_done, 1)
                    if runs(kind, 0):
                        pool.wait_ge(rows_done, c + 1)
                        wait_apart(pool, copied, c + 1, passed_pool)
                        for t in range(TT):
                            for k in range(2):
                                pool.indirect_dma_start(out=sorted_dram, out_offset=bass.IndirectOffsetOnAxis(ap=row_of[parity][:, t, k:k + 1], axis=0),
                                                        in_=rows[parity][k][:, t, :], in_offset=None).then_inc(scattered[parity], 16)

                each_body(pool, body)
                pool.wait_ge(pads_done, 1)
                for e in range(E_N):
                    pool.indirect_dma_start(out=sorted_dram, out_offset=bass.IndirectOffsetOnAxis(ap=pad_at[:, e:e + 1], axis=0),
                                            in_=pad_row[:], in_offset=None).then_inc(pads_out, 16)
                pool.wait_ge(pads_out, E_N * 16)
                for i in range(2):
                    pool.wait_ge(scattered[i], NSEQ // 2 * 2 * TT * 16)

            @block.tensor
            def _(pe):
                pe.wait_ge(loaded, 48)
                pe.wait_ge(made, 4)

                def body(c, kind, parity):
                    if runs(kind, 0):
                        pe.wait_ge(chosen_done, c + 1)
                        for t in range(TT + 1):
                            out = count_ps[:, t * E_N:(t + 1) * E_N]
                            for before in range(t):
                                mm = pe.matmul(out, ones_bf[:], chosen[:, before, :], start=(before == 0), stop=(before == t - 1 == TT - 1),
                                               skip_group_check=True)
                            if t < TT:
                                pe.matmul(out, before_bf[:], chosen[:, t, :], start=(t == 0), stop=True, skip_group_check=True)
                        mm.then_inc(counted, 1)
                    if runs(kind, 1):
                        b, i = c + 1, 1 - parity
                        pe.wait_ge(ln_steps, b * 4 + 4)
                        for kc in range(KC):
                            for t in range(TT):
                                mm = pe.transpose(turn_ps[i][kc][:, t * P:(t + 1) * P], rows[i][0][:, t, kc * P:(kc + 1) * P], ident[:])
                        mm.then_inc(turned, 1)
                        pe.wait_ge(ht_done, b + 1)
                        for t in range(TT):
                            for kc in range(KC):
                                mm = pe.matmul(gate_ps[i][:, t * E_N:(t + 1) * E_N], ht[i][:, kc, t * P:(t + 1) * P], gate[:, kc, :],
                                               start=(kc == 0), stop=(kc == KC - 1), skip_group_check=True)
                        mm.then_inc(gated, 1)

                each_body(pe, body)

            @block.scalar
            def _(act):
                act.wait_ge(loaded, 48)

                def body(c, kind, parity):
                    if runs(kind, 0):
                        act.wait_ge(diff_done, c + 1)
                        act.activation(ratio[:], diff[:], ACT.Exp).then_inc(ratio_done, 1)
                    if runs(kind, 1):
                        b, i = c + 1, 1 - parity
                        act.wait_ge(turned, b + 1)
                        for kc in range(KC):
                            ins = act.activation(ht[i][:, kc, :], turn_ps[i][kc][:], ACT.Identity, scale=ln_scale[:, kc:kc + 1],
                                                 bias=ln_shift[:, kc:kc + 1])
                        ins.then_inc(ht_done, 1)
                        act.activation(rows[i][1][:, :, 0:D], rows[i][0][:, :, 0:D], ACT.Copy).then_inc(copied, 1)

                each_body(act, body)

            @block.vector
            def _(dve):
                dve.wait_ge(made, MADE_ALL)
                dve.tensor_copy(iota_t[:], iota_ti[:])
                dve.tensor_copy(iota_p[:], iota_pi[:])
                dve.tensor_copy(iota_e[:], iota_i[:]).then_inc(set_up, 1)
                dve.wait_ge(set_up, 1)
                dve.tensor_scalar(next_row[0][:], iota_e[:], float(REGION), None, ALU.mult).then_inc(set_up, 1)
                dve.wait_ge(set_up, 2)

                def body(c, kind, parity):
                    if runs(kind, 1):
                        b = c + 1
                        for t in range(TT):
                            ins = dve.bn_stats(stats[:, t, :], y_sb[:, b * TT + t, :])
                        ins.then_inc(ln_steps, 1)
                        wait_apart(dve, ln_steps, b * 4 + 1, passed)
                        for t in range(TT):
                            ins = dve.bn_aggr(mv[:, t, :], stats[:, t, :])
                        ins.then_inc(ln_steps, 1)
                        dve.wait_ge(ln_steps, b * 4 + 2)
                        dve.tensor_scalar(var_eps[:], mv[:, :, 1], EPS, None, ALU.add).then_inc(ln_steps, 1)
                    if runs(kind, 0):
                        step = 0

                        def done(ins, apart=False):
                            nonlocal step
                            step += 1
                            ins.then_inc(steps, 1)
                            if apart:
                                wait_apart(dve, steps, c * STEPS + step, passed)
                            else:
                                dve.wait_ge(steps, c * STEPS + step)

                        dve.wait_ge(gated, c + 1)
                        done(dve.tensor_copy(logits[:].rearrange("p t e -> p (t e)"), gate_ps[parity][:, 0:TT * E_N]), apart=True)
                        for t in range(TT):
                            ins = dve.max(top[:, t, :], logits[:, t, :])
                        done(ins, apart=True)
                        for t in range(TT):
                            ins = dve.max_index(top_at[:, t, :], top[:, t, :], logits[:, t, :])
                        dve.tensor_tensor(diff[:], top[:, :, 1], top[:, :, 0], ALU.subtract).then_inc(diff_done, 1)
                        done(ins)
                        done(dve.tensor_copy(expert_of[:], top_at[:, :, 0:2]))
                        for k in range(2):
                            ins = dve.tensor_tensor(one_hot[:, :, k, :], iota_e[:].unsqueeze(1).to_broadcast([P, TT, E_N]),
                                                    expert_of[:, :, k:k + 1].to_broadcast([P, TT, E_N]), ALU.is_equal)
                        done(ins)
                        dve.tensor_tensor(chosen[:], one_hot[:, :, 0, :], one_hot[:, :, 1, :], ALU.add).then_inc(chosen_done, 1)
                        dve.wait_ge(ratio_done, c + 1)
                        done(dve.tensor_scalar(denom[:], ratio[:], 1.0, None, ALU.add))
                        weight = [rows[parity][k][:, :, WEIGHT] for k in range(2)]
                        done(dve.reciprocal(weight[0], denom[:]))
                        dve.tensor_tensor(weight[1], weight[0], ratio[:], ALU.mult)
                        for k in range(2):
                            dve.tensor_copy(rows[parity][k][:, :, PLACE].bitcast(I32), place[:, bass.ds(c * TT, TT), k])
                        dve.wait_ge(counted, c + 1)
                        dve.tensor_tensor(next_row[1 - parity][:], count_ps[:, TT * E_N:(TT + 1) * E_N], next_row[parity][:], ALU.add)
                        done(dve.tensor_tensor(base[:], count_ps[:, 0:TT * E_N].rearrange("p (t e) -> p t e", t=TT),
                                               next_row[parity][:].unsqueeze(1).to_broadcast([P, TT, E_N]), ALU.add))
                        for k in range(2):
                            ins = dve.tensor_tensor(picked[:, :, k, :], one_hot[:, :, k, :], base[:], ALU.mult)
                        done(ins)
                        dve.tensor_reduce(row_f[:], picked[:], AX_X, ALU.add).then_inc(rowf_done, 1)
                        dve.wait_ge(rowf_done, c + 1)
                        dve.tensor_copy(row_of[parity][:], row_f[:]).then_inc(rows_done, 1)
                        assert step == STEPS
                    if runs(kind, 1):
                        b, i = c + 1, 1 - parity
                        wait(dve, scattered[i], (b - i) * (TT * 16))
                        dve.wait_ge(rstd_done, b + 1)
                        for t in range(TT):
                            ins = dve.tensor_scalar(rows[i][0][:, t, 0:D], y_sb[:, b * TT + t, :], mv[:, t, 0:1], rstd[:, t:t + 1], ALU.subtract, ALU.mult)
                        ins.then_inc(ln_steps, 1)

                each_body(dve, body)
                dve.wait_ge(steps, NSEQ * STEPS)
                step = NSEQ * STEPS

                def done(ins):
                    nonlocal step
                    step += 1
                    ins.then_inc(steps, 1)
                    dve.wait_ge(steps, step)

                done(dve.tensor_tensor(pad_f[:], next_row[0][:], iota_p[:].to_broadcast([P, E_N]), ALU.add))
                dve.tensor_copy(pad_at[:], pad_f[:]).then_inc(pads_done, 1)
                done(dve.scalar_tensor_tensor(out=padded[:], in0=iota_e[:], scalar=-float(REGION), in1=next_row[0][:], op0=ALU.mult, op1=ALU.add))
                done(dve.tensor_scalar(padded[:], padded[:], float(P - 1), None, ALU.add))
                done(dve.tensor_copy(padded_i[:], padded[:]))
                shift = P.bit_length() - 1
                done(dve.tensor_scalar(padded_i[:], padded_i[:], shift, None, ALU.logical_shift_right))
                done(dve.tensor_copy(n_tiles[:], padded_i[:]))
                done(dve.tensor_tensor_scan(tiles_upto[:], ones[:], n_tiles[:], 0.0, ALU.mult, ALU.add))
                done(dve.tensor_tensor(passed_tile[:], iota_t[:].unsqueeze(2).to_broadcast([1, MT + 1, E_N]),
                                       tiles_upto[0:1, :].unsqueeze(1).to_broadcast([1, MT + 1, E_N]), ALU.is_ge))
                done(dve.tensor_scalar(padded[:], n_tiles[:], -float(P), float(REGION), ALU.mult, ALU.add))
                done(dve.tensor_tensor(skipped[:], passed_tile[:], padded[0:1, :].unsqueeze(1).to_broadcast([1, MT + 1, E_N]), ALU.mult))
                done(dve.tensor_reduce(tile_f[:], skipped[:], AX_X, ALU.add))
                done(dve.scalar_tensor_tensor(out=tile_f[:], in0=iota_t[:], scalar=float(P), in1=tile_f[:], op0=ALU.mult, op1=ALU.add))
                done(dve.tensor_scalar(tile_f[:], tile_f[:], float(PAD_TILE), None, ALU.min))
                done(dve.tensor_copy(tile_row[:], tile_f[:]))
                done(dve.tensor_reduce(tile_f[:], passed_tile[:], AX_X, ALU.add))
                done(dve.tensor_scalar(tile_f[:], tile_f[:], float(E_N - 1), None, ALU.min))
                done(dve.tensor_copy(tile_expert[:], tile_f[:]))

    return tile_expert, tile_row, ln_scale, ln_shift


def expert_phase(nc, consts, weights, tile_expert, tile_row, ln_scale, ln_shift, sorted_dram, expert_dram):
    ident = consts["ident"]
    w1, w2, w3 = (dst for _, dst, _ in weights["parts"])
    with ExitStack() as ctx:
        def sb(n, shape, dt=F32):
            return [ctx.enter_context(nc.sbuf_tensor(f"expert_{n}{i}", shape, dt)) for i in range(2)]

        def psum(n, count):
            return [ctx.enter_context(nc.psum_tensor(f"expert_{n}{i}", [P, HID], F32)) for i in range(count)]

        def sem(n):
            return ctx.enter_context(nc.semaphore(f"expert_{n}"))

        meta = sb("meta", [P, ROW - D])
        rows, rows_t = sb("rows", [P, D]), sb("rows_t", [P, KC, P])
        silu, hidden, hidden_t, result = sb("silu", [P, HID]), sb("hidden", [P, HID]), sb("hidden_t", [P, HC, P]), sb("result", [P, D])
        turn_ps, a_ps, b_ps, ht_ps, out_ps = psum("turn", 1), psum("a", 2), psum("b", 2), psum("ht", 1), psum("out", 2)
        passed = sem("passed")
        rows_in, meta_in = [sem(f"rows_in{i}") for i in range(2)], [sem(f"meta_in{i}") for i in range(2)]
        turned, rows_t_done, a_done, b_done, silu_done, hidden_done = (
            sem(n) for n in ("turned", "rows_t_done", "a_done", "b_done", "silu_done", "hidden_done"))
        ht_full, ht_done, out_full, result_done = (sem(n) for n in ("ht_full", "ht_done", "out_full", "result_done"))
        stored = [sem(f"stored{i}") for i in range(2)]

        def each_step(eng, emit):
            for j in range(-2, 2):
                emit(j, j % 2)
            with eng.Fori(0, MT // 2 - 2) as i:
                for k in range(2):
                    emit(i * 2 + (k + 2), k)
            for j in range(MT - 3, MT):
                emit(j, j % 2)

        def parts(j):
            static = isinstance(j, int)
            return (j + 2 if not static or j < MT - 2 else None,
                    j + 1 if not static or -1 <= j < MT - 1 else None,
                    j if not static or j >= 0 else None)

        assert MT % 2 == 1

        with nc.Block() as block:

            @block.sync
            def _(sp):
                def row(j):
                    return sp.value_load(tile_row[0:1, bass.ds(j, 1)], min_val=0, max_val=PAD_TILE)

                def load(j, k):
                    sp.dma_start(rows[k][:], sorted_dram[bass.ds(row(j), P), 0:D]).then_inc(rows_in[k], 16)

                def load_meta(j, k):
                    wait(sp, stored[k], (j - k) * 8)
                    sp.dma_start(meta[k][:], sorted_dram[bass.ds(row(j), P), D:ROW]).then_inc(meta_in[k], 16)

                def tile(j, k):
                    if not isinstance(j, int) or j + 2 <= MT - 1:
                        sp.wait_ge(turned, j + 1)
                        load(j + 2, k)
                    load_meta(j, k)

                load(0, 0)
                load(1, 1)
                tile(0, 0)
                tile(1, 1)
                with sp.Fori(0, MT // 2 - 1 - 1) as i:
                    for k in range(2):
                        tile(i * 2 + (2 + k), k)
                for j in range(MT - 3, MT):
                    tile(j, j % 2)

            @block.gpsimd
            def _(pool):
                def scatter(j, k):
                    pool.wait_ge(result_done, j + 1)
                    wait(pool, stored[1 - k], (j - k) * 8 + (16 if k else 0))
                    wait_apart(pool, meta_in[k], (j - k) * 8 + 16, passed)
                    pool.indirect_dma_start(out=expert_dram, out_offset=bass.IndirectOffsetOnAxis(ap=meta[k][:, 0:1].bitcast(U32), axis=0),
                                            in_=result[k][:], in_offset=None).then_inc(stored[k], 16)

                for j in range(2):
                    scatter(j, j)
                with pool.Fori(0, MT // 2 - 1) as i:
                    for k in range(2):
                        scatter(i * 2 + (2 + k), k)
                scatter(MT - 1, 0)
                pool.wait_ge(stored[0], (MT // 2 + 1) * 16)
                pool.wait_ge(stored[1], MT // 2 * 16)

            @block.tensor
            def _(pe):
                pe.wait_ge(weights["in"], 3 * E_N * 16)

                def expert(j):
                    return pe.value_load(tile_expert[0:1, bass.ds(j, 1)], min_val=0, max_val=E_N - 1)

                def step(j, k):
                    turn, hid, out = parts(j)
                    if out is not None:
                        pe.wait_ge(hidden_done, out + 1)
                        wait(pe, ht_done, out)
                        for hc in range(HC):
                            mm = pe.transpose(ht_ps[0][:, hc * P:(hc + 1) * P], hidden[k][:, hc * P:(hc + 1) * P], ident[:])
                        mm.then_inc(ht_full, 1)
                    if turn is not None:
                        pe.wait_ge(rows_in[k], (turn - k) * 8 + 16)
                        wait(pe, rows_t_done, turn)
                        for kc in range(KC):
                            mm = pe.transpose(turn_ps[0][:, kc * P:(kc + 1) * P], rows[k][:, kc * P:(kc + 1) * P], ident[:])
                        mm.then_inc(turned, 1)
                    if hid is not None:
                        h = 1 - k
                        e = expert(hid)
                        pe.wait_ge(rows_t_done, hid + 1)
                        for ps, wt, full in ((a_ps, w1, a_done), (b_ps, w2, b_done)):
                            for kc in range(KC):
                                mm = pe.matmul(ps[h][:], rows_t[h][:, kc, :], wt[:, e, kc, :], start=(kc == 0), stop=(kc == KC - 1))
                            mm.then_inc(full, 1)
                    if out is not None:
                        e = expert(out)
                        pe.wait_ge(ht_done, out + 1)
                        for hc in range(HC):
                            mm = pe.matmul(out_ps[k][:, 0:D], hidden_t[k][:, hc, :], w3[:, e, hc, :], start=(hc == 0), stop=(hc == HC - 1))
                        mm.then_inc(out_full, 1)

                each_step(pe, step)

            @block.scalar
            def _(act):
                def step(j, k):
                    turn, hid, out = parts(j)
                    if out is not None:
                        act.wait_ge(ht_full, out + 1)
                        act.activation(hidden_t[k][:].rearrange("p c n -> p (c n)"), ht_ps[0][:], ACT.Copy).then_inc(ht_done, 1)
                    if turn is not None:
                        act.wait_ge(turned, turn + 1)
                        for kc in range(KC):
                            ins = act.activation(rows_t[k][:, kc, :], turn_ps[0][:, kc * P:(kc + 1) * P], ACT.Identity,
                                                 scale=ln_scale[:, kc:kc + 1], bias=ln_shift[:, kc:kc + 1])
                        ins.then_inc(rows_t_done, 1)
                    if hid is not None:
                        act.wait_ge(a_done, hid + 1)
                        act.activation(silu[1 - k][:], a_ps[1 - k][:], ACT.Silu).then_inc(silu_done, 1)

                each_step(act, step)

            @block.vector
            def _(dve):
                def step(j, k):
                    turn, hid, out = parts(j)
                    if hid is not None:
                        h = 1 - k
                        dve.wait_ge(silu_done, hid + 1)
                        dve.wait_ge(b_done, hid + 1)
                        dve.tensor_tensor(hidden[h][:], b_ps[h][:], silu[h][:], ALU.mult).then_inc(hidden_done, 1)
                    if out is not None:
                        dve.wait_ge(out_full, out + 1)
                        wait(dve, stored[k], (out - k) * 8)
                        dve.wait_ge(meta_in[k], (out - k) * 8 + 16)
                        dve.tensor_scalar(result[k][:], out_ps[k][:, 0:D], meta[k][:, 1:2], None, ALU.mult).then_inc(result_done, 1)

                each_step(dve, step)


def combine_phase(nc, x_sb, expert_dram, out_dram):
    RING = 3
    with ExitStack() as ctx:
        got = [[ctx.enter_context(nc.sbuf_tensor(f"got{i}_{k}", [P, TT, D], F32)) for k in range(2)] for i in range(RING)]
        fetched = [ctx.enter_context(nc.semaphore(f"fetched{i}")) for i in range(RING)]
        summed, stored = ctx.enter_context(nc.semaphore("summed")), ctx.enter_context(nc.semaphore("stored"))
        with nc.Block() as block:

            @block.sync
            def _(sp):
                for c in range(NSEQ):
                    if c >= RING:
                        sp.wait_ge(summed, 2 * (c - RING + 1))
                    for k in range(2):
                        first = (k * NSEQ + c) * SEQ
                        sp.dma_start(got[c % RING][k][:], expert_dram[first:first + SEQ, :].rearrange("(t p) d -> p t d", p=P)
                                     ).then_inc(fetched[c % RING], 16)

            @block.vector
            def _(dve):
                for c in range(NSEQ):
                    dve.wait_ge(fetched[c % RING], (c // RING + 1) * 32)
                    xs = x_sb[:, c * TT:(c + 1) * TT, :]
                    for k in range(2):
                        dve.tensor_tensor(xs, got[c % RING][k][:], xs, ALU.add).then_inc(summed, 1)
                        dve.wait_ge(summed, 2 * c + k + 1)

            @block.scalar
            def _(act):
                for c in range(NSEQ):
                    act.wait_ge(summed, 2 * c + 2)
                    act.dma_start(out_dram[c].rearrange("(t p) d -> p t d", p=P), x_sb[:, c * TT:(c + 1) * TT, :]).then_inc(stored, 16)
                act.wait_ge(stored, NSEQ * 16)


def decoder_layer(nc, a, out_dram):
    with ExitStack() as ctx:
        x_sb = ctx.enter_context(nc.sbuf_tensor("x_sb", [P, NT, D], F32))
        sorted_dram = nc.dram_tensor("sorted_rows", (PAD_TILE + P, ROW), F32).ap()
        expert_dram = nc.dram_tensor("expert_rows", ((2 * NT + 1) * P, D), F32).ap()
        consts = make_constants(nc, ctx)
        attention_phase(nc, consts, x_sb, "self", {n: a["L0_attn_" + m] for n, m in dict(
            wq="Wq", wk="Wk", wv="Wv", wo="Wo", bq="bq", bk="bk", bv="bv", bo="bo").items()}, x_dram=a["x"])
        cross_phase(nc, consts, x_sb, {n: a["L0_xattn_" + m] for n, m in dict(
            wq="Wq", wk="Wk", wv="Wv", bq="bq", bk="bk", bv="bv").items()}, a["ctx_1024"])
        with ExitStack() as moe:
            y_sb = moe.enter_context(nc.sbuf_tensor("y_sb", [P, NT, D], F32))
            attention_phase(nc, consts, x_sb, "ffn", {n: a["L0_ffn_" + m] for n, m in dict(
                wq="wq", wk="wk", wv="wv", wo="wo", bo="bo", ln_scale="ln1_scale", ln_shift="ln1_shift").items()}, y_sb=y_sb)
            w1, w2 = (moe.enter_context(nc.sbuf_tensor(n, [P, E_N, KC, HID], F32)) for n in ("w1_sb", "w2_sb"))
            w3 = moe.enter_context(nc.sbuf_tensor("w3_sb", [P, E_N, HC, D], F32))
            weights = {"in": moe.enter_context(nc.semaphore("expert_weights_in")),
                       "parts": [("w1", w1, KC), ("w2", w2, KC), ("w3", w3, HC)]}
            w = {n: a["L0_ffn_" + n] for n in ("gate_w", "ln2_scale", "ln2_shift", "w1", "w2", "w3")}
            tiles = routing_phase(nc, moe, consts, y_sb, w, sorted_dram, weights)
            expert_phase(nc, consts, weights, *tiles, sorted_dram, expert_dram)
        combine_phase(nc, x_sb, expert_dram, out_dram)


_INS = ["x", "ctx_1024"] + ["L0_attn_" + n for n in ("Wq", "bq", "Wk", "bk", "Wv", "bv", "Wo", "bo")] + [
    "L0_xattn_" + n for n in ("Wq", "bq", "Wk", "bk", "Wv", "bv")] + [
    "L0_ffn_" + n for n in ("ln1_scale", "ln1_shift", "wq", "wk", "wv", "wo", "bo", "ln2_scale", "ln2_shift", "gate_w", "w1", "w2", "w3")]


def kernel(**inputs):
    import numpy as _np
    import concourse.bacc as _bacc
    from concourse import mybir as _mybir
    from concourse.bass_utils import run_bass_kernel_spmd as _run

    nc = _bacc.Bacc("TRN2", target_bir_lowering=False, num_devices=1)
    arrays, args = {}, {}
    for name in _INS:
        a = _np.ascontiguousarray(inputs[name])
        arrays[f"in_{name}_dram"] = a
        args[name] = nc.dram_tensor(f"in_{name}_dram", a.shape, _mybir.dt.from_np(a.dtype), kind="ExternalInput").ap()
    out = nc.dram_tensor("out_0_dram", (NSEQ, SEQ, D), F32, kind="ExternalOutput").ap()
    decoder_layer(nc, args, out)
    r = _run(nc, [arrays], core_ids=[0])
    return r.results[0]["out_0_dram"]
```

```python
from contextlib import ExitStack

import concourse.bass as bass
from concourse import mybir

ALU = mybir.AluOpType
ACT = mybir.ActivationFunctionType
AX_X = mybir.AxisListType.X
F32 = mybir.dt.float32
F32R = mybir.dt.float32r
BF16 = mybir.dt.bfloat16
I32 = mybir.dt.int32
U32 = mybir.dt.uint32

P = 128
NSEQ = 8
SEQ = 512
D = 256
KC = D // P
TT = SEQ // P
NT = NSEQ * TT
H = 16
DK = D // H
HG = 4
NG = H // HG
EPS = 1e-5
MASKED = -1e30

E_N = 8
HID = 512
HC = HID // P
MT = (2 * NSEQ * SEQ + E_N * (P - 1)) // P
REGION = NT * P + P
PAD_TILE = E_N * REGION
PLACE, WEIGHT = D, D + 1
ROW = D + 2


def wait(eng, sem, value):
    if not (isinstance(value, int) and value <= 0):
        eng.wait_ge(sem, value)


def wait_apart(eng, sem, value, passed):
    eng.wait_ge(sem, value)
    eng.sem_inc(passed, 1)


SPLIT = ((0, 0), (0, 1), (1, 0))


PRO, FIRST, MID, LAST, DRAIN = -1, 0, 1, NSEQ - 1, NSEQ


def each_body(eng, emit):
    emit(-1, PRO, 1)
    emit(0, FIRST, 0)
    with eng.Fori(0, (NSEQ - 2) // 2) as i:
        for k in range(2):
            emit(i * 2 + (1 + k), MID, (1 + k) % 2)
    emit(NSEQ - 1, LAST, 1)
    emit(NSEQ, DRAIN, 0)


def runs(kind, off):
    at = {PRO: -1, FIRST: 0, MID: 1, LAST: NSEQ - 1, DRAIN: NSEQ}[kind] + off
    return 0 <= at < NSEQ


class Turns:

    def __init__(self, hooks):
        self.jobs = [(name, off, bank) for at in sorted(hooks) for name, off, bank in hooks[at] if bank is not None]

    def count(self, kind, bank, upto=None):
        n = 0
        for name, off, b in self.jobs:
            if name == upto:
                break
            n += b == bank and runs(kind, off)
        return n

    def before(self, c, kind, name):
        bank = next(b for n, _, b in self.jobs if n == name)
        local = self.count(kind, bank, name)
        pro = self.count(PRO, bank)
        if kind == PRO:
            return local
        if kind == FIRST:
            return pro + local
        first = pro + self.count(FIRST, bank)
        mid = self.count(MID, bank)
        if kind == DRAIN:
            return first + mid * (NSEQ - 2) + self.count(LAST, bank) + local
        return (c - 1) * mid + (first + local)


QROWS = (0, 0, 0, 1, 1, 2)
KROWS = (0, 1, 2, 0, 1, 0)
SROWS = len(QROWS) * DK
MROWS = SROWS + 3

ROW_UNITS = [(0, (0, 1, 2, 3)), (1, (0, 1)), (1, (2, 3))] + [(2, (h,)) for h in range(HG)] + [(3, (h,)) for h in range(HG)]
KEY_UNITS = [(0, (h,)) for h in range(HG)] + [(1, (h,)) for h in range(HG)] + [(2, (0, 1)), (2, (2, 3)), (3, (0, 1, 2, 3))]
NU = len(ROW_UNITS)
assert NU == len(KEY_UNITS)
KEY_DONE = [max(u for u, (kt, _) in enumerate(KEY_UNITS) if kt == t) + 1 for t in range(TT)]
ROW_BANKS = 3
PT_OFF = [HG * sum(SEQ - P * j for j in range(t)) for t in range(TT + 1)]
PV_AT = {1: 0, 4: 1, 7: 2, 9: 3}
VCOLS = 32


def row_before(u, g4):
    return g4 * NU + (u - ROW_BANKS + 1 if u >= ROW_BANKS else {0: 9, 1: 10, 2: 8}[u] + 1 - NU)


ATT_HOOKS = {
    (0, 0): [("stats1", 1, None)],
    (0, 2): [("mx3", -1, None)],
    (0, 3): [("ut0", -1, 0)],
    (0, 4): [("mt3", -1, 1), ("norm1", 1, None)],
    (0, 6): [("stats2", 1, None)],
    (0, 8): [("norm2", 1, None)],
    (1, 0): [("ht0", 1, 0)],
    (1, 1): [("ht1", 1, 1), ("mx0", 0, None)],
    (1, 2): [("ut1", -1, 0)],
    (1, 4): [("mt0", 0, 1)],
    (1, 6): [("q0", 1, 0)],
    (1, 8): [("k0", 1, 1)],
    (1, 9): [("bias", 1, None)],
    (2, 0): [("q1", 1, 0)],
    (2, 1): [("mx1", 0, None)],
    (2, 2): [("ut2", -1, 0)],
    (2, 3): [("mt1", 0, 1)],
    (2, 6): [("k1", 1, 1)],
    (3, 0): [("v0", 1, 0)],
    (3, 1): [("mx2", 0, None), ("v1", 1, 1)],
    (3, 3): [("ut3", -1, 0)],
    (3, 4): [("mt2", 0, 1)],
    (3, 6): [("ct0", -1, 0)],
    (3, 7): [("ct1", -1, 1)],
    (3, 9): [("wo0", -1, 0)],
    (3, 10): [("wo1", -1, 1), ("out", -1, None)],
}
ATT_TURNS = Turns(ATT_HOOKS)
PARTS = ("q0", "k0", "q1", "k1")
LAG_ACT, LAG_SPLIT, LAG_STORE = 1, 2, 4


def attention_phase(nc, consts, x_sb, name, w, x_dram=None, y_sb=None, out_dram=None):
    first = x_dram is not None
    ident, ident_bf, neg_mask, minus_half = consts["ident"], consts["ident_bf"], consts["neg_mask"], consts["minus_half"]
    part_dram = nc.dram_tensor(f"{name}_parts", (2, 4, 3, P, SEQ), BF16).ap()
    max_dram = nc.dram_tensor(f"{name}_max", (NG, 3, HG * TT, P), BF16).ap()
    with ExitStack() as ctx:
        def sb(n, shape, dt=F32):
            return ctx.enter_context(nc.sbuf_tensor(f"{name}_{n}", shape, dt))

        def sem(n):
            return ctx.enter_context(nc.semaphore(f"{name}_{n}"))

        def pair(n, shape):
            return [sb(f"{n}_{part}", shape, F32R) for part in ("hi", "lo")]

        w_parts = [pair(n, [P, KC, D]) for n in ("wq", "wk", "wv")]
        wo = sb("wo", [P, KC, D])
        bo_row = sb("bo_row", [P, D])
        if first:
            bq, bk = sb("bq", [P, KC]), sb("bk", [P, KC])
            bv_row = sb("bv_row", [P, D])
        else:
            ln_scale, ln_shift = sb("ln_scale", [P, KC]), sb("ln_shift", [P, KC])
        stats, mv = sb("stats", [P, TT, 6]), sb("mv", [P, TT, 2])
        var_eps, rstd = sb("var_eps", [P, TT]), sb("rstd", [P, TT])
        rstd2 = None if first else sb("rstd2", [P, TT])
        hn = sb("hn", [P, TT, D])
        ht = pair("ht", [P, KC, SEQ])
        proj32 = [sb(f"proj32_{i}", [P, SEQ]) for i in range(2)]
        rest32 = [sb(f"rest32_{i}", [P, SEQ]) for i in range(2)]
        parts = [sb(f"parts_{n}", [P, 3, SEQ], BF16) for n in PARTS]
        q_rows = [sb(f"q_rows{g}", [MROWS, HG, SEQ], BF16) for g in range(NG)]
        k_rows = [sb(f"k_rows{g}", [MROWS, HG, SEQ], BF16) for g in range(NG)]
        maxes = [sb(f"maxes{i}", [P, HG, TT]) for i in range(2)]
        max_rest = sb("max_rest", [P, HG * TT])
        max_bf = sb("max_bf", [P, HG * TT], BF16)
        max_parts = sb("max_parts", [P, P])
        max_rows = sb("max_rows", [3 * HG * TT, P], BF16)
        probs = [sb(f"probs{i}", [P, PT_OFF[TT]]) for i in range(2)]
        values = [sb(f"values{i}", [P, TT, H, VCOLS]) for i in range(2)]
        ctx_raw = sb("ctx_raw", [P, SEQ])
        sums = sb("sums", [P, TT, HG])
        ctx_tok = sb("ctx_tok", [P, TT, D])
        w_loaded = [probs[0][:, n * KC * D:(n + 1) * KC * D].rearrange("p (c n) -> p c n", c=KC) for n in range(3)]
        ctx_t = hn[:].rearrange("p t d -> p (t d)").rearrange("p (c n) -> p c n", c=KC)

        row_ps = [ctx.enter_context(nc.psum_tensor(f"{name}_row{i}", [P, SEQ], F32)) for i in range(ROW_BANKS)]
        key_ps = [ctx.enter_context(nc.psum_tensor(f"{name}_key{i}", [P, SEQ], F32)) for i in range(2)]
        ctx_ps = ctx.enter_context(nc.psum_tensor(f"{name}_ctx", [P, SEQ], F32))
        misc_ps = [ctx.enter_context(nc.psum_tensor(f"{name}_misc{i}", [P, SEQ], F32)) for i in range(2)]

        weights_in = sem("weights_in")
        x_in = [sem(f"x_in{i}") for i in range(2)] if first else None
        setup_done, ones_done = sem("setup_done"), sem("ones_done")
        ln_steps, rstd_done, resid_done = sem("ln_steps"), sem("rstd_done"), sem("resid_done")
        proj_done, split_done, low_done = sem("proj_done"), sem("split_done"), sem("low_done")
        parts_out = [[sem(f"parts_out{i}{half}") for half in range(2)] for i in range(2)]
        rows_in = [sem(f"rows_in{g}") for g in range(NG)]
        row_scores, row_max = sem("row_scores"), sem("row_max")
        max_steps, max_out = sem("max_steps"), [sem(f"max_out{i}") for i in range(2)]
        max_in = [sem(f"max_in{g}") for g in range(NG)]
        key_scores, exp_done, mask_done = sem("key_scores"), sem("exp_done"), sem("mask_done")
        pv_done, ctx_out, sums_done = sem("pv_done"), sem("ctx_out"), sem("sums_done")
        LN_ALL = 4 if first else 8
        W_ALL = 16 * (11 if first else 7)
        passed = consts["passed"]
        misc_full, misc_free = [sem(f"misc_full{i}") for i in range(2)], [sem(f"misc_free{i}") for i in range(2)]
        w_high, ht_high, ht_low = sem("w_high"), sem("ht_high"), sem("ht_low")
        stream_done, stream_out = (None, None) if first else (sem("stream_done"), sem("stream_out"))

        def slots(c, kind):
            for g in range(NG):
                row = (c, g) if runs(kind, 0) else None
                back2 = (c, g - 2) if g >= 2 else (c - 1, g + 2)
                key = back2 if runs(kind, 0 if g >= 2 else -1) else None
                back3 = (c, 0) if g == 3 else (c - 1, g + 1)
                pv = back3 if runs(kind, 0 if g == 3 else -1) else None
                yield g, row, key, pv

        def hooks(c, kind, g, step):
            for job, off, bank in ATT_HOOKS.get((g, step), []):
                if runs(kind, off):
                    turn = ATT_TURNS.before(c, kind, job) if bank is not None else None
                    yield job, c + off, bank, turn

        def late_hooks(c, kind, g, at, lag, flush=True):
            if lag <= at < NU:
                yield from hooks(c, kind, g, at - lag)
            if at == (NU - 1 if flush else NU):
                for step in range(NU - lag, NU):
                    yield from hooks(c, kind, g, step)

        def tiles(c):
            return bass.ds(c * TT, TT)

        with nc.Block() as block:

            @block.sync
            def _(sp):
                def load_x(c, parity):
                    sp.dma_start(x_sb[:, tiles(c), :],
                                 x_dram[bass.ds(c, 1), :, :].rearrange("o (t p) d -> p (o t) d", p=P)).then_inc(x_in[parity], 16)

                if first:
                    load_x(0, 0)
                    load_x(1, 1)
                sp.dma_start(wo[:], w["wo"].rearrange("(c p) n -> p c n", p=P)).then_inc(weights_in, 16)
                if first:
                    for src, dst in zip((w["wq"], w["wk"], w["wv"]), w_loaded):
                        for kc in range(KC):
                            sp.dma_start(dst[:, kc, :].rearrange("p (h k) -> p h k", h=H),
                                         src[:, kc * P:(kc + 1) * P, :].rearrange("h p k -> p h k")).then_inc(weights_in, 16)
                    for src, dst in ((w["bq"], bq), (w["bk"], bk)):
                        sp.dma_start(dst[:], src.rearrange("(c g) k -> (g k) c", c=KC),
                                     allow_slow_non_contiguous=True).then_inc(weights_in, 16)
                    sp.dma_start(bv_row[:], w["bv"].rearrange("(o h) k -> o (h k)", o=1).to_broadcast([P, D])).then_inc(weights_in, 16)
                else:
                    for src, dst in zip((w["wq"], w["wk"], w["wv"]), w_loaded):
                        sp.dma_start(dst, src.rearrange("(c p) n -> p c n", p=P)).then_inc(weights_in, 16)
                    for src, dst in ((w["ln_scale"], ln_scale), (w["ln_shift"], ln_shift)):
                        sp.dma_start(dst[:], src.rearrange("(c p) -> p c", p=P),
                                     allow_slow_non_contiguous=True).then_inc(weights_in, 16)
                sp.dma_start(bo_row[:], w["bo"].rearrange("(o n) -> o n", o=1).to_broadcast([P, D])).then_inc(weights_in, 16)

                def store_parts(c, j, parity):
                    sp.wait_ge(low_done, c * 4 + (j + 1))
                    sp.dma_start(part_dram[parity, j].rearrange("s p t -> p s t"), parts[j][:]).then_inc(parts_out[parity][j // 2], 16)

                def load_rows(c, g, parity):
                    wait_apart(sp, parts_out[parity][g // 2], (c - parity) * 16 + 32, passed["sp"])
                    wait(sp, key_scores, ((c - 1) * NG + (g + 1)) * NU)
                    for rows, order, j0 in ((q_rows, QROWS, 0), (k_rows, KROWS, 1)):
                        src = part_dram[parity, j0 + g // 2 * 2]
                        for r, part in enumerate(order):
                            sp.dma_start(rows[g][r * DK:(r + 1) * DK, :, :],
                                         src[part, (g % 2) * 64:(g % 2) * 64 + 64, :].rearrange("(h d) t -> d h t", h=HG)
                                         ).then_inc(rows_in[g], 16)

                def body(c, kind, parity):
                    if first and kind in (PRO, FIRST):
                        for b in range(2, 4) if kind == PRO else range(4, NSEQ):
                            wait(sp, x_in[b % 2], b // 2 * 16)
                            load_x(b, b % 2)
                    for g, row, key, pv in slots(c, kind):
                        for step in range(NU):
                            for job, b, bank, turn in hooks(c, kind, g, step):
                                if job[:2] == "mt":
                                    mg = int(job[2])
                                    sp.wait_ge(misc_free[1], turn + 1)
                                    sp.dma_start(max_dram[mg].rearrange("s r t -> (s r) t"), max_rows[:]).then_inc(max_out[mg % 2], 16)
                                    sp.wait_ge(max_out[mg % 2], (b * 2 + (mg // 2 + 1)) * 16)
                                    sp.dma_start(q_rows[mg][SROWS:MROWS, :, :].rearrange("s h t -> s (h t)"),
                                                 max_dram[mg].rearrange("s r t -> s (r t)")).then_inc(max_in[mg], 16)
                            for job, b, bank, turn in late_hooks(c, kind, g, step, LAG_STORE, flush=False):
                                if job in PARTS:
                                    store_parts(b, PARTS.index(job), 1 - parity)
                        if g < 2 and runs(kind, 0):
                            load_rows(c, g + 2, parity)
                        if g >= 2 and runs(kind, 1) and not (kind == PRO and g == 2):
                            load_rows(c + 1, g - 2, 1 - parity)
                        for job, b, bank, turn in late_hooks(c, kind, g, NU, LAG_STORE, flush=False):
                            if job in PARTS:
                                store_parts(b, PARTS.index(job), 1 - parity)
                                if kind == PRO and job == "k0":
                                    load_rows(0, 0, 0)
                            elif job == "out" and not first:
                                sp.wait_ge(stream_done, (b + 1) * 2)
                                sp.dma_start(out_dram[bass.ds(b * SEQ, SEQ), :].rearrange("(t p) d -> p t d", p=P),
                                             x_sb[:, tiles(b), :]).then_inc(stream_out, 16)

                each_body(sp, body)
                if not first:
                    sp.wait_ge(stream_out, NSEQ * 16)
                for mg in range(NG):
                    sp.wait_ge(max_in[mg], 16 * NSEQ)

            @block.tensor
            def _(pe):
                def rows_unit(c, g, u):
                    qt, heads = ROW_UNITS[u]
                    n = (qt + 1) * P
                    out = row_ps[u % ROW_BANKS]
                    if u == 0:
                        pe.wait_ge(rows_in[g], (c + 1) * (16 * 2 * len(QROWS)))
                    wait(pe, row_max, row_before(u, c * NG + g))
                    for k, h in enumerate(heads):
                        pe.matmul(out[:, k * n:(k + 1) * n], q_rows[g][0:SROWS, h, qt * P:(qt + 1) * P],
                                  k_rows[g][0:SROWS, h, 0:n], start=(k == 0), stop=False, skip_group_check=True)
                    diag = out[:, 0:len(heads) * n].rearrange("p (h n) -> p h n", n=n)[:, :, qt * P:n]
                    pe.matmul(diag, ident_bf[:], neg_mask[:, 0:len(heads), :], start=False, stop=True,
                              skip_group_check=True).then_inc(row_scores, 1)

                def key_unit(c, g, u):
                    kt, heads = KEY_UNITS[u]
                    n = SEQ - kt * P
                    out = key_ps[(u + g) % 2]
                    if u == 0:
                        pe.wait_ge(max_in[g], (c + 1) * 16)
                    wait(pe, exp_done, (c * NG + g) * NU + (u - 1))
                    for k, h in enumerate(heads):
                        mm = pe.matmul(out[:, k * n:(k + 1) * n], k_rows[g][0:MROWS, h, kt * P:(kt + 1) * P],
                                       q_rows[g][0:MROWS, h, kt * P:SEQ], start=True, stop=True, skip_group_check=True)
                    mm.then_inc(key_scores, 1)

                def pv(c, g, kt, parity):
                    if kt == 0:
                        wait(pe, ctx_out, c * NG + g)
                    pe.wait_ge(mask_done, (c * NG + g) * TT + (kt + 1))
                    p = probs[g % 2][:, PT_OFF[kt]:PT_OFF[kt + 1]].rearrange("p (h n) -> p h n", h=HG)
                    for h in range(HG):
                        mm = pe.matmul(ctx_ps[VCOLS * h:VCOLS * (h + 1), kt * P:SEQ], values[parity][:, kt, g * HG + h, :],
                                       p[:, h, :], start=(kt == 0), stop=(kt == TT - 1), skip_group_check=True)
                    if kt == TT - 1:
                        mm.then_inc(pv_done, 1)

                def transposes(out, pieces, sem_):
                    for k, piece in enumerate(pieces):
                        mm = pe.transpose(out[:, k * P:(k + 1) * P], piece, ident[:])
                    mm.then_inc(sem_, 1)

                def split_product(out, lhs, rhs, sem_=None):
                    for kc in range(KC):
                        for a, b in SPLIT:
                            mm = pe.matmul(out, lhs(kc, a), rhs(kc, b), start=(kc == 0 and a == b), stop=(kc == KC - 1 and a == 1),
                                           skip_group_check=True)
                    if sem_ is not None:
                        mm.then_inc(sem_, 1)

                def product(out, lhs, rhs, sem_=None):
                    for kc in range(KC):
                        mm = pe.matmul(out, lhs(kc), rhs(kc), start=(kc == 0), stop=(kc == KC - 1), skip_group_check=True)
                    if sem_ is not None:
                        mm.then_inc(sem_, 1)

                def body(c, kind, parity):
                    if kind == FIRST:
                        pe.wait_ge(ones_done, NG)
                    for g, row, key, pvg in slots(c, kind):
                        for step in range(NU):
                            if row:
                                rows_unit(*row, step)
                            if key:
                                key_unit(*key, step)
                            if pvg and step in PV_AT:
                                pv(*pvg, PV_AT[step], parity if g == 3 else 1 - parity)
                            for job, b, bank, turn in hooks(c, kind, g, step):
                                if bank is None:
                                    continue
                                out, full = misc_ps[bank], misc_full[bank]
                                wait(pe, misc_free[bank], turn)
                                k = int(job[2]) if len(job) == 3 else int(job[1])
                                if job[:2] == "ut":
                                    pe.wait_ge(ctx_out, b * NG + (k + 1))
                                    transposes(out, [ctx_raw[:, t * P:(t + 1) * P] for t in range(TT)], full)
                                elif job[:2] == "mt":
                                    pe.wait_ge(max_steps, (b * NG + (k + 1)) * 4)
                                    pe.transpose(out[:, 0:P], max_parts[:], ident[:]).then_inc(full, 1)
                                elif job[:2] == "ht":
                                    if k == 0:
                                        pe.wait_ge(ln_steps, (b + 1) * LN_ALL)
                                    transposes(out, [hn[:, t, k * P:(k + 1) * P] for t in range(TT)], full)
                                elif job[0] in "qk":
                                    if kind == PRO and job == "q0":
                                        pe.wait_ge(setup_done, 1 + 3)
                                    if job == "q0":
                                        pe.wait_ge(ht_low, (b + 1) * 2)
                                    wt = w_parts["qk".index(job[0])]
                                    split_product(out[:], lambda kc, i: wt[i][:, kc, k * P:(k + 1) * P], lambda kc, i: ht[i][:, kc, :], full)
                                elif job[0] == "v":
                                    for t in range(2):
                                        split_product(out[:, t * D:(t + 1) * D], lambda kc, i: ht[i][:, kc, (2 * k + t) * P:(2 * k + t + 1) * P],
                                                      lambda kc, i: w_parts[2][i][:, kc, :], full if t == 1 else None)
                                elif job[:2] == "ct":
                                    transposes(out, [ctx_tok[:, t, k * P:(k + 1) * P] for t in range(TT)], full)
                                elif job[:2] == "wo":
                                    if k == 0:
                                        pe.wait_ge(misc_free[1], ATT_TURNS.before(c, kind, "ct1") + 1)
                                    for t in range(2):
                                        product(out[:, t * D:(t + 1) * D], lambda kc: ctx_t[:, kc, (2 * k + t) * P:(2 * k + t + 1) * P],
                                                lambda kc: wo[:, kc, :], full if t == 1 else None)

                each_body(pe, body)

            @block.scalar
            def _(act):
                act.wait_ge(weights_in, W_ALL)
                for n in range(3):
                    act.activation(w_parts[n][0][:], w_loaded[n], ACT.Copy).then_inc(w_high, 1)

                def exp_unit(c, g, u):
                    kt, heads = KEY_UNITS[u]
                    n = SEQ - kt * P
                    if u == 0:
                        wait(act, pv_done, c * NG + (g - 1))
                    act.wait_ge(key_scores, (c * NG + g) * NU + (u + 1))
                    at = PT_OFF[kt] + heads[0] * n
                    act.activation(probs[g % 2][:, at:at + len(heads) * n], key_ps[(u + g) % 2][:, 0:len(heads) * n],
                                   ACT.Exp, scale=DK ** -0.5).then_inc(exp_done, 1)

                def body(c, kind, parity):
                    for g, row, key, pvg in slots(c, kind):
                        for step in range(NU):
                            if key:
                                exp_unit(*key, step)
                            for job, b, bank, turn in late_hooks(c, kind, g, step, LAG_ACT):
                                if job == "norm2" and not first:
                                    act.wait_ge(rstd_done, b * 2 + 2)
                                    for t in range(TT):
                                        ins = act.activation(hn[:, t, :], y_sb[:, b * TT + t, :], ACT.Copy, scale=rstd2[:, t:t + 1])
                                    ins.then_inc(ln_steps, 1)
                                if bank is None or job[:2] in ("ut", "wo") or job[0] == "v":
                                    continue
                                k = int(job[2]) if len(job) == 3 else int(job[1])
                                act.wait_ge(misc_full[bank], turn + 1)
                                src, free = misc_ps[bank], misc_free[bank]
                                if job[:2] == "mt":
                                    act.activation(max_rows[:], src[0:3 * HG * TT, 0:P], ACT.Copy).then_inc(free, 1)
                                elif job[:2] == "ht":
                                    if first:
                                        act.activation(proj32[k][:], src[:], ACT.Copy).then_inc(free, 1)
                                    else:
                                        act.activation(proj32[k][:], src[:], ACT.Identity, scale=ln_scale[:, k:k + 1],
                                                       bias=ln_shift[:, k:k + 1]).then_inc(free, 1)
                                    wait_apart(act, free, turn + 1, passed["act"])
                                    act.activation(ht[0][:, k, :], proj32[k][:], ACT.Copy).then_inc(ht_high, 1)
                                elif job[:2] == "ct":
                                    act.activation(ctx_t[:, k, :], src[:], ACT.Copy).then_inc(free, 1)
                                else:
                                    j = PARTS.index(job)
                                    wait(act, low_done, b * 4 + (j - 1))
                                    if first:
                                        bias = (bq if job[0] == "q" else bk)[:, k:k + 1]
                                        act.activation(proj32[j % 2][:], src[:], ACT.Identity, bias=bias).then_inc(proj_done, 1)
                                        act.activation(parts[j][:, 0, :], src[:], ACT.Identity, bias=bias).then_inc(free, 1)
                                    else:
                                        act.activation(proj32[j % 2][:], src[:], ACT.Copy).then_inc(proj_done, 1)
                                        act.activation(parts[j][:, 0, :], src[:], ACT.Copy).then_inc(free, 1)
                        if pvg:
                            pc, pg = pvg
                            act.wait_ge(pv_done, pc * NG + (pg + 1))
                            act.activation(ctx_raw[:], ctx_ps[:], ACT.Copy).then_inc(ctx_out, 1)

                each_body(act, body)

            @block.vector
            def _(dve):
                def ln_stats(b, n, src):
                    base = b * LN_ALL + n * 4
                    for t in range(TT):
                        ins = dve.bn_stats(stats[:, t, :], src(t))
                    ins.then_inc(ln_steps, 1)
                    wait_apart(dve, ln_steps, base + 1, passed["dve"])
                    for t in range(TT):
                        ins = dve.bn_aggr(mv[:, t, :], stats[:, t, :])
                    ins.then_inc(ln_steps, 1)
                    dve.wait_ge(ln_steps, base + 2)
                    dve.tensor_scalar(var_eps[:], mv[:, :, 1], EPS, None, ALU.add).then_inc(ln_steps, 1)

                def ln_apply(b, n, src, dst):
                    dve.wait_ge(rstd_done, b * (LN_ALL // 4) + (n + 1))
                    for t in range(TT):
                        ins = dve.tensor_scalar(dst(t), src(t), mv[:, t, 0:1], rstd[:, t:t + 1], ALU.subtract, ALU.mult)
                    ins.then_inc(ln_steps, 1)

                def split(b, bank, turn, j):
                    dve.wait_ge(misc_free[bank], turn + 1)
                    dve.tensor_tensor(rest32[j % 2][:], proj32[j % 2][:], parts[j][:, 0, :], ALU.subtract).then_inc(split_done, 1)
                    dve.wait_ge(split_done, (b * 4 + j) * 2 + 1)
                    dve.tensor_copy(parts[j][:, 1, :], rest32[j % 2][:]).then_inc(split_done, 1)

                def take_values(b, bank, turn, k, parity):
                    dve.wait_ge(misc_full[bank], turn + 1)
                    out = values[parity][:, 2 * k:2 * k + 2, :, 0:DK]
                    src = misc_ps[bank][:].rearrange("p (t h n) -> p t h n", t=2, h=H)
                    if first:
                        for t in range(2):
                            ins = dve.tensor_tensor(out[:, t], src[:, t], bv_row[:].rearrange("p (h n) -> p h n", h=H), ALU.add)
                    else:
                        ins = dve.tensor_copy(out, src)
                    ins.then_inc(misc_free[bank], 1)

                def max_to_parts(b, g):
                    g4 = b * NG + g
                    mflat = maxes[g % 2][:].rearrange("p h t -> p (h t)")
                    m = HG * TT
                    dve.wait_ge(row_max, (g4 + 1) * NU)
                    dve.tensor_scalar(max_bf[:], mflat, -1.0, None, ALU.mult).then_inc(max_steps, 1)
                    dve.wait_ge(max_steps, g4 * 4 + 1)
                    dve.tensor_copy(max_parts[:, 0:m], max_bf[:])
                    dve.scalar_tensor_tensor(out=max_rest[:], in0=mflat, scalar=-1.0, in1=max_bf[:],
                                             op0=ALU.mult, op1=ALU.subtract).then_inc(max_steps, 1)
                    dve.wait_ge(max_steps, g4 * 4 + 2)
                    dve.tensor_copy(max_bf[:], max_rest[:]).then_inc(max_steps, 1)
                    dve.wait_ge(max_steps, g4 * 4 + 3)
                    dve.tensor_copy(max_parts[:, m:2 * m], max_bf[:])
                    dve.tensor_tensor(max_parts[:, 2 * m:3 * m], max_rest[:], max_bf[:], ALU.subtract).then_inc(max_steps, 1)

                def body(c, kind, parity):
                    for g, row, key, pvg in slots(c, kind):
                        if kind == PRO and g == 1:
                            for i in range(2):
                                dve.memset(values[i][:, :, :, DK:DK + 1], 1.0)
                                dve.memset(values[i][:, :, :, DK + 1:VCOLS], 0.0)
                            dve.memset(max_parts[:], 0.0).then_inc(setup_done, 1)
                            dve.wait_ge(setup_done, 1)
                            for n in range(3):
                                dve.wait_ge(w_high, n + 1)
                                dve.tensor_tensor(w_parts[n][1][:], w_loaded[n], w_parts[n][0][:], ALU.subtract).then_inc(setup_done, 1)
                        for step in range(NU):
                            if row:
                                qt, heads = ROW_UNITS[step]
                                n = (qt + 1) * P
                                dve.wait_ge(row_scores, (c * NG + g) * NU + (step + 1))
                                dve.tensor_reduce(maxes[g % 2][:, heads[0]:heads[-1] + 1, qt],
                                                  row_ps[step % ROW_BANKS][:, 0:len(heads) * n].rearrange("p (h n) -> p h n", n=n),
                                                  AX_X, ALU.max).then_inc(row_max, 1)
                            for job, b, bank, turn in late_hooks(c, kind, g, step, LAG_SPLIT):
                                if job in PARTS:
                                    split(b, bank, turn, PARTS.index(job))
                                elif job[:2] == "ht":
                                    k = int(job[2])
                                    dve.wait_ge(ht_high, b * 2 + (k + 1))
                                    dve.tensor_tensor(ht[1][:, k, :], proj32[k][:], ht[0][:, k, :], ALU.subtract).then_inc(ht_low, 1)
                            for job, b, bank, turn in late_hooks(c, kind, g, step, LAG_ACT):
                                if job in ("v0", "v1"):
                                    take_values(b, bank, turn, int(job[1]), 1 - parity)
                            for job, b, bank, turn in hooks(c, kind, g, step):
                                xt = (lambda t: x_sb[:, b * TT + t, :])
                                if job[:2] == "mx":
                                    max_to_parts(b, int(job[2]))
                                elif job == "stats1":
                                    if first:
                                        wait_apart(dve, x_in[1 - parity], (b - (1 - parity)) * 8 + 16, passed["dve"])
                                    ln_stats(b, 0, xt)
                                elif job == "norm1":
                                    if first:
                                        ln_apply(b, 0, xt, lambda t: hn[:, t, :])
                                    else:
                                        ln_apply(b, 0, xt, lambda t: y_sb[:, b * TT + t, :])
                                elif job == "stats2" and not first:
                                    dve.tensor_tensor(var_eps[:], mv[:, :, 1], rstd[:], ALU.mult).then_inc(ln_steps, 1)
                                    dve.wait_ge(ln_steps, b * LN_ALL + 5)
                                    dve.tensor_tensor(var_eps[:], var_eps[:], rstd[:], ALU.mult).then_inc(ln_steps, 1)
                                    dve.wait_ge(ln_steps, b * LN_ALL + 6)
                                    dve.tensor_scalar(var_eps[:], var_eps[:], EPS, None, ALU.add).then_inc(ln_steps, 1)
                                elif job[:2] == "ut":
                                    k = int(job[2])
                                    dve.wait_ge(misc_full[bank], turn + 1)
                                    src = misc_ps[bank][:].rearrange("p (t h n) -> p t h n", t=TT, h=HG)
                                    dve.reciprocal(sums[:], src[:, :, :, DK]).then_inc(sums_done, 1)
                                    dve.wait_ge(sums_done, b * NG + (k + 1))
                                    dve.tensor_tensor(
                                        ctx_tok[:, :, k * HG * DK:(k + 1) * HG * DK].rearrange("p t (h n) -> p t h n", h=HG),
                                        src[:, :, :, 0:DK], sums[:].unsqueeze(3).to_broadcast([P, TT, HG, DK]),
                                        ALU.mult).then_inc(misc_free[bank], 1)
                                elif job in ("wo0", "wo1"):
                                    k = int(job[2])
                                    dve.wait_ge(misc_full[bank], turn + 1)
                                    dve.wait_ge(resid_done, b + 1)
                                    xs = x_sb[:, bass.ds(b * TT + 2 * k, 2), :]
                                    src = misc_ps[bank][:].rearrange("p (t n) -> p t n", t=2)
                                    if first:
                                        dve.tensor_tensor(xs, src, xs, ALU.add).then_inc(misc_free[bank], 1)
                                    else:
                                        ys = y_sb[:, bass.ds(b * TT + 2 * k, 2), :]
                                        dve.tensor_tensor(ys, src, ys, ALU.add).then_inc(misc_free[bank], 1)
                                        dve.wait_ge(misc_free[bank], turn + 1)
                                        dve.tensor_tensor(xs, ys, xs, ALU.add).then_inc(stream_done, 1)
                each_body(dve, body)

            @block.gpsimd
            def _(pool):
                def body(c, kind, parity):
                    for g, row, key, pvg in slots(c, kind):
                        if kind == PRO and g == 1:
                            pool.wait_ge(rstd_done, LN_ALL // 4)
                            for n, rows in enumerate(k_rows):
                                pool.memset(rows[SROWS:MROWS, :, :], 1.0).then_inc(ones_done, 1)
                                pool.wait_ge(ones_done, n + 1)
                            pool.wait_ge(weights_in, W_ALL)
                        for step in range(NU):
                            if key:
                                kc_, kg = key
                                for kt in range(TT):
                                    if step == KEY_DONE[kt] - 1:
                                        wait_apart(pool, exp_done, (kc_ * NG + kg) * NU + KEY_DONE[kt], passed["pool"])
                                        p = probs[kg % 2][:, PT_OFF[kt]:PT_OFF[kt + 1]].rearrange("p (h n) -> p h n", h=HG)[:, :, 0:P]
                                        pool.affine_select(out=p, in_=p, compare_op=ALU.is_ge, fill=0.0, base=0,
                                                           pattern=[[0, HG], [1, P]], channel_multiplier=-1).then_inc(mask_done, 1)
                            for job, b, bank, turn in hooks(c, kind, g, step):
                                n_ln = LN_ALL // 4
                                if job == "norm1":
                                    pool.wait_ge(ln_steps, b * LN_ALL + 3)
                                    pool.tensor_tensor(rstd[:], var_eps[:], minus_half[:].to_broadcast([P, TT]), ALU.pow).then_inc(rstd_done, 1)
                                elif job == "norm2" and not first:
                                    pool.wait_ge(ln_steps, b * LN_ALL + 7)
                                    pool.tensor_tensor(rstd2[:], var_eps[:], minus_half[:].to_broadcast([P, TT]), ALU.pow).then_inc(rstd_done, 1)
                                elif job == "bias":
                                    pool.wait_ge(ln_steps, (b + 1) * LN_ALL)
                                    r = (x_sb if first else y_sb)[:, tiles(b), :]
                                    pool.tensor_tensor(r, r, bo_row[:].unsqueeze(1).to_broadcast([P, TT, D]), ALU.add).then_inc(resid_done, 1)
                            for job, b, bank, turn in late_hooks(c, kind, g, step, LAG_SPLIT):
                                if job in PARTS:
                                    j = PARTS.index(job)
                                    pool.wait_ge(split_done, (b * 4 + j) * 2 + 2)
                                    pool.tensor_tensor(parts[j][:, 2, :], rest32[j % 2][:], parts[j][:, 1, :], ALU.subtract).then_inc(low_done, 1)

                each_body(pool, body)


def make_constants(nc, ctx):
    ident = ctx.enter_context(nc.sbuf_tensor("ident", [P, P], F32))
    ident_bf = ctx.enter_context(nc.sbuf_tensor("ident_bf", [P, P], BF16))
    neg_mask = ctx.enter_context(nc.sbuf_tensor("neg_mask", [P, P], BF16))
    minus_half = ctx.enter_context(nc.sbuf_tensor("minus_half", [P, 1], F32))
    filled = ctx.enter_context(nc.semaphore("filled"))
    passed = {e: ctx.enter_context(nc.semaphore(f"passed_{e}")) for e in ("sp", "dve", "pool", "act")}
    with nc.Block() as block:

        @block.gpsimd
        def _(pool):
            pool.memset(minus_half[:], -0.5)
            pool.memset(ident[:], 0.0)
            pool.memset(ident_bf[:], 0.0)
            pool.memset(neg_mask[:], 0.0).then_inc(filled, 1)
            pool.wait_ge(filled, 1)
            for t in (ident, ident_bf):
                pool.affine_select(out=t[:], in_=t[:], compare_op=ALU.not_equal, fill=1.0, base=0,
                                   pattern=[[-1, P]], channel_multiplier=1)
            pool.affine_select(out=neg_mask[:], in_=neg_mask[:], compare_op=ALU.is_ge, fill=MASKED, base=0,
                               pattern=[[-1, P]], channel_multiplier=1).then_inc(filled, 1)

    neg_mask = neg_mask[:].unsqueeze(1).to_broadcast([P, HG, P])
    return dict(ident=ident, ident_bf=ident_bf, neg_mask=neg_mask, minus_half=minus_half, passed=passed)


CROSS_HOOKS = {
    (0, 0): [("stats", 1, None), ("ct0", 1, 0)],
    (0, 1): [("ct1", 1, 1)],
    (1, 0): [("norm", 1, None)],
    (1, 1): [("k0", 1, 0)],
    (1, 2): [("k1", 1, 1)],
    (2, 0): [("ht0", 1, 0)],
    (2, 1): [("ht1", 1, 1)],
    (2, 2): [("v0", 1, 0)],
    (3, 0): [("q0", 1, 0)],
    (3, 1): [("q1", 1, 1)],
    (3, 2): [("v1", 1, 1)],
}
CROSS_TURNS = Turns(CROSS_HOOKS)
CROSS_STEPS = 3


def cross_phase(nc, consts, x_sb, w, ctx_dram):
    ident, minus_half = consts["ident"], consts["minus_half"]
    with ExitStack() as ctx:
        def sb(n, shape, dt=F32):
            return ctx.enter_context(nc.sbuf_tensor(f"cross_{n}", shape, dt))

        def psum(n):
            return [ctx.enter_context(nc.psum_tensor(f"cross_{n}{i}", [P, SEQ], F32)) for i in range(2)]

        def sem(n):
            return ctx.enter_context(nc.semaphore(f"cross_{n}"))

        def pair(n, shape):
            return [sb(f"{n}_{part}", shape, F32R) for part in ("hi", "lo")]

        w_rows = [sb(f"{n}_rows", [P, KC, D]) for n in ("wq", "wk", "wv")]
        w_turned = [pair(f"{n}_turned", [P, KC, D]) for n in ("wq", "wk", "wv")]
        bq, bk, bv_row = sb("bq", [P, KC]), sb("bk", [P, KC]), sb("bv_row", [P, D])
        stats, mv = sb("stats", [P, TT, 6]), sb("mv", [P, TT, 2])
        var_eps, rstd = sb("var_eps", [P, TT]), sb("rstd", [P, TT])
        hn, ht = sb("hn", [P, TT, D]), pair("ht", [P, KC, SEQ])
        ctx_in_sb = [sb(f"ctx_in{i}", [P, TT, D]) for i in range(2)]
        ctx_t = pair("ctx_t", [P, KC, SEQ])
        q_t = [pair(f"q_t{i}", [P, KC, SEQ]) for i in range(2)]
        k_t = [pair(f"k_t{i}", [P, KC, SEQ]) for i in range(2)]
        values = [pair(f"values{i}", [P, TT, D]) for i in range(2)]
        row_max, minus_max = sb("row_max", [P, 2]), sb("minus_max", [P, 2])
        sums, inv_sums = sb("sums", [P, TT]), sb("inv_sums", [P, TT])
        probs = [sb(f"probs{i}", [P, SEQ]) for i in range(2)]
        probs_t = [pair(f"probs_t{i}", [P, TT, P]) for i in range(2)]
        score_ps, turn_ps, out_ps, misc_ps = psum("score"), psum("turn"), psum("out"), psum("misc")

        weights_in, w_full, w_high, w_ready = sem("weights_in"), sem("w_full"), sem("w_high"), sem("w_ready")
        turn_high, misc_high, bias_added = sem("turn_high"), [sem(f"misc_high{i}") for i in range(2)], sem("bias_added")
        ctx_loaded = [sem(f"ctx_loaded{i}") for i in range(2)]
        ln_steps, rstd_done = sem("ln_steps"), sem("rstd_done")
        scores_done, max_done, minus_done, exp_done = sem("scores_done"), sem("max_done"), sem("minus_done"), sem("exp_done")
        turn_full, turn_free, out_full, inv_done, out_free = (sem(n) for n in ("turn_full", "turn_free", "out_full", "inv_done", "out_free"))
        misc_full, misc_free = [sem(f"misc_full{i}") for i in range(2)], [sem(f"misc_free{i}") for i in range(2)]
        passed = consts["passed"]["dve"]
        W_ALL = 6 * 16

        def slots(c, kind):
            for qt in range(TT):
                score = (c, qt) if runs(kind, 0) else None
                turn = ((c, qt - 1) if qt >= 1 else (c - 1, TT - 1)) if runs(kind, 0 if qt >= 1 else -1) else None
                out = ((c, qt - 2) if qt >= 2 else (c - 1, qt + 2)) if runs(kind, 0 if qt >= 2 else -1) else None
                yield qt, score, turn, out

        def hooks(c, kind, g, step):
            for job, off, bank in CROSS_HOOKS.get((g, step), []):
                if runs(kind, off):
                    turn = CROSS_TURNS.before(c, kind, job) if bank is not None else None
                    yield job, c + off, bank, turn

        with nc.Block() as block:

            @block.sync
            def _(sp):
                for src, dst in zip((w["wq"], w["wk"], w["wv"]), w_rows):
                    sp.dma_start(dst[:], src.rearrange("(c p) n -> p c n", p=P)).then_inc(weights_in, 16)
                for src, dst in ((w["bq"], bq), (w["bk"], bk)):
                    sp.dma_start(dst[:], src.rearrange("(c p) -> p c", p=P),
                                 allow_slow_non_contiguous=True).then_inc(weights_in, 16)
                sp.dma_start(bv_row[:], w["bv"].rearrange("(o n) -> o n", o=1).to_broadcast([P, D])).then_inc(weights_in, 16)

                sp.dma_start(ctx_in_sb[0][:], ctx_dram[0].rearrange("(t p) d -> p t d", p=P)).then_inc(ctx_loaded[0], 16)
                sp.dma_start(ctx_in_sb[1][:], ctx_dram[1].rearrange("(t p) d -> p t d", p=P)).then_inc(ctx_loaded[1], 16)
                mid_turns = CROSS_TURNS.count(MID, 1)
                at = CROSS_TURNS.before(-1, PRO, "ct1") + 1
                sp.wait_ge(misc_free[1], at)
                sp.dma_start(ctx_in_sb[0][:], ctx_dram[2].rearrange("(t p) d -> p t d", p=P)).then_inc(ctx_loaded[0], 16)
                at = CROSS_TURNS.before(0, FIRST, "ct1") + 1
                sp.wait_ge(misc_free[1], at)
                sp.dma_start(ctx_in_sb[1][:], ctx_dram[3].rearrange("(t p) d -> p t d", p=P)).then_inc(ctx_loaded[1], 16)
                with sp.Fori(0, (NSEQ - 4) // 2) as i:
                    for k in range(2):
                        sp.wait_ge(misc_free[1], i * (2 * mid_turns) + (at + (k + 1) * mid_turns))
                        sp.dma_start(ctx_in_sb[k][:], ctx_dram[bass.ds(i * 2 + (4 + k), 1), :, :].rearrange("o (t p) d -> p (o t) d", p=P)
                                     ).then_inc(ctx_loaded[k], 16)

            @block.tensor
            def _(pe):
                pe.wait_ge(weights_in, W_ALL)
                for rows, out in zip(w_rows, (misc_ps[0], misc_ps[1], score_ps[0])):
                    for kc in range(KC):
                        for ec in range(KC):
                            mm = pe.transpose(out[:, (kc * KC + ec) * P:(kc * KC + ec + 1) * P],
                                              rows[:, ec, kc * P:(kc + 1) * P], ident[:])
                    mm.then_inc(w_full, 1)
                pe.wait_ge(w_ready, 3)

                def product(out, n, lhs, rhs, sem_=None):
                    for kc in range(n):
                        for a, b in SPLIT:
                            mm = pe.matmul(out, lhs(kc, a), rhs(kc, b), start=(kc == 0 and a == b), stop=(kc == n - 1 and a == 1),
                                           skip_group_check=True)
                    if sem_ is not None:
                        mm.then_inc(sem_, 1)

                def body(c, kind, parity):
                    for qt, score, turn_, out_ in slots(c, kind):
                        for step in range(CROSS_STEPS):
                            if step == 0 and score:
                                n = c * TT + qt
                                wait(pe, exp_done, n - 1)
                                product(score_ps[qt % 2][:], KC, lambda kc, i: q_t[parity][i][:, kc, qt * P:(qt + 1) * P],
                                        lambda kc, i: k_t[parity][i][:, kc, :], scores_done)
                            if step == 1 and turn_:
                                tc, tq = turn_
                                n = tc * TT + tq
                                pe.wait_ge(exp_done, n + 1)
                                wait(pe, turn_free, n - 1)
                                for kt in range(TT):
                                    mm = pe.transpose(turn_ps[tq % 2][:, kt * P:(kt + 1) * P], probs[tq % 2][:, kt * P:(kt + 1) * P], ident[:])
                                mm.then_inc(turn_full, 1)
                            if step == 2 and out_:
                                oc, oq = out_
                                n = oc * TT + oq
                                op = parity if qt >= 2 else 1 - parity
                                pe.wait_ge(turn_free, n + 1)
                                wait(pe, out_free, n - 1)
                                product(out_ps[oq % 2][:, 0:D], TT, lambda kt, i: probs_t[oq % 2][i][:, kt, :], lambda kt, i: values[op][i][:, kt, :],
                                        out_full)
                            for job, b, bank, turn in hooks(c, kind, qt, step):
                                if bank is None:
                                    continue
                                out, full = misc_ps[bank], misc_full[bank]
                                wait(pe, misc_free[bank], turn)
                                k = int(job[-1])
                                if job[:2] == "ct":
                                    if k == 0:
                                        pe.wait_ge(ctx_loaded[1 - parity], (b - (1 - parity)) * 8 + 16)
                                    for t in range(TT):
                                        mm = pe.transpose(out[:, t * P:(t + 1) * P], ctx_in_sb[1 - parity][:, t, k * P:(k + 1) * P], ident[:])
                                    mm.then_inc(full, 1)
                                elif job[:2] == "ht":
                                    pe.wait_ge(ln_steps, (b + 1) * 4)
                                    for t in range(TT):
                                        mm = pe.transpose(out[:, t * P:(t + 1) * P], hn[:, t, k * P:(k + 1) * P], ident[:])
                                    mm.then_inc(full, 1)
                                elif job[0] in "qk":
                                    if k == 0:
                                        pe.wait_ge(misc_free[1], CROSS_TURNS.before(c, kind, job[0] + "1"))
                                    src, wt = (ht, w_turned[0]) if job[0] == "q" else (ctx_t, w_turned[1])
                                    product(out[:], KC, lambda kc, i: wt[i][:, kc, k * P:(k + 1) * P], lambda kc, i: src[i][:, kc, :], full)
                                else:
                                    for t in range(2):
                                        product(out[:, t * D:(t + 1) * D], KC, lambda kc, i: ctx_t[i][:, kc, (2 * k + t) * P:(2 * k + t + 1) * P],
                                                lambda kc, i: w_turned[2][i][:, kc, :], full if t == 1 else None)

                each_body(pe, body)

            @block.scalar
            def _(act):
                for n, src in enumerate((misc_ps[0], misc_ps[1], score_ps[0])):
                    act.wait_ge(w_full, n + 1)
                    act.activation(w_turned[n][0][:].rearrange("p c n -> p (c n)"), src[:], ACT.Copy).then_inc(w_high, 1)
                act.wait_ge(weights_in, W_ALL)

                def body(c, kind, parity):
                    for qt, score, turn_, out_ in slots(c, kind):
                        for step in range(CROSS_STEPS):
                            if step == 0 and score:
                                n = c * TT + qt
                                act.wait_ge(minus_done, n + 1)
                                act.activation(probs[qt % 2][:], score_ps[qt % 2][:], ACT.Exp, bias=minus_max[:, qt % 2:qt % 2 + 1],
                                               accum_out=sums[:, qt:qt + 1]).then_inc(exp_done, 1)
                            if step == 1 and turn_:
                                tc, tq = turn_
                                act.wait_ge(turn_full, tc * TT + tq + 1)
                                act.activation(probs_t[tq % 2][0][:].rearrange("p t n -> p (t n)"), turn_ps[tq % 2][:], ACT.Copy).then_inc(turn_high, 1)
                            for job, b, bank, turn in hooks(c, kind, qt, step):
                                if bank is None:
                                    continue
                                k = int(job[-1])
                                act.wait_ge(misc_full[bank], turn + 1)
                                src, high = misc_ps[bank], misc_high[bank]
                                if job[:2] in ("ct", "ht"):
                                    act.activation((ctx_t if job[0] == "c" else ht)[0][:, k, :], src[:], ACT.Copy).then_inc(high, 1)
                                elif job[0] == "v":
                                    act.activation(values[1 - parity][0][:, 2 * k:2 * k + 2, :], src[:].rearrange("p (t n) -> p t n", t=2),
                                                   ACT.Copy).then_inc(high, 1)
                                else:
                                    dst, bias = (q_t, bq) if job[0] == "q" else (k_t, bk)
                                    act.activation(dst[1 - parity][0][:, k, :], src[:], ACT.Identity, bias=bias[:, k:k + 1]).then_inc(high, 1)

                each_body(act, body)

            @block.vector
            def _(dve):
                def low(out, src, high):
                    return dve.tensor_tensor(out, src, high, ALU.subtract)

                for n, src in enumerate((misc_ps[0], misc_ps[1], score_ps[0])):
                    dve.wait_ge(w_high, n + 1)
                    hi, lo = (part[:].rearrange("p c n -> p (c n)") for part in w_turned[n])
                    low(lo, src[:], hi).then_inc(w_ready, 1)

                def body(c, kind, parity):
                    for qt, score, turn_, out_ in slots(c, kind):
                        for step in range(CROSS_STEPS):
                            if step == 0 and score:
                                n = c * TT + qt
                                dve.wait_ge(scores_done, n + 1)
                                dve.tensor_reduce(row_max[:, qt % 2:qt % 2 + 1], score_ps[qt % 2][:], AX_X, ALU.max).then_inc(max_done, 1)
                                dve.wait_ge(max_done, n + 1)
                                dve.tensor_scalar(minus_max[:, qt % 2:qt % 2 + 1], row_max[:, qt % 2:qt % 2 + 1], -1.0, None, ALU.mult).then_inc(minus_done, 1)
                            if step == 1 and turn_:
                                tc, tq = turn_
                                dve.wait_ge(turn_high, tc * TT + tq + 1)
                                hi, lo = (part[:].rearrange("p t n -> p (t n)") for part in probs_t[tq % 2])
                                low(lo, turn_ps[tq % 2][:], hi).then_inc(turn_free, 1)
                            if step == 2 and out_:
                                oc, oq = out_
                                n = oc * TT + oq
                                dve.wait_ge(bias_added, oc + 1)
                                dve.wait_ge(exp_done, n + 1)
                                dve.reciprocal(inv_sums[:, oq:oq + 1], sums[:, oq:oq + 1]).then_inc(inv_done, 1)
                                dve.wait_ge(inv_done, n + 1)
                                dve.wait_ge(out_full, n + 1)
                                xs = x_sb[:, oc * TT + oq, :]
                                dve.scalar_tensor_tensor(out=xs, in0=out_ps[oq % 2][:, 0:D], scalar=inv_sums[:, oq:oq + 1], in1=xs,
                                                         op0=ALU.mult, op1=ALU.add).then_inc(out_free, 1)
                            for job, b, bank, turn in hooks(c, kind, qt, step):
                                xt = (lambda t: x_sb[:, b * TT + t, :])
                                if job == "stats":
                                    for t in range(TT):
                                        ins = dve.bn_stats(stats[:, t, :], xt(t))
                                    ins.then_inc(ln_steps, 1)
                                    wait_apart(dve, ln_steps, b * 4 + 1, passed)
                                    for t in range(TT):
                                        ins = dve.bn_aggr(mv[:, t, :], stats[:, t, :])
                                    ins.then_inc(ln_steps, 1)
                                    dve.wait_ge(ln_steps, b * 4 + 2)
                                    dve.tensor_scalar(var_eps[:], mv[:, :, 1], EPS, None, ALU.add).then_inc(ln_steps, 1)
                                elif job == "norm":
                                    dve.wait_ge(rstd_done, b + 1)
                                    for t in range(TT):
                                        ins = dve.tensor_scalar(hn[:, t, :], xt(t), mv[:, t, 0:1], rstd[:, t:t + 1], ALU.subtract, ALU.mult)
                                    ins.then_inc(ln_steps, 1)
                                else:
                                    k = int(job[-1])
                                    dve.wait_ge(misc_high[bank], turn + 1)
                                    src = misc_ps[bank]
                                    if job[:2] in ("ct", "ht"):
                                        hi, lo = (part[:, k, :] for part in (ctx_t if job[0] == "c" else ht))
                                        ins = low(lo, src[:], hi)
                                    elif job[0] == "v":
                                        hi, lo = (part[:, 2 * k:2 * k + 2, :] for part in values[1 - parity])
                                        ins = low(lo, src[:].rearrange("p (t n) -> p t n", t=2), hi)
                                    else:
                                        dst, bias = (q_t, bq) if job[0] == "q" else (k_t, bk)
                                        hi, lo = (part[:, k, :] for part in dst[1 - parity])
                                        ins = dve.scalar_tensor_tensor(out=lo, in0=src[:], scalar=bias[:, k:k + 1], in1=hi, op0=ALU.add,
                                                                       op1=ALU.subtract)
                                    ins.then_inc(misc_free[bank], 1)

                each_body(dve, body)

            @block.gpsimd
            def _(pool):
                pool.wait_ge(weights_in, W_ALL)

                def body(c, kind, parity):
                    if runs(kind, 1):
                        b = c + 1
                        pool.wait_ge(ln_steps, b * 4 + 3)
                        pool.tensor_tensor(rstd[:], var_eps[:], minus_half[:].to_broadcast([P, TT]), ALU.pow).then_inc(rstd_done, 1)
                        pool.wait_ge(ln_steps, (b + 1) * 4)
                        xs = x_sb[:, bass.ds(b * TT, TT), :]
                        pool.tensor_tensor(xs, xs, bv_row[:].unsqueeze(1).to_broadcast([P, TT, D]), ALU.add).then_inc(bias_added, 1)

                each_body(pool, body)




W_CHUNKS = 2 * E_N * KC // NSEQ


class Spare:

    def __init__(self, tensor):
        self.flat, self.at = tensor[:].rearrange("p t d -> p (t d)"), 0

    def take(self, a, b):
        self.at += a * b
        assert self.at <= NT * D
        return self.flat[:, self.at - a * b:self.at].rearrange("p (a b) -> p a b", a=a)


def routing_phase(nc, ctx, consts, x_sb, y_sb, w, sorted_dram, result_dram, weights):
    ident, minus_half = consts["ident"], consts["minus_half"]

    def keep(n, shape, dt=F32):
        return ctx.enter_context(nc.sbuf_tensor(f"moe_{n}", shape, dt))

    tile_expert, tile_row = keep("tile_expert", [1, MT + 1], I32), keep("tile_row", [1, MT + 1], I32)
    ln_scale, ln_shift = keep("ln_scale", [P, KC]), keep("ln_shift", [P, KC])
    with ExitStack() as inner:
        def sb(n, shape, dt=F32):
            return inner.enter_context(nc.sbuf_tensor(f"route_{n}", shape, dt))

        def sem(n):
            return inner.enter_context(nc.semaphore(f"route_{n}"))

        def psum(n):
            return inner.enter_context(nc.psum_tensor(f"route_{n}", [P, SEQ], F32))

        gate = sb("gate", [P, KC, E_N])
        stats, mv = sb("stats", [P, TT, 6]), sb("mv", [P, TT, 2])
        var_eps, rstd = sb("var_eps", [P, TT]), sb("rstd", [P, TT])
        spare = Spare(x_sb)
        rows = [[spare.take(TT, ROW) for k in range(2)] for i in range(2)]
        ht = [spare.take(KC, SEQ) for i in range(2)]
        loaded_w = [spare.take(1, HID)[:, 0] for i in range(2)]
        logits, top, top_at = sb("logits", [P, TT, E_N]), sb("top", [P, TT, 8]), sb("top_at", [P, TT, 8], U32)
        expert_of, one_hot = sb("expert_of", [P, TT, 2]), sb("one_hot", [P, TT, 2, E_N])
        chosen = sb("chosen", [P, TT, E_N], BF16)
        diff, ratio, denom = sb("diff", [P, TT]), sb("ratio", [P, TT]), sb("denom", [P, TT])
        base, picked = sb("base", [P, TT, E_N]), sb("picked", [P, TT, 2, E_N])
        row_f = sb("row_f", [P, TT, 2])
        row_of = [sb(f"row_of{i}", [P, TT, 2], U32) for i in range(2)]
        next_row = [sb(f"next_row{i}", [P, E_N]) for i in range(2)]
        iota_i, iota_e = sb("iota_i", [P, E_N], I32), sb("iota_e", [P, E_N])
        iota_ti, iota_t = sb("iota_ti", [1, MT + 1], I32), sb("iota_t", [1, MT + 1])
        place = sb("place", [P, NT], I32)
        before_bf, ones_bf, ones = sb("before_bf", [P, P], BF16), sb("ones_bf", [P, P], BF16), sb("ones", [P, E_N])
        pad_row, pad_at = sb("pad_row", [P, ROW]), sb("pad_at", [1, E_N], I32)
        padded, padded_i, n_tiles, tiles_upto = sb("padded", [P, E_N]), sb("padded_i", [P, E_N], I32), sb("n_tiles", [P, E_N]), sb("tiles_upto", [P, E_N])
        passed_tile, skipped, tile_f = sb("passed_tile", [1, MT + 1, E_N]), sb("skipped", [1, MT + 1, E_N]), sb("tile_f", [1, MT + 1])
        turn_ps = [[psum(f"turn{i}{k}") for k in range(2)] for i in range(2)]
        gate_ps = [psum(f"gate{i}") for i in range(2)]
        count_ps = psum("count")

        loaded, made, set_up = sem("loaded"), sem("made"), sem("set_up")
        ln_steps, rstd_done, copied = sem("ln_steps"), sem("rstd_done"), sem("copied")
        turned, ht_done, gated = sem("turned"), sem("ht_done"), sem("gated")
        steps, diff_done, chosen_done, counted, ratio_done, rows_done = (
            sem(n) for n in ("steps", "diff_done", "chosen_done", "counted", "ratio_done", "rows_done"))
        rowf_done = sem("rowf_done")
        scattered = [sem(f"scattered{i}") for i in range(2)]
        pads_done, rows_out = sem("pads_done"), sem("rows_out")
        passed, passed_pool = consts["passed"]["dve"], consts["passed"]["pool"]
        w_in, w_high, w_low = [sem(f"w_in{i}") for i in range(2)], sem("w_high"), sem("w_low")
        w_hi, w_lo = weights["hidden"]
        MADE_ALL = 5
        STEPS = 9

        with nc.Block() as block:

            @block.sync
            def _(sp):
                sp.dma_start(gate[:], w["gate_w"].rearrange("(c p) n -> p c n", p=P)).then_inc(loaded, 16)
                for src, dst in ((w["ln2_scale"], ln_scale), (w["ln2_shift"], ln_shift)):
                    sp.dma_start(dst[:], src.rearrange("(c p) -> p c", p=P), allow_slow_non_contiguous=True).then_inc(loaded, 16)
                sp.wait_ge(made, MADE_ALL)
                sp.dma_start(sorted_dram[PAD_TILE:PAD_TILE + P, :], pad_row[:]).then_inc(rows_out, 16)
                sp.dma_start(result_dram[NT * P:(NT + 1) * P, :], pad_row[:, 0:D]).then_inc(rows_out, 16)
                for c in range(NSEQ):
                    for n in range(c * W_CHUNKS, (c + 1) * W_CHUNKS):
                        wait(sp, w_low, n - 1)
                        name, e, kc = ("w1", "w2")[n // (E_N * KC)], n // KC % E_N, n % KC
                        sp.dma_start(loaded_w[n % 2], w[name][e, kc * P:(kc + 1) * P, :]).then_inc(w_in[n % 2], 16)
                    sp.wait_ge(ln_steps, (c + 1) * 4)
                    sp.dma_start(weights["out"][:, c], w["w3"][c].rearrange("(c p) n -> p c n", p=P)).then_inc(weights["in"], 16)
                sp.wait_ge(pads_done, 1)
                for e in range(E_N):
                    at = sp.value_load(pad_at[0:1, e:e + 1], min_val=0, max_val=PAD_TILE - P)
                    sp.dma_start(sorted_dram[bass.ds(at, P), :], pad_row[:]).then_inc(rows_out, 16)
                sp.wait_ge(rows_out, (2 + E_N) * 16)

            @block.gpsimd
            def _(pool):
                def set_up_constants():
                    pool.iota(iota_i[:], pattern=[[1, E_N]], base=0, channel_multiplier=0)
                    pool.iota(iota_ti[:], pattern=[[1, MT + 1]], base=0, channel_multiplier=0)
                    pool.iota(place[:], pattern=[[P, NT]], base=0, channel_multiplier=1).then_inc(made, 1)
                    pool.memset(before_bf[:], 1.0).then_inc(made, 1)
                    pool.wait_ge(made, 2)
                    pool.affine_select(out=before_bf[:], in_=before_bf[:], compare_op=ALU.is_ge, fill=0.0, base=-1,
                                       pattern=[[1, P]], channel_multiplier=-1).then_inc(made, 1)
                    pool.memset(ones_bf[:], 1.0)
                    pool.memset(ones[:], 1.0)
                    pool.memset(pad_row[:], 0.0).then_inc(made, 1)
                    pool.wait_ge(made, 4)
                    pool.iota(pad_row[:, PLACE:PLACE + 1].bitcast(I32), pattern=[[0, 1]], base=NT * P, channel_multiplier=1).then_inc(made, 1)

                def body(c, kind, parity):
                    if runs(kind, 1):
                        pool.wait_ge(ln_steps, c * 4 + 7)
                        pool.tensor_tensor(rstd[:], var_eps[:], minus_half[:].to_broadcast([P, TT]), ALU.pow).then_inc(rstd_done, 1)
                    if kind == PRO:
                        set_up_constants()
                    if runs(kind, 0):
                        pool.wait_ge(rows_done, c + 1)
                        wait_apart(pool, copied, c + 1, passed_pool)
                        for t in range(TT):
                            for k in range(2):
                                pool.indirect_dma_start(out=sorted_dram, out_offset=bass.IndirectOffsetOnAxis(ap=row_of[parity][:, t, k:k + 1], axis=0),
                                                        in_=rows[parity][k][:, t, :], in_offset=None).then_inc(scattered[parity], 16)

                each_body(pool, body)
                for i in range(2):
                    pool.wait_ge(scattered[i], NSEQ // 2 * 2 * TT * 16)

            @block.tensor
            def _(pe):
                pe.wait_ge(loaded, 48)

                def body(c, kind, parity):
                    if kind == FIRST:
                        pe.wait_ge(made, 4)
                    if runs(kind, 0):
                        pe.wait_ge(chosen_done, c + 1)
                        for t in range(TT + 1):
                            out = count_ps[:, t * E_N:(t + 1) * E_N]
                            for before in range(t):
                                mm = pe.matmul(out, ones_bf[:], chosen[:, before, :], start=(before == 0), stop=(before == t - 1 == TT - 1),
                                               skip_group_check=True)
                            if t < TT:
                                pe.matmul(out, before_bf[:], chosen[:, t, :], start=(t == 0), stop=True, skip_group_check=True)
                        mm.then_inc(counted, 1)
                    if runs(kind, 1):
                        b, i = c + 1, 1 - parity
                        pe.wait_ge(ln_steps, b * 4 + 4)
                        for kc in range(KC):
                            for t in range(TT):
                                mm = pe.transpose(turn_ps[i][kc][:, t * P:(t + 1) * P], rows[i][0][:, t, kc * P:(kc + 1) * P], ident[:])
                        mm.then_inc(turned, 1)
                        pe.wait_ge(ht_done, b + 1)
                        for t in range(TT):
                            for kc in range(KC):
                                mm = pe.matmul(gate_ps[i][:, t * E_N:(t + 1) * E_N], ht[i][:, kc, t * P:(t + 1) * P], gate[:, kc, :],
                                               start=(kc == 0), stop=(kc == KC - 1), skip_group_check=True)
                        mm.then_inc(gated, 1)

                each_body(pe, body)

            @block.scalar
            def _(act):
                act.wait_ge(loaded, 48)

                def high(c, m):
                    act.wait_ge(w_in[m % 2], c * (W_CHUNKS // 2 * 16) + (m // 2 + 1) * 16)
                    act.activation(w_hi[:, c * W_CHUNKS + m, :], loaded_w[m % 2], ACT.Copy).then_inc(w_high, 1)

                def body(c, kind, parity):
                    if runs(kind, 0):
                        for m in range(0, W_CHUNKS // 2):
                            high(c, m)
                        act.wait_ge(diff_done, c + 1)
                        act.activation(ratio[:], diff[:], ACT.Exp).then_inc(ratio_done, 1)
                        for m in range(W_CHUNKS // 2, W_CHUNKS):
                            high(c, m)
                    if runs(kind, 1):
                        b, i = c + 1, 1 - parity
                        act.wait_ge(turned, b + 1)
                        for kc in range(KC):
                            ins = act.activation(ht[i][:, kc, :], turn_ps[i][kc][:], ACT.Identity, scale=ln_scale[:, kc:kc + 1],
                                                 bias=ln_shift[:, kc:kc + 1])
                        ins.then_inc(ht_done, 1)
                        act.activation(rows[i][1][:, :, 0:D], rows[i][0][:, :, 0:D], ACT.Copy).then_inc(copied, 1)

                each_body(act, body)

            @block.vector
            def _(dve):
                def low(c, m):
                    dve.wait_ge(w_high, c * W_CHUNKS + (m + 1))
                    n = c * W_CHUNKS + m
                    dve.tensor_tensor(w_lo[:, n, :], loaded_w[m % 2], w_hi[:, n, :], ALU.subtract).then_inc(w_low, 1)

                def body(c, kind, parity):
                    if kind == FIRST:
                        dve.wait_ge(made, MADE_ALL)
                        dve.tensor_copy(iota_t[:], iota_ti[:])
                        dve.tensor_copy(iota_e[:], iota_i[:]).then_inc(set_up, 1)
                        dve.wait_ge(set_up, 1)
                        dve.tensor_scalar(next_row[0][:], iota_e[:], float(REGION), None, ALU.mult).then_inc(set_up, 1)
                        dve.wait_ge(set_up, 2)
                    if runs(kind, 1):
                        b = c + 1
                        for t in range(TT):
                            ins = dve.bn_stats(stats[:, t, :], y_sb[:, b * TT + t, :])
                        ins.then_inc(ln_steps, 1)
                        wait_apart(dve, ln_steps, b * 4 + 1, passed)
                        for t in range(TT):
                            ins = dve.bn_aggr(mv[:, t, :], stats[:, t, :])
                        ins.then_inc(ln_steps, 1)
                        dve.wait_ge(ln_steps, b * 4 + 2)
                        dve.tensor_scalar(var_eps[:], mv[:, :, 1], EPS, None, ALU.add).then_inc(ln_steps, 1)
                    if runs(kind, 0):
                        for m in range(0, W_CHUNKS // 2):
                            low(c, m)
                        step = 0

                        def done(ins, apart=False):
                            nonlocal step
                            step += 1
                            ins.then_inc(steps, 1)
                            if apart:
                                wait_apart(dve, steps, c * STEPS + step, passed)
                            else:
                                dve.wait_ge(steps, c * STEPS + step)

                        dve.wait_ge(gated, c + 1)
                        done(dve.tensor_copy(logits[:].rearrange("p t e -> p (t e)"), gate_ps[parity][:, 0:TT * E_N]), apart=True)
                        for t in range(TT):
                            ins = dve.max(top[:, t, :], logits[:, t, :])
                        done(ins, apart=True)
                        for t in range(TT):
                            ins = dve.max_index(top_at[:, t, :], top[:, t, :], logits[:, t, :])
                        dve.tensor_tensor(diff[:], top[:, :, 1], top[:, :, 0], ALU.subtract).then_inc(diff_done, 1)
                        done(ins)
                        done(dve.tensor_copy(expert_of[:], top_at[:, :, 0:2]))
                        for k in range(2):
                            ins = dve.tensor_tensor(one_hot[:, :, k, :], iota_e[:].unsqueeze(1).to_broadcast([P, TT, E_N]),
                                                    expert_of[:, :, k:k + 1].to_broadcast([P, TT, E_N]), ALU.is_equal)
                        done(ins)
                        dve.tensor_tensor(chosen[:], one_hot[:, :, 0, :], one_hot[:, :, 1, :], ALU.add).then_inc(chosen_done, 1)
                        dve.wait_ge(ratio_done, c + 1)
                        done(dve.tensor_scalar(denom[:], ratio[:], 1.0, None, ALU.add))
                        weight = [rows[parity][k][:, :, WEIGHT] for k in range(2)]
                        done(dve.reciprocal(weight[0], denom[:]))
                        dve.tensor_tensor(weight[1], weight[0], ratio[:], ALU.mult)
                        for k in range(2):
                            dve.tensor_copy(rows[parity][k][:, :, PLACE].bitcast(I32), place[:, bass.ds(c * TT, TT)])
                        dve.wait_ge(counted, c + 1)
                        dve.tensor_tensor(next_row[1 - parity][:], count_ps[:, TT * E_N:(TT + 1) * E_N], next_row[parity][:], ALU.add)
                        done(dve.tensor_tensor(base[:], count_ps[:, 0:TT * E_N].rearrange("p (t e) -> p t e", t=TT),
                                               next_row[parity][:].unsqueeze(1).to_broadcast([P, TT, E_N]), ALU.add))
                        for k in range(2):
                            ins = dve.tensor_tensor(picked[:, :, k, :], one_hot[:, :, k, :], base[:], ALU.mult)
                        done(ins)
                        dve.tensor_reduce(row_f[:], picked[:], AX_X, ALU.add).then_inc(rowf_done, 1)
                        dve.wait_ge(rowf_done, c + 1)
                        dve.tensor_copy(row_of[parity][:], row_f[:]).then_inc(rows_done, 1)
                        assert step == STEPS
                    if runs(kind, 1):
                        b, i = c + 1, 1 - parity
                        wait(dve, scattered[i], (b - i) * (TT * 16))
                        dve.wait_ge(rstd_done, b + 1)
                        for t in range(TT):
                            ins = dve.tensor_scalar(rows[i][0][:, t, 0:D], y_sb[:, b * TT + t, :], mv[:, t, 0:1], rstd[:, t:t + 1], ALU.subtract, ALU.mult)
                        ins.then_inc(ln_steps, 1)
                    if runs(kind, 0):
                        for m in range(W_CHUNKS // 2, W_CHUNKS):
                            low(c, m)

                each_body(dve, body)
                dve.wait_ge(steps, NSEQ * STEPS)
                step = NSEQ * STEPS

                def done(ins):
                    nonlocal step
                    step += 1
                    ins.then_inc(steps, 1)
                    dve.wait_ge(steps, step)

                dve.tensor_copy(pad_at[:], next_row[0][0:1, :]).then_inc(pads_done, 1)
                done(dve.scalar_tensor_tensor(out=padded[:], in0=iota_e[:], scalar=-float(REGION), in1=next_row[0][:], op0=ALU.mult, op1=ALU.add))
                done(dve.tensor_scalar(padded[:], padded[:], float(P - 1), None, ALU.add))
                done(dve.tensor_copy(padded_i[:], padded[:]))
                shift = P.bit_length() - 1
                done(dve.tensor_scalar(padded_i[:], padded_i[:], shift, None, ALU.logical_shift_right))
                done(dve.tensor_copy(n_tiles[:], padded_i[:]))
                done(dve.tensor_tensor_scan(tiles_upto[:], ones[:], n_tiles[:], 0.0, ALU.mult, ALU.add))
                done(dve.tensor_tensor(passed_tile[:], iota_t[:].unsqueeze(2).to_broadcast([1, MT + 1, E_N]),
                                       tiles_upto[0:1, :].unsqueeze(1).to_broadcast([1, MT + 1, E_N]), ALU.is_ge))
                done(dve.tensor_scalar(padded[:], n_tiles[:], -float(P), float(REGION), ALU.mult, ALU.add))
                done(dve.tensor_tensor(skipped[:], passed_tile[:], padded[0:1, :].unsqueeze(1).to_broadcast([1, MT + 1, E_N]), ALU.mult))
                done(dve.tensor_reduce(tile_f[:], skipped[:], AX_X, ALU.add))
                done(dve.scalar_tensor_tensor(out=tile_f[:], in0=iota_t[:], scalar=float(P), in1=tile_f[:], op0=ALU.mult, op1=ALU.add))
                done(dve.tensor_scalar(tile_f[:], tile_f[:], float(PAD_TILE), None, ALU.min))
                done(dve.tensor_copy(tile_row[:], tile_f[:]))
                done(dve.tensor_reduce(tile_f[:], passed_tile[:], AX_X, ALU.add))
                done(dve.tensor_scalar(tile_f[:], tile_f[:], float(E_N - 1), None, ALU.min))
                done(dve.tensor_copy(tile_expert[:], tile_f[:]))

    return tile_expert, tile_row, ln_scale, ln_shift


def expert_phase(nc, consts, x_sb, weights, tile_expert, tile_row, ln_scale, ln_shift, sorted_dram, result_dram):
    ident = consts["ident"]
    hidden_w = [part[:].rearrange("p (w e c) n -> p w e c n", w=2, e=E_N) for part in weights["hidden"]]
    w3 = weights["out"]
    with ExitStack() as ctx:
        def sb(n, shape, dt=F32):
            return [ctx.enter_context(nc.sbuf_tensor(f"expert_{n}{i}", shape, dt)) for i in range(2)]

        spare = Spare(x_sb)

        def two(a, b):
            return [spare.take(a, b) for i in range(2)]

        def psum(n, count):
            return [ctx.enter_context(nc.psum_tensor(f"expert_{n}{i}", [P, HID], F32)) for i in range(count)]

        def sem(n):
            return ctx.enter_context(nc.semaphore(f"expert_{n}"))

        meta = sb("meta", [P, ROW - D])
        rows, rows_t32, hidden_t = two(1, D), two(KC, P), two(HC, P)
        silu, hidden, result = two(1, HID), two(1, HID), two(1, D)
        rows, silu, hidden, result = ([b[:, 0] for b in bufs] for bufs in (rows, silu, hidden, result))
        rows_t = [sb(f"rows_t_{part}", [P, KC, P], F32R) for part in ("hi", "lo")]
        turn_ps, a_ps, b_ps, ht_ps, out_ps = psum("turn", 1), psum("a", 2), psum("b", 2), psum("ht", 1), psum("out", 2)
        passed, passed_act = consts["passed"]["pool"], consts["passed"]["act"]
        rows_in, meta_in = [sem(f"rows_in{i}") for i in range(2)], [sem(f"meta_in{i}") for i in range(2)]
        rows_high, rows_low = sem("rows_high"), sem("rows_low")
        turned, rows_t_done, a_done, b_done, silu_done, hidden_done = (
            sem(n) for n in ("turned", "rows_t_done", "a_done", "b_done", "silu_done", "hidden_done"))
        ht_full, ht_done, out_full, result_done = (sem(n) for n in ("ht_full", "ht_done", "out_full", "result_done"))
        stored = [sem(f"stored{i}") for i in range(2)]

        def each_step(eng, emit):
            for j in range(-2, 2):
                emit(j, j % 2)
            with eng.Fori(0, MT // 2 - 2) as i:
                for k in range(2):
                    emit(i * 2 + (k + 2), k)
            for j in range(MT - 3, MT):
                emit(j, j % 2)

        def parts(j):
            static = isinstance(j, int)
            return (j + 2 if not static or j < MT - 2 else None,
                    j + 1 if not static or -1 <= j < MT - 1 else None,
                    j if not static or j >= 0 else None)

        assert MT % 2 == 1

        with nc.Block() as block:

            @block.sync
            def _(sp):
                def row(j):
                    return sp.value_load(tile_row[0:1, bass.ds(j, 1)], min_val=0, max_val=PAD_TILE)

                def load(j, k):
                    sp.dma_start(rows[k], sorted_dram[bass.ds(row(j), P), 0:D]).then_inc(rows_in[k], 16)

                def load_meta(j, k):
                    wait(sp, stored[k], (j - k) * 8)
                    sp.dma_start(meta[k][:], sorted_dram[bass.ds(row(j), P), D:ROW]).then_inc(meta_in[k], 16)

                def tile(j, k):
                    if not isinstance(j, int) or j + 2 <= MT - 1:
                        sp.wait_ge(turned, j + 1)
                        load(j + 2, k)
                    load_meta(j, k)

                load(0, 0)
                load(1, 1)
                tile(0, 0)
                tile(1, 1)
                with sp.Fori(0, MT // 2 - 1 - 1) as i:
                    for k in range(2):
                        tile(i * 2 + (2 + k), k)
                for j in range(MT - 3, MT):
                    tile(j, j % 2)

            @block.gpsimd
            def _(pool):
                def scatter(j, k):
                    pool.wait_ge(result_done, j + 1)
                    wait(pool, stored[1 - k], (j - k) * 8 + (16 if k else 0))
                    wait_apart(pool, meta_in[k], (j - k) * 8 + 16, passed)
                    pool.indirect_dma_start(out=result_dram, out_offset=bass.IndirectOffsetOnAxis(ap=meta[k][:, 0:1].bitcast(U32), axis=0),
                                            in_=result[k], in_offset=None, compute_op=ALU.add).then_inc(stored[k], 16)

                for j in range(2):
                    scatter(j, j)
                with pool.Fori(0, MT // 2 - 1) as i:
                    for k in range(2):
                        scatter(i * 2 + (2 + k), k)
                scatter(MT - 1, 0)
                pool.wait_ge(stored[0], (MT // 2 + 1) * 16)
                pool.wait_ge(stored[1], MT // 2 * 16)

            @block.tensor
            def _(pe):
                pe.wait_ge(weights["in"], E_N * 16)

                def expert(j):
                    return pe.value_load(tile_expert[0:1, bass.ds(j, 1)], min_val=0, max_val=E_N - 1)

                def step(j, k):
                    turn, hid, out = parts(j)
                    if out is not None:
                        pe.wait_ge(hidden_done, out + 1)
                        wait(pe, ht_done, out)
                        for hc in range(HC):
                            mm = pe.transpose(ht_ps[0][:, hc * P:(hc + 1) * P], hidden[k][:, hc * P:(hc + 1) * P], ident[:])
                        mm.then_inc(ht_full, 1)
                    if turn is not None:
                        pe.wait_ge(rows_in[k], (turn - k) * 8 + 16)
                        wait(pe, rows_t_done, turn)
                        for kc in range(KC):
                            mm = pe.transpose(turn_ps[0][:, kc * P:(kc + 1) * P], rows[k][:, kc * P:(kc + 1) * P], ident[:])
                        mm.then_inc(turned, 1)
                    if hid is not None:
                        h = 1 - k
                        e = expert(hid)
                        pe.wait_ge(rows_low, hid + 1)
                        for n, (ps, full) in enumerate(((a_ps, a_done), (b_ps, b_done))):
                            for kc in range(KC):
                                for x, y in SPLIT:
                                    mm = pe.matmul(ps[h][:], rows_t[x][h][:, kc, :], hidden_w[y][:, n, e, kc, :], start=(kc == 0 and x == y),
                                                   stop=(kc == KC - 1 and x == 1))
                            mm.then_inc(full, 1)
                    if out is not None:
                        e = expert(out)
                        pe.wait_ge(ht_done, out + 1)
                        for hc in range(HC):
                            mm = pe.matmul(out_ps[k][:, 0:D], hidden_t[k][:, hc, :], w3[:, e, hc, :], start=(hc == 0), stop=(hc == HC - 1))
                        mm.then_inc(out_full, 1)

                each_step(pe, step)

            @block.scalar
            def _(act):
                def step(j, k):
                    turn, hid, out = parts(j)
                    if out is not None:
                        act.wait_ge(ht_full, out + 1)
                        act.activation(hidden_t[k].rearrange("p c n -> p (c n)"), ht_ps[0][:], ACT.Copy).then_inc(ht_done, 1)
                    if turn is not None:
                        act.wait_ge(turned, turn + 1)
                        for kc in range(KC):
                            ins = act.activation(rows_t32[k][:, kc, :], turn_ps[0][:, kc * P:(kc + 1) * P], ACT.Identity,
                                                 scale=ln_scale[:, kc:kc + 1], bias=ln_shift[:, kc:kc + 1])
                        ins.then_inc(rows_t_done, 1)
                        wait_apart(act, rows_t_done, turn + 1, passed_act)
                        act.activation(rows_t[0][k][:], rows_t32[k], ACT.Copy).then_inc(rows_high, 1)
                    if hid is not None:
                        act.wait_ge(a_done, hid + 1)
                        act.activation(silu[1 - k], a_ps[1 - k][:], ACT.Silu).then_inc(silu_done, 1)

                each_step(act, step)

            @block.vector
            def _(dve):
                def step(j, k):
                    turn, hid, out = parts(j)
                    if turn is not None:
                        dve.wait_ge(rows_high, turn + 1)
                        dve.tensor_tensor(rows_t[1][k][:], rows_t32[k], rows_t[0][k][:], ALU.subtract).then_inc(rows_low, 1)
                    if hid is not None:
                        h = 1 - k
                        dve.wait_ge(silu_done, hid + 1)
                        dve.wait_ge(b_done, hid + 1)
                        dve.tensor_tensor(hidden[h], b_ps[h][:], silu[h], ALU.mult).then_inc(hidden_done, 1)
                    if out is not None:
                        dve.wait_ge(out_full, out + 1)
                        wait(dve, stored[k], (out - k) * 8)
                        dve.wait_ge(meta_in[k], (out - k) * 8 + 16)
                        dve.tensor_scalar(result[k], out_ps[k][:, 0:D], meta[k][:, 1:2], None, ALU.mult).then_inc(result_done, 1)

                each_step(dve, step)


def output_phase(nc, result_dram, out_dram):
    with nc.semaphore("copied_out") as copied_out, nc.Block() as block:

        @block.sync
        def _(sp):
            for c in range(NSEQ):
                sp.dma_start(out_dram[c], result_dram[c * SEQ:(c + 1) * SEQ, :]).then_inc(copied_out, 16)
            sp.wait_ge(copied_out, NSEQ * 16)


def decoder_layer(nc, a, out_dram):
    with ExitStack() as ctx:
        x_sb = ctx.enter_context(nc.sbuf_tensor("x_sb", [P, NT, D], F32))
        sorted_dram = nc.dram_tensor("sorted_rows", (PAD_TILE + P, ROW), F32).ap()
        result_dram = nc.dram_tensor("result_rows", ((NT + 1) * P, D), F32).ap()
        consts = make_constants(nc, ctx)
        attention_phase(nc, consts, x_sb, "self", {n: a["L0_attn_" + m] for n, m in dict(
            wq="Wq", wk="Wk", wv="Wv", wo="Wo", bq="bq", bk="bk", bv="bv", bo="bo").items()}, x_dram=a["x"])
        cross_phase(nc, consts, x_sb, {n: a["L0_xattn_" + m] for n, m in dict(
            wq="Wq", wk="Wk", wv="Wv", bq="bq", bk="bk", bv="bv").items()}, a["ctx_1024"])
        with ExitStack() as moe:
            y_sb = moe.enter_context(nc.sbuf_tensor("y_sb", [P, NT, D], F32))
            attention_phase(nc, consts, x_sb, "ffn", {n: a["L0_ffn_" + m] for n, m in dict(
                wq="wq", wk="wk", wv="wv", wo="wo", bo="bo", ln_scale="ln1_scale", ln_shift="ln1_shift").items()}, y_sb=y_sb, out_dram=result_dram)
            hidden_w = [moe.enter_context(nc.sbuf_tensor(f"hidden_w_{part}", [P, 2 * E_N * KC, HID], F32R)) for part in ("hi", "lo")]
            weights = {"in": moe.enter_context(nc.semaphore("expert_weights_in")), "hidden": hidden_w,
                       "out": y_sb[:].rearrange("p (e c) d -> p e c d", e=E_N)}
            w = {n: a["L0_ffn_" + n] for n in ("gate_w", "ln2_scale", "ln2_shift", "w1", "w2", "w3")}
            tiles = routing_phase(nc, moe, consts, x_sb, y_sb, w, sorted_dram, result_dram, weights)
            expert_phase(nc, consts, x_sb, weights, *tiles, sorted_dram, result_dram)
        output_phase(nc, result_dram, out_dram)


_INS = ["x", "ctx_1024"] + ["L0_attn_" + n for n in ("Wq", "bq", "Wk", "bk", "Wv", "bv", "Wo", "bo")] + [
    "L0_xattn_" + n for n in ("Wq", "bq", "Wk", "bk", "Wv", "bv")] + [
    "L0_ffn_" + n for n in ("ln1_scale", "ln1_shift", "wq", "wk", "wv", "wo", "bo", "ln2_scale", "ln2_shift", "gate_w", "w1", "w2", "w3")]


def kernel(**inputs):
    import numpy as _np
    import concourse.bacc as _bacc
    from concourse import mybir as _mybir
    from concourse.bass_utils import run_bass_kernel_spmd as _run

    nc = _bacc.Bacc("TRN2", target_bir_lowering=False, num_devices=1)
    arrays, args = {}, {}
    for name in _INS:
        a = _np.ascontiguousarray(inputs[name])
        arrays[f"in_{name}_dram"] = a
        args[name] = nc.dram_tensor(f"in_{name}_dram", a.shape, _mybir.dt.from_np(a.dtype), kind="ExternalInput").ap()
    out = nc.dram_tensor("out_0_dram", (NSEQ, SEQ, D), F32, kind="ExternalOutput").ap()
    decoder_layer(nc, args, out)
    r = _run(nc, [arrays], core_ids=[0])
    return r.results[0]["out_0_dram"]
```
